# Optimizing a Trainium2 kernel written in Bass

```python
import numpy as np
import jax
import jax.numpy as jnp

def _softmax(x, axis=-1):
    return jax.nn.softmax(x, axis=axis)

def _gelu(x):
    return jax.nn.gelu(x, approximate=True)

def _silu(x):
    return jax.nn.silu(x)

def _sigmoid(x):
    return jax.nn.sigmoid(x)

def _layernorm(x, axis=-1, eps=1e-05):
    m = jnp.mean(x, axis=axis, keepdims=True)
    v = jnp.var(x, axis=axis, keepdims=True)
    return (x - m) / jnp.sqrt(v + eps)

def _scatter_add(tgt, idx, src, axis=0):
    return tgt.at[idx].add(src)

def _segment_sum(src, seg, n):
    return jax.ops.segment_sum(src, seg, n)
kernel_name = 'mk_vit_tower_postln_d2_tok_img256_r4_27402e'

def setup_inputs(seed: int=0):
    np.random.seed(seed)
    _w = jnp.asarray

    def _rec_inputs():
        import jax
        import jax.numpy as jnp
        _rk = jax.random.key(seed)
        x = -0.000125008 + 0.999885 * jax.random.normal(jax.random.fold_in(_rk, 1), (64, 64, 64, 64), jnp.float32)
        return x
    x = _rec_inputs()

    def _L0_tok_setup():
        import jax, jax.numpy as jnp
        import numpy as np
        B, C, H, W = (32, 64, 64, 64)
        STRIDE, HEADS = (4, 8)

        def _ln(x, w, b):
            mu = x.mean(-1, keepdims=True)
            var = ((x - mu) ** 2).mean(-1, keepdims=True)
            return (x - mu) * jax.lax.rsqrt(var + 1e-05) * w + b
        key = jax.random.key(seed)
        ks = jax.random.split(key, 4)
        return {'features': jax.random.normal(ks[0], (B, C, H, W), dtype=jnp.float32), 'ln_q_w': jnp.ones((C,), jnp.float32), 'ln_q_b': jnp.zeros((C,), jnp.float32), 'Wq': jax.random.normal(ks[1], (C, C), dtype=jnp.float32) * 0.02, 'ln_kv_w': jnp.ones((C,), jnp.float32), 'ln_kv_b': jnp.zeros((C,), jnp.float32), 'Wkv': jax.random.normal(ks[2], (2 * C, C), dtype=jnp.float32) * 0.02, 'proj_w': jax.random.normal(ks[3], (C, C), dtype=jnp.float32) * 0.02, 'proj_b': jnp.zeros((C,), jnp.float32), 'conv_stride': STRIDE, 'num_heads': HEADS}
    _L0_tok_all = _L0_tok_setup()
    _L0_tok_in = {k: v for k, v in _L0_tok_all.items() if k in ('ln_q_w', 'ln_q_b', 'Wq', 'ln_kv_w', 'ln_kv_b', 'Wkv', 'proj_w', 'proj_b')}
    del _L0_tok_all

    def _L0_attn_setup():
        import jax, jax.numpy as jnp
        import numpy as np
        HIDDEN = 64
        BLOCK_SIZE = 128
        BLOCK_K = 64
        LN_EPS = 1e-05

        def _layernorm(x, g, b):
            m = jnp.mean(x, axis=-1, keepdims=True)
            v = jnp.var(x, axis=-1, keepdims=True)
            return (x - m) * jax.lax.rsqrt(v + LN_EPS) * g + b

        def _l2norm(x):
            n = jnp.linalg.norm(x, axis=-1, keepdims=True)
            return x / jnp.maximum(n, 1e-12)
        key = jax.random.key(seed)
        ks = jax.random.split(key, 8)
        B, N, D = (8, 1024, 64)
        xg = 0.01 * np.sqrt(6.0 / (D + D))
        eg = 0.01 * np.sqrt(6.0 / (BLOCK_K + BLOCK_SIZE))
        return {'tokens': jax.random.normal(ks[0], (B, N, D), jnp.float32), 'W_q': jax.random.uniform(ks[1], (HIDDEN, D), jnp.float32, -xg, xg), 'W_k': jax.random.uniform(ks[2], (HIDDEN, D), jnp.float32, -xg, xg), 'W_v': jax.random.uniform(ks[3], (D, D), jnp.float32, -xg, xg), 'W_o': jax.random.uniform(ks[4], (D, D), jnp.float32, -xg, xg), 'E_block': jax.random.uniform(ks[5], (BLOCK_K, BLOCK_SIZE), jnp.float32, -eg, eg), 'F_block': jax.random.uniform(ks[6], (BLOCK_K, BLOCK_SIZE), jnp.float32, -eg, eg), 'g1': jnp.ones((D,), jnp.float32), 'b1': jnp.zeros((D,), jnp.float32), 'g2': jnp.ones((D,), jnp.float32), 'b2': jnp.zeros((D,), jnp.float32), 'scale': jnp.float32(1.0)}
    _L0_attn_all = _L0_attn_setup()
    _L0_attn_in = {k: v for k, v in _L0_attn_all.items() if k in ('W_q', 'W_k', 'W_v', 'W_o', 'E_block', 'F_block', 'g1', 'b1', 'g2', 'b2', 'scale')}
    del _L0_attn_all

    def _L0_ffn_setup():
        import jax, jax.numpy as jnp
        import numpy as np
        B, S, D = (8, 1024, 64)
        H = 4 * D
        CAPACITY = 0.5
        key = jax.random.key(seed)
        ks = jax.random.split(key, 6)
        x = jax.random.normal(ks[0], (B, S, D), dtype=jnp.float32)
        attention_mask = jnp.zeros((B, 1, 1, S), dtype=jnp.float32)
        wr = jax.random.normal(ks[1], (D, 1), dtype=jnp.float32) * 0.02
        br = jnp.zeros((1,), dtype=jnp.float32)
        w1 = jax.random.normal(ks[2], (D, H), dtype=jnp.float32) * 0.02
        b1 = jnp.zeros((H,), dtype=jnp.float32)
        w2 = jax.random.normal(ks[3], (H, D), dtype=jnp.float32) * 0.02
        b2 = jnp.zeros((D,), dtype=jnp.float32)
        return {'x': x, 'attention_mask': attention_mask, 'wr': wr, 'br': br, 'w1': w1, 'b1': b1, 'w2': w2, 'b2': b2}
    _L0_ffn_all = _L0_ffn_setup()
    _L0_ffn_in = {k: v for k, v in _L0_ffn_all.items() if k in ('attention_mask', 'wr', 'br', 'w1', 'b1', 'w2', 'b2')}
    del _L0_ffn_all

    def _L1_attn_setup():
        import jax, jax.numpy as jnp
        import numpy as np
        import math
        D = 64
        K = 32
        B = 2
        L = 512
        MAX_SEQ = 2048
        PI = math.pi

        def _content_stream(x, Wk1, bk1, Wk2, bk2, Wq1, bq1, Wq2, bq2, Wvc, bvc):
            Bc, Lc, Dc = x.shape
            key_phase = jnp.tanh(jnp.tanh(x @ Wk1 + bk1) @ Wk2 + bk2) * PI
            query_phase = jnp.tanh(jnp.tanh(x @ Wq1 + bq1) @ Wq2 + bq2) * PI
            value = x @ Wvc + bvc
            cos_k = jnp.cos(key_phase)[..., None]
            sin_k = jnp.sin(key_phase)[..., None]
            v_e = value[:, :, None, :]
            mem_real = jnp.cumsum(cos_k * v_e, axis=1)
            mem_imag = jnp.cumsum(sin_k * v_e, axis=1)
            cos_q = jnp.cos(query_phase)[..., None]
            sin_q = jnp.sin(query_phase)[..., None]
            retrieved = (mem_real * cos_q + mem_imag * sin_q).sum(axis=2)
            positions = jnp.arange(1, Lc + 1, dtype=jnp.float32)
            norm = jnp.sqrt(positions * K)[None, :, None]
            return retrieved / norm

        def _pos_stream(x, base_phases, Wvp, bvp):
            Bc, Lc, Dc = x.shape
            phases = base_phases[:Lc][None]
            value = x @ Wvp + bvp
            cos_p = jnp.cos(phases)
            sin_p = jnp.sin(phases)
            mem_real = jnp.cumsum(value * cos_p, axis=1)
            mem_imag = jnp.cumsum(value * sin_p, axis=1)
            retrieved = mem_real * cos_p + mem_imag * sin_p
            positions = jnp.arange(1, Lc + 1, dtype=jnp.float32)
            return retrieved / jnp.sqrt(positions)[None, :, None]
        key = jax.random.key(seed)
        ks = jax.random.split(key, 24)
        s = 0.02
        inp = {}
        inp['x'] = jax.random.normal(ks[0], (B, L, D), dtype=jnp.float32)
        inp['base_phases'] = jax.random.normal(ks[1], (MAX_SEQ, D), dtype=jnp.float32) * PI
        inp['Wk1'] = jax.random.normal(ks[2], (D, D), dtype=jnp.float32) * s
        inp['bk1'] = jnp.zeros((D,), jnp.float32)
        inp['Wk2'] = jax.random.normal(ks[3], (D, K), dtype=jnp.float32) * s
        inp['bk2'] = jnp.zeros((K,), jnp.float32)
        inp['Wq1'] = jax.random.normal(ks[4], (D, D), dtype=jnp.float32) * s
        inp['bq1'] = jnp.zeros((D,), jnp.float32)
        inp['Wq2'] = jax.random.normal(ks[5], (D, K), dtype=jnp.float32) * s
        inp['bq2'] = jnp.zeros((K,), jnp.float32)
        inp['Wvc'] = jax.random.normal(ks[6], (D, D), dtype=jnp.float32) * s
        inp['bvc'] = jnp.zeros((D,), jnp.float32)
        inp['Wvp'] = jax.random.normal(ks[7], (D, D), dtype=jnp.float32) * s
        inp['bvp'] = jnp.zeros((D,), jnp.float32)
        inp['Wg1'] = jax.random.normal(ks[8], (D, D // 4), dtype=jnp.float32) * s
        inp['bg1'] = jnp.zeros((D // 4,), jnp.float32)
        inp['Wg2'] = jax.random.normal(ks[9], (D // 4, 2), dtype=jnp.float32) * s
        inp['bg2'] = jnp.zeros((2,), jnp.float32)
        inp['ln_g'] = jnp.ones((D,), jnp.float32)
        inp['ln_b'] = jnp.zeros((D,), jnp.float32)
        inp['Wo'] = jax.random.normal(ks[10], (D, D), dtype=jnp.float32) * s
        inp['bo'] = jnp.zeros((D,), jnp.float32)
        return inp
    _L1_attn_all = _L1_attn_setup()
    _L1_attn_in = {k: v for k, v in _L1_attn_all.items() if k in ('base_phases', 'Wk1', 'bk1', 'Wk2', 'bk2', 'Wq1', 'bq1', 'Wq2', 'bq2', 'Wvc', 'bvc', 'Wvp', 'bvp', 'Wg1', 'bg1', 'Wg2', 'bg2', 'ln_g', 'ln_b', 'Wo', 'bo')}
    del _L1_attn_all

    def _L1_ffn_setup():
        import jax, jax.numpy as jnp
        import numpy as np
        B, S, H, F, E, K = (8, 1024, 64, 128, 16, 2)
        EPS = 1e-05
        key = jax.random.key(seed)
        ks = jax.random.split(key, 9)
        sc = 0.02
        return {'x': jax.random.normal(ks[0], (B, S, H), dtype=jnp.float32), 'gate_w': jax.random.normal(ks[1], (H, E), dtype=jnp.float32) * sc, 'gate_b': jnp.zeros((E,), dtype=jnp.float32), 'w1': jax.random.normal(ks[2], (E, H, F), dtype=jnp.float32) * sc, 'b1': jnp.zeros((E, F), dtype=jnp.float32), 'w2': jax.random.normal(ks[3], (E, F, H), dtype=jnp.float32) * sc, 'b2': jnp.zeros((E, H), dtype=jnp.float32), 'gamma': jnp.ones((H,), dtype=jnp.float32), 'beta': jnp.zeros((H,), dtype=jnp.float32)}
    _L1_ffn_all = _L1_ffn_setup()
    _L1_ffn_in = {k: v for k, v in _L1_ffn_all.items() if k in ('gate_w', 'gate_b', 'w1', 'b1', 'w2', 'b2', 'gamma', 'beta')}
    del _L1_ffn_all
    return {'x': x, 'L0_tok_ln_q_w': _L0_tok_in['ln_q_w'], 'L0_tok_ln_q_b': _L0_tok_in['ln_q_b'], 'L0_tok_Wq': _L0_tok_in['Wq'], 'L0_tok_ln_kv_w': _L0_tok_in['ln_kv_w'], 'L0_tok_ln_kv_b': _L0_tok_in['ln_kv_b'], 'L0_tok_Wkv': _L0_tok_in['Wkv'], 'L0_tok_proj_w': _L0_tok_in['proj_w'], 'L0_tok_proj_b': _L0_tok_in['proj_b'], 'L0_attn_W_q': _L0_attn_in['W_q'], 'L0_attn_W_k': _L0_attn_in['W_k'], 'L0_attn_W_v': _L0_attn_in['W_v'], 'L0_attn_W_o': _L0_attn_in['W_o'], 'L0_attn_E_block': _L0_attn_in['E_block'], 'L0_attn_F_block': _L0_attn_in['F_block'], 'L0_attn_g1': _L0_attn_in['g1'], 'L0_attn_b1': _L0_attn_in['b1'], 'L0_attn_g2': _L0_attn_in['g2'], 'L0_attn_b2': _L0_attn_in['b2'], 'L0_attn_scale': _L0_attn_in['scale'], 'L0_ffn_attention_mask': _L0_ffn_in['attention_mask'], 'L0_ffn_wr': _L0_ffn_in['wr'], 'L0_ffn_br': _L0_ffn_in['br'], 'L0_ffn_w1': _L0_ffn_in['w1'], 'L0_ffn_b1': _L0_ffn_in['b1'], 'L0_ffn_w2': _L0_ffn_in['w2'], 'L0_ffn_b2': _L0_ffn_in['b2'], 'L1_attn_base_phases': _L1_attn_in['base_phases'], 'L1_attn_Wk1': _L1_attn_in['Wk1'], 'L1_attn_bk1': _L1_attn_in['bk1'], 'L1_attn_Wk2': _L1_attn_in['Wk2'], 'L1_attn_bk2': _L1_attn_in['bk2'], 'L1_attn_Wq1': _L1_attn_in['Wq1'], 'L1_attn_bq1': _L1_attn_in['bq1'], 'L1_attn_Wq2': _L1_attn_in['Wq2'], 'L1_attn_bq2': _L1_attn_in['bq2'], 'L1_attn_Wvc': _L1_attn_in['Wvc'], 'L1_attn_bvc': _L1_attn_in['bvc'], 'L1_attn_Wvp': _L1_attn_in['Wvp'], 'L1_attn_bvp': _L1_attn_in['bvp'], 'L1_attn_Wg1': _L1_attn_in['Wg1'], 'L1_attn_bg1': _L1_attn_in['bg1'], 'L1_attn_Wg2': _L1_attn_in['Wg2'], 'L1_attn_bg2': _L1_attn_in['bg2'], 'L1_attn_ln_g': _L1_attn_in['ln_g'], 'L1_attn_ln_b': _L1_attn_in['ln_b'], 'L1_attn_Wo': _L1_attn_in['Wo'], 'L1_attn_bo': _L1_attn_in['bo'], 'L1_ffn_gate_w': _L1_ffn_in['gate_w'], 'L1_ffn_gate_b': _L1_ffn_in['gate_b'], 'L1_ffn_w1': _L1_ffn_in['w1'], 'L1_ffn_b1': _L1_ffn_in['b1'], 'L1_ffn_w2': _L1_ffn_in['w2'], 'L1_ffn_b2': _L1_ffn_in['b2'], 'L1_ffn_gamma': _L1_ffn_in['gamma'], 'L1_ffn_beta': _L1_ffn_in['beta']}

def reference(x, L0_tok_ln_q_w, L0_tok_ln_q_b, L0_tok_Wq, L0_tok_ln_kv_w, L0_tok_ln_kv_b, L0_tok_Wkv, L0_tok_proj_w, L0_tok_proj_b, L0_attn_W_q, L0_attn_W_k, L0_attn_W_v, L0_attn_W_o, L0_attn_E_block, L0_attn_F_block, L0_attn_g1, L0_attn_b1, L0_attn_g2, L0_attn_b2, L0_attn_scale, L0_ffn_attention_mask, L0_ffn_wr, L0_ffn_br, L0_ffn_w1, L0_ffn_b1, L0_ffn_w2, L0_ffn_b2, L1_attn_base_phases, L1_attn_Wk1, L1_attn_bk1, L1_attn_Wk2, L1_attn_bk2, L1_attn_Wq1, L1_attn_bq1, L1_attn_Wq2, L1_attn_bq2, L1_attn_Wvc, L1_attn_bvc, L1_attn_Wvp, L1_attn_bvp, L1_attn_Wg1, L1_attn_bg1, L1_attn_Wg2, L1_attn_bg2, L1_attn_ln_g, L1_attn_ln_b, L1_attn_Wo, L1_attn_bo, L1_ffn_gate_w, L1_ffn_gate_b, L1_ffn_w1, L1_ffn_b1, L1_ffn_w2, L1_ffn_b2, L1_ffn_gamma, L1_ffn_beta):
    import jax
    import jax.numpy as jnp

    def _L0_tok_ref(features, ln_q_w, ln_q_b, Wq, ln_kv_w, ln_kv_b, Wkv, proj_w, proj_b, conv_stride, num_heads):
        import jax, jax.numpy as jnp
        import numpy as np
        B, C, H, W = (32, 64, 64, 64)
        STRIDE, HEADS = (4, 8)

        def _ln(x, w, b):
            mu = x.mean(-1, keepdims=True)
            var = ((x - mu) ** 2).mean(-1, keepdims=True)
            return (x - mu) * jax.lax.rsqrt(var + 1e-05) * w + b
        s = conv_stride
        b, c, hh, ww = features.shape
        h, w = (hh // s, ww // s)
        hw, n, d = (h * w, s * s, c // num_heads)
        scale = c ** (-0.5)
        x = features.reshape(b, c, h, s, w, s)
        reduce_feats = x.mean((3, 5)).reshape(b, c, hw).transpose(0, 2, 1)
        unf = x.transpose(0, 1, 2, 4, 3, 5).reshape(b, c, hw, n).transpose(0, 2, 3, 1)
        q = _ln(reduce_feats, ln_q_w, ln_q_b) @ Wq.T
        q = q.reshape(b, hw, num_heads, d).transpose(0, 2, 1, 3)
        kv = _ln(unf, ln_kv_w, ln_kv_b) @ Wkv.T
        kv = kv.reshape(b, hw, n, 2, num_heads, d).transpose(3, 0, 4, 1, 2, 5)
        k, v = (kv[0], kv[1])
        attn = jax.nn.softmax(jnp.einsum('bhpd,bhpnd->bhpn', q * scale, k), axis=-1)
        aggre = jnp.einsum('bhpn,bhpnd->bhpd', attn, v)
        aggre = aggre.transpose(0, 2, 1, 3).reshape(b, hw, c)
        return reduce_feats + aggre @ proj_w.T + proj_b

    def _L0_attn_ref(tokens, W_q, W_k, W_v, W_o, E_block, F_block, g1, b1, g2, b2, scale):
        import jax, jax.numpy as jnp
        import numpy as np
        HIDDEN = 64
        BLOCK_SIZE = 128
        BLOCK_K = 64
        LN_EPS = 1e-05

        def _layernorm(x, g, b):
            m = jnp.mean(x, axis=-1, keepdims=True)
            v = jnp.var(x, axis=-1, keepdims=True)
            return (x - m) * jax.lax.rsqrt(v + LN_EPS) * g + b

        def _l2norm(x):
            n = jnp.linalg.norm(x, axis=-1, keepdims=True)
            return x / jnp.maximum(n, 1e-12)
        B, N, D = tokens.shape
        nb = N // BLOCK_SIZE
        tn = _layernorm(tokens, g1, b1)
        Q = tn @ W_q.T
        K = tn @ W_k.T
        V = tn @ W_v.T
        Q = _l2norm(Q)
        K = _l2norm(K)
        Kb = K.reshape(B, nb, BLOCK_SIZE, HIDDEN)
        Vb = V.reshape(B, nb, BLOCK_SIZE, D)
        K_proj = jnp.einsum('bnsh,ks->bnkh', Kb, E_block).reshape(B, nb * BLOCK_K, HIDDEN)
        V_proj = jnp.einsum('bnsv,ks->bnkv', Vb, F_block).reshape(B, nb * BLOCK_K, D)
        s = jax.nn.softplus(scale) / jnp.sqrt(jnp.float32(HIDDEN))
        scores = jnp.einsum('bnh,bkh->bnk', Q, K_proj) * s
        weights = jax.nn.softmax(scores, axis=-1)
        attn = jnp.einsum('bnk,bkv->bnv', weights, V_proj)
        out = tokens + attn @ W_o.T * 0.1
        return _layernorm(out, g2, b2)

    def _L0_ffn_ref(x, attention_mask, wr, br, w1, b1, w2, b2):
        import jax, jax.numpy as jnp
        import numpy as np
        B, S, D = (8, 1024, 64)
        H = 4 * D
        CAPACITY = 0.5
        b, s, d = x.shape
        weights = (jnp.einsum('bsd,do->bso', x, wr) + br)[..., 0]
        k = max(1, int(CAPACITY * s))
        kk = k - 1 if k > 1 else 1
        _, idx = jax.lax.top_k(weights, k)
        sel_idx = idx[:, :kk]
        sel = jnp.take_along_axis(x, sel_idx[:, :, None], axis=1)
        h = jax.nn.gelu(jnp.einsum('bkd,dh->bkh', sel, w1) + b1)
        y = jnp.einsum('bkh,hd->bkd', h, w2) + b2
        w_sel = jnp.take_along_axis(weights, sel_idx, axis=1)
        y = y * w_sel[..., None]
        batch_idx = jnp.arange(b)[:, None]
        processed = jnp.zeros_like(x).at[batch_idx, sel_idx].set(y)
        return processed + x

    def _L1_attn_ref(x, base_phases, Wk1, bk1, Wk2, bk2, Wq1, bq1, Wq2, bq2, Wvc, bvc, Wvp, bvp, Wg1, bg1, Wg2, bg2, ln_g, ln_b, Wo, bo):
        import jax, jax.numpy as jnp
        import numpy as np
        import math
        D = 64
        K = 32
        B = 2
        L = 512
        MAX_SEQ = 2048
        PI = math.pi

        def _content_stream(x, Wk1, bk1, Wk2, bk2, Wq1, bq1, Wq2, bq2, Wvc, bvc):
            Bc, Lc, Dc = x.shape
            key_phase = jnp.tanh(jnp.tanh(x @ Wk1 + bk1) @ Wk2 + bk2) * PI
            query_phase = jnp.tanh(jnp.tanh(x @ Wq1 + bq1) @ Wq2 + bq2) * PI
            value = x @ Wvc + bvc
            cos_k = jnp.cos(key_phase)[..., None]
            sin_k = jnp.sin(key_phase)[..., None]
            v_e = value[:, :, None, :]
            mem_real = jnp.cumsum(cos_k * v_e, axis=1)
            mem_imag = jnp.cumsum(sin_k * v_e, axis=1)
            cos_q = jnp.cos(query_phase)[..., None]
            sin_q = jnp.sin(query_phase)[..., None]
            retrieved = (mem_real * cos_q + mem_imag * sin_q).sum(axis=2)
            positions = jnp.arange(1, Lc + 1, dtype=jnp.float32)
            norm = jnp.sqrt(positions * K)[None, :, None]
            return retrieved / norm

        def _pos_stream(x, base_phases, Wvp, bvp):
            Bc, Lc, Dc = x.shape
            phases = base_phases[:Lc][None]
            value = x @ Wvp + bvp
            cos_p = jnp.cos(phases)
            sin_p = jnp.sin(phases)
            mem_real = jnp.cumsum(value * cos_p, axis=1)
            mem_imag = jnp.cumsum(value * sin_p, axis=1)
            retrieved = mem_real * cos_p + mem_imag * sin_p
            positions = jnp.arange(1, Lc + 1, dtype=jnp.float32)
            return retrieved / jnp.sqrt(positions)[None, :, None]
        pos_retrieved = _pos_stream(x, base_phases, Wvp, bvp)
        content_retrieved = _content_stream(x, Wk1, bk1, Wk2, bk2, Wq1, bq1, Wq2, bq2, Wvc, bvc)
        gates = jax.nn.softmax(jax.nn.relu(x @ Wg1 + bg1) @ Wg2 + bg2, axis=-1)
        combined = gates[:, :, 0:1] * pos_retrieved + gates[:, :, 1:2] * content_retrieved
        mu = combined.mean(axis=-1, keepdims=True)
        var = ((combined - mu) ** 2).mean(axis=-1, keepdims=True)
        normed = (combined - mu) / jnp.sqrt(var + 1e-05) * ln_g + ln_b
        return x + normed @ Wo + bo

    def _L1_ffn_ref(x, gate_w, gate_b, w1, b1, w2, b2, gamma, beta):
        import jax, jax.numpy as jnp
        import numpy as np
        B, S, H, F, E, K = (8, 1024, 64, 128, 16, 2)
        EPS = 1e-05
        gate_logits = x @ gate_w + gate_b
        topk_vals, topk_idx = jax.lax.top_k(gate_logits, K)
        topk_w = jax.nn.softmax(topk_vals, axis=-1)
        h = jax.nn.relu(jnp.einsum('bsh,ehf->bsef', x, w1) + b1)
        expert_out = jnp.einsum('bsef,efh->bseh', h, w2) + b2
        sel = jnp.take_along_axis(expert_out, topk_idx[:, :, :, None], axis=2)
        moe = jnp.sum(topk_w[..., None] * sel, axis=2)
        y = x + moe
        mu = jnp.mean(y, axis=-1, keepdims=True)
        var = jnp.var(y, axis=-1, keepdims=True)
        return (y - mu) / jnp.sqrt(var + EPS) * gamma + beta
    h = _L0_tok_ref(x, L0_tok_ln_q_w, L0_tok_ln_q_b, L0_tok_Wq, L0_tok_ln_kv_w, L0_tok_ln_kv_b, L0_tok_Wkv, L0_tok_proj_w, L0_tok_proj_b, 4, 8)
    h = _layernorm(h + _L0_attn_ref(h, L0_attn_W_q, L0_attn_W_k, L0_attn_W_v, L0_attn_W_o, L0_attn_E_block, L0_attn_F_block, L0_attn_g1, L0_attn_b1, L0_attn_g2, L0_attn_b2, L0_attn_scale), axis=-1)
    h = _layernorm(h + _L0_ffn_ref(h, L0_ffn_attention_mask, L0_ffn_wr, L0_ffn_br, L0_ffn_w1, L0_ffn_b1, L0_ffn_w2, L0_ffn_b2), axis=-1)
    h = _layernorm(h + _L1_attn_ref(h, L1_attn_base_phases, L1_attn_Wk1, L1_attn_bk1, L1_attn_Wk2, L1_attn_bk2, L1_attn_Wq1, L1_attn_bq1, L1_attn_Wq2, L1_attn_bq2, L1_attn_Wvc, L1_attn_bvc, L1_attn_Wvp, L1_attn_bvp, L1_attn_Wg1, L1_attn_bg1, L1_attn_Wg2, L1_attn_bg2, L1_attn_ln_g, L1_attn_ln_b, L1_attn_Wo, L1_attn_bo), axis=-1)
    h = _layernorm(h + _L1_ffn_ref(h, L1_ffn_gate_w, L1_ffn_gate_b, L1_ffn_w1, L1_ffn_b1, L1_ffn_w2, L1_ffn_b2, L1_ffn_gamma, L1_ffn_beta), axis=-1)
    return h

_drawn_inputs = setup_inputs


def setup_inputs(seed=0):
    import zlib

    import numpy as np

    out = dict(_drawn_inputs(seed))
    spreads = {'L0_tok_ln_q_w': (1.0, 0.6),
     'L0_tok_ln_q_b': (0.0, 0.8),
     'L0_tok_ln_kv_w': (1.0, 0.6),
     'L0_tok_ln_kv_b': (0.0, 0.654),
     'L0_tok_proj_b': (0.0, 0.1),
     'L0_attn_g1': (1.0, 0.6),
     'L0_attn_b1': (0.0, 2.0),
     'L0_attn_g2': (1.0, 0.2),
     'L0_attn_b2': (0.0, 0.1),
     'L0_ffn_b1': (0.0, 0.8),
     'L0_ffn_b2': (0.0, 0.8),
     'L1_attn_bk1': (0.0, 0.8),
     'L1_attn_bk2': (0.0, 0.8),
     'L1_attn_bq1': (0.0, 0.8),
     'L1_attn_bq2': (0.0, 0.8),
     'L1_attn_bvc': (0.0, 0.1),
     'L1_attn_bvp': (0.0, 0.8),
     'L1_attn_bg1': (0.0, 0.8),
     'L1_attn_bg2': (0.0, 0.8),
     'L1_attn_ln_g': (1.0, 0.6),
     'L1_attn_ln_b': (0.0, 0.8),
     'L1_attn_bo': (0.0, 0.1),
     'L1_ffn_gate_b': (0.0, 0.276),
     'L1_ffn_b1': (0.0, 0.8),
     'L1_ffn_b2': (0.0, 0.288),
     'L1_ffn_gamma': (1.0, 0.2),
     'L1_ffn_beta': (0.0, 0.1)}
    factors = {'L0_tok_Wq': 8.0,
     'L0_attn_W_q': 64.0,
     'L0_attn_W_k': 64.0,
     'L0_attn_W_v': 64.0,
     'L0_attn_W_o': 64.0,
     'L0_attn_E_block': 64.0,
     'L0_attn_F_block': 64.0,
     'L0_ffn_wr': 8.0,
     'L0_ffn_w1': 8.0,
     'L0_ffn_w2': 8.0,
     'L1_attn_base_phases': 8.0,
     'L1_attn_Wk1': 8.0,
     'L1_attn_Wk2': 8.0,
     'L1_attn_Wq1': 8.0,
     'L1_attn_Wq2': 8.0,
     'L1_attn_Wvp': 8.0,
     'L1_attn_Wg1': 8.0,
     'L1_attn_Wg2': 8.0,
     'L1_ffn_w1': 7.668,
     'L1_ffn_w2': 5.682}
    for name, (base, spread) in spreads.items():
        noise = np.random.default_rng([zlib.crc32(name.encode()), seed]).standard_normal(out[name].shape)
        drawn = base * np.exp(spread * noise) if base else spread * noise
        out[name] = jnp.asarray(drawn.astype(out[name].dtype))
    for name, factor in factors.items():
        out[name] = (out[name] * factor).astype(out[name].dtype)
    return out
```

```python
from contextlib import ExitStack

import numpy as np
import concourse.bass as bass
from concourse import mybir

F32 = mybir.dt.float32
BF16 = mybir.dt.bfloat16
ALU = mybir.AluOpType
ACT = mybir.ActivationFunctionType
AX = mybir.AxisListType

B, C, IMG = 64, 64, 64
STRIDE, HEADS = 4, 8
HD = C // HEADS
SIDE = IMG // STRIDE
TOK = SIDE * SIDE
PX = STRIDE * STRIDE
PIX = IMG * IMG
P = 128
NP = B // 2
CH = 512
NCH = PIX // CH
CP = CH // PX
EPS = 1e-5


class Pack:

    def __init__(self):
        self.parts, self.at, self.n = [], {}, 0

    def add(self, name, a):
        a = np.asarray(a, np.float32)
        full = np.zeros((P, a.shape[1]), np.float32)
        full[: a.shape[0]] = a
        self.at[name] = (self.n, a.shape[1], a.shape[0])
        self.parts.append(full)
        self.n += a.shape[1]

    def array(self):
        return np.ascontiguousarray(np.concatenate(self.parts, axis=1))


def twice(m):
    m = np.asarray(m, np.float32)
    out = np.zeros((2 * m.shape[0], 2 * m.shape[1]), np.float32)
    out[: m.shape[0], : m.shape[1]] = m
    out[m.shape[0]:, m.shape[1]:] = m
    return out


def column(v):
    v = np.asarray(v, np.float32).reshape(-1, 1)
    return np.concatenate([v, v], axis=0)


def shape_constants():
    k = Pack()
    eye = np.eye(P, dtype=np.float32)
    k.add("ident", eye)
    k.add("centre", twice(np.eye(C) - 1.0 / C))
    k.add("mean", twice(np.full((C, C), 1.0 / C)))
    var_sel = np.zeros((P, 2, 32), np.float32)
    head_sel = np.zeros((P, 2, 32), np.float32)
    spread = np.zeros((P, NCH, P), np.float32)
    for a in range(2):
        for img in range(2):
            for h in range(HEADS):
                row = 16 * a + 8 * img + h
                lo = 64 * img + HD * h
                var_sel[64 * img:64 * img + 64, a, row] = 1.0 / C
                head_sel[lo:lo + HD, a, row] = 1.0
                for g in range(4):
                    spread[32 * g + row, 4 * a + g, lo:lo + HD] = 1.0
    k.add("var_sel", var_sel.reshape(P, -1))
    k.add("head_sel", head_sel.reshape(P, -1))
    part, col = np.arange(P)[:, None], np.arange(TOK)[None]
    k.add("earlier", np.concatenate([col < part, col < part + P], axis=1))
    k.add("priority", np.broadcast_to(16.0 - np.arange(16)[None], (P, 16)))
    k.add("causal", part <= col)
    k.add("ones", np.ones((P, TOK)))
    k.add("root", np.broadcast_to(1 / np.sqrt(col + 1.0), (P, TOK)))
    k.add("root32", np.broadcast_to(1 / np.sqrt((col + 1.0) * 32), (P, TOK)))
    cosine = (np.arange(P)[:, None] // 32) % 2 == 0
    k.add("turn_sign", np.where(cosine, -1.0, 1.0))
    k.add("turn_scale", np.where(cosine, -PI, PI))
    k.add("turn_bias", np.where(cosine, PI / 2, 0.0))
    k.add("spread", spread.reshape(P, -1))
    return k


def weights(x):
    w = Pack()
    wkv = np.asarray(x["L0_tok_Wkv"])
    w.add("tok_wq", twice(np.asarray(x["L0_tok_Wq"]).T))
    w.add("tok_wk", twice(wkv[:C].T))
    w.add("tok_wv", twice(wkv[C:].T))
    w.add("tok_wp", twice(np.asarray(x["L0_tok_proj_w"]).T))
    w.add("at_wq", twice(np.asarray(x["L0_attn_W_q"]).T))
    kv = [twice(np.asarray(x[n]).T) for n in ("L0_attn_W_k", "L0_attn_W_v")]
    w.add("at_wkv", np.concatenate(kv, axis=1))
    w.add("at_wo", twice(np.asarray(x["L0_attn_W_o"]).T))
    w.add("at_e", np.asarray(x["L0_attn_E_block"]).T)
    w.add("at_f", np.asarray(x["L0_attn_F_block"]).T)
    for name in ("L0_attn_g1", "L0_attn_b1", "L0_attn_g2", "L0_attn_b2"):
        w.add(name, column(x[name]))
    w.add("ff_wr", np.tile(np.broadcast_to(np.asarray(x["L0_ffn_wr"]), (C, P)), (2, 1)))
    w.add("L0_ffn_br", np.broadcast_to(np.asarray(x["L0_ffn_br"]).reshape(1, 1), (P, 1)))
    w.add("ff_w1", np.tile(np.asarray(x["L0_ffn_w1"]), (2, 1)))
    w.add("ff_b1", np.asarray(x["L0_ffn_b1"]).reshape(2, P).T)
    w.add("ff_w2", np.concatenate(np.split(np.asarray(x["L0_ffn_w2"]), 2), axis=1))
    w.add("ff_b2", column(x["L0_ffn_b2"]))

    def features(m):
        m = np.asarray(m)
        return np.concatenate([m, m], axis=1)

    for n in ("k", "q"):
        w.add(f"ho_w{n}1", twice(x[f"L1_attn_W{n}1"]))
        w.add(f"ho_w{n}2", twice(features(x[f"L1_attn_W{n}2"])))
        w.add(f"ho_b{n}2", column(features(np.asarray(x[f"L1_attn_b{n}2"])[None])))
        w.add(f"L1_attn_b{n}1", column(x[f"L1_attn_b{n}1"]))
    w.add("ho_wvp", twice(x["L1_attn_Wvp"]))
    w.add("ho_wvc", twice(x["L1_attn_Wvc"]))
    w.add("ho_bvc", np.broadcast_to(column(x["L1_attn_bvc"]).T, (P, P)))
    w.add("ho_wg1", twice(x["L1_attn_Wg1"]))
    w.add("ho_bg1", column(x["L1_attn_bg1"]))
    for k, n in enumerate("ab"):
        w.add(f"ho_wg2{n}", twice(np.broadcast_to(np.asarray(x["L1_attn_Wg2"])[:, k:k + 1], (C // 4, C))))
        w.add(f"ho_bg2{n}", np.broadcast_to(np.asarray(x["L1_attn_bg2"])[k:k + 1].reshape(1, 1), (P, 1)))
    w.add("ho_phases", np.tile(np.asarray(x["L1_attn_base_phases"])[:TOK].T, (2, 1)))
    w.add("mo_gate", twice(x["L1_ffn_gate_w"]))
    w.add("mo_gate_b", np.broadcast_to(np.asarray(x["L1_ffn_gate_b"])[None], (P, 16)))
    w.add("mo_b1", np.asarray(x["L1_ffn_b1"]).T)
    b2 = np.zeros((P, QT, P), np.float32)
    for t in range(QT):
        b2[32 * t:32 * t + 32, t] = twice(x["L1_ffn_b2"])
    w.add("mo_b2", b2.reshape(P, -1))
    w.add("mo_gamma", np.broadcast_to(np.asarray(x["L1_ffn_gamma"])[None], (P, C)))
    w.add("mo_beta", np.broadcast_to(np.asarray(x["L1_ffn_beta"])[None], (P, C)))
    w.add("ho_wo", twice(x["L1_attn_Wo"]))
    for name in ("L1_attn_bvp", "L1_attn_ln_g", "L1_attn_ln_b", "L1_attn_bo"):
        w.add(name, column(x[name]))
    w.add("L0_attn_scale", np.broadcast_to(np.asarray(x["L0_attn_scale"]).reshape(1, 1), (P, 1)))
    for name in ("L0_tok_ln_q_w", "L0_tok_ln_q_b", "L0_tok_ln_kv_w", "L0_tok_ln_kv_b", "L0_tok_proj_b"):
        w.add(name, column(x[name]))
    return w


class Sems:

    def __init__(self, nc, ctx, phase, names):
        self.s = {n: ctx.semaphore(f"{phase}_{n}") for n in names.split()}

    def __getitem__(self, n):
        return self.s[n]


def past(count):
    return max(count, 0) if isinstance(count, int) else count


def tokenizer(nc, ctx, x, K, W, H, psum):
    NX = 4

    def sb(name, cols, dt=F32):
        return ctx.enter_context(nc.sbuf_tensor(name, [P, cols], dt))

    def sem(name):
        return ctx.semaphore("tok_" + name)

    xt = sb("tok_x", NX * PIX)
    sq = sb("tok_sq", NCH * CH)
    kq = sb("tok_kq", NCH * CH)
    half = sb("tok_half", PIX // 2)
    quarter = sb("tok_quarter", PIX // 4)
    eighth = half[:, 0:PIX // 8]
    pooled = sb("tok_pooled", 2 * TOK)
    base = sb("tok_base", 2 * TOK)
    qsq = sb("tok_qsq", TOK)
    qr = sb("tok_qr", TOK)
    qn = sb("tok_qn", TOK)
    qa = sb("tok_qa", TOK)
    qs = sb("tok_qs", 2 * TOK)
    rstd = sb("tok_rstd", 2 * CH)
    score = sb("tok_score", CH)
    shifted = sb("tok_shifted", CH)
    top = sb("tok_top", CP)
    expd = sb("tok_exp", CH)
    den = sb("tok_den", CP)
    rden = sb("tok_rden", CP)
    er = sb("tok_er", CH)
    attn = sb("tok_attn", CH)
    wide = sb("tok_wide", 4 * CH)
    zp = sb("tok_zp", 2 * CH)
    z = sb("tok_z", TOK)
    wkc = sb("tok_wkc", P)
    wvc = sb("tok_wvc", P)
    wks, wvs = kq[:, 0:P], kq[:, P:2 * P]
    small = sb("tok_small", 4)
    lnq16, bv, pbz = small[:, 0:1], small[:, 1:2], small[:, 2:3]

    ps = psum
    VAR, SCORE = 4, 5

    x_in = [sem(f"x_in{s}") for s in range(NX)]
    names = ("prep_dve prep_pe prep_act prep2_pe prep2_act half quarter eighth pooled cx sq var rstd qc qsq qv qr qn qa qq qs base "
             "kx kq scored s1 top shifted exp den rden er attn wide_mm wide vx zmul zred pj tok")
    S = Sems(nc, ctx, "tok", names)

    def mm(out, lhsT, rhs, start=True, stop=True, **kw):
        return nc.tensor.matmul(out, lhsT, rhs, start=start, stop=stop, **kw)

    def pixel_mm(out, lhsT, slot, c):
        n = STRIDE * IMG
        for k in range(CH // n):
            at = slot * PIX + c * CH + k * n
            v = xt[:, at:at + n].rearrange("p (i w j) -> p w i j", i=STRIDE, w=SIDE, j=STRIDE)
            last = mm(out[:, k * n:(k + 1) * n], lhsT, v)
        return last

    def patches(v):
        return v.rearrange("p (a b) -> p a b", b=PX)

    def over_pixels(v, n):
        return v.unsqueeze(2).broadcast_to([P, n, PX])

    block = ctx.enter_context(nc.Block())

    @block.sync
    def _(sp):
        for s in range(NX):
            sp.dma_start(xt[:, s * PIX:(s + 1) * PIX], x[s]).then_inc(x_in[s], 16)
        with sp.Fori(0, NP // NX - 1) as i:
            for s in range(NX):
                sp.wait_ge(S["vx"], i * (NX * NCH) + NCH * (s + 1))
                sp.dma_start(xt[:, s * PIX:(s + 1) * PIX], x[i * NX + (NX + s)]).then_inc(x_in[s], 16)

    @block.gpsimd
    def _(pool):
        def pool_pair(n, s, x_loads):
            pool.wait_ge(x_in[s], x_loads)
            pool.wait_ge(S["base"], past(n - 1))
            pool.wait_ge(S["qc"], past(n - 1))
            pool.wait_ge(S["pooled"], n)
            v = xt[:, s * PIX:(s + 1) * PIX].rearrange("p (h i w) -> p h i w", i=STRIDE, w=IMG)
            h = half[:, :].rearrange("p (h i w) -> p h i w", i=2, w=IMG)
            nc.gpsimd.tensor_tensor(h, v[:, :, 0:2], v[:, :, 2:4], ALU.add).then_inc(S["half"], 1)
            pool.wait_ge(S["half"], n + 1)
            q = quarter[:, :].rearrange("p (h w) -> p h w", w=IMG)
            nc.gpsimd.tensor_tensor(q, h[:, :, 0], h[:, :, 1], ALU.add).then_inc(S["quarter"], 1)
            pool.wait_ge(S["quarter"], n + 1)
            q = quarter[:, :].rearrange("p (t j) -> p t j", j=4)
            e = eighth[:, :].rearrange("p (t j) -> p t j", j=2)
            nc.gpsimd.tensor_tensor(e, q[:, :, 0:2], q[:, :, 2:4], ALU.add).then_inc(S["eighth"], 1)
            pool.wait_ge(S["eighth"], n + 1)
            o = pooled[:, (s % 2) * TOK:(s % 2 + 1) * TOK]
            nc.gpsimd.tensor_tensor(o, e[:, :, 0], e[:, :, 1], ALU.add).then_inc(S["pooled"], 1)

        for s in range(2):
            pool_pair(s, s, 16)

        def step(i, s, last):
            n = i * NX + s
            pool.wait_ge(S["exp"], n + 1)
            pool.wait_ge(S["rstd"], n + 1)
            pool.wait_ge(S["attn"], n)
            nc.gpsimd.tensor_tensor(er[:, :], expd[:, :], rstd[:, (s % 2) * CH:(s % 2 + 1) * CH], ALU.mult).then_inc(S["er"], 1)
            pool.wait_ge(S["er"], n + 1)
            pool.wait_ge(S["rden"], n + 1)
            pool.wait_ge(S["wide_mm"], n * NCH)
            nc.gpsimd.tensor_tensor(patches(attn[:, :]), patches(er[:, :]), over_pixels(rden[:, :], CP), ALU.mult).then_inc(S["attn"], 1)
            if not (last and s >= NX - 2):
                t = (s + 2) % NX
                pool_pair(n + 2, t, 16 * i + 16 * ((s + 2) // NX + 1))

        for s in range(NX):
            step(0, s, False)
        with pool.Fori(1, NP // NX - 1) as i:
            for s in range(NX):
                step(i, s, False)
        for s in range(NX):
            step(NP // NX - 1, s, True)

    @block.tensor
    def _(pe):
        pe.wait_ge(S["prep_dve"], 3)
        mm(ps[:, 0, 0:P], K("centre"), wks[:, :])
        mm(ps[:, 0, P:2 * P], K("centre"), wvs[:, :])
        mm(ps[:, 1, 0:1], W("tok_wv"), W("L0_tok_ln_kv_b")).then_inc(S["prep_pe"], 1)
        pe.wait_ge(S["prep_act"], 3)
        mm(ps[:, 1, 1:2], W("tok_wp"), bv).then_inc(S["prep2_pe"], 1)
        pe.wait_ge(S["prep2_act"], 1)

        def stage_a(n, s, x_loads, first=False):
            def var_mm(c0):
                pe.wait_ge(S["sq"], n * NCH + c0 + 4)
                if c0 == 0:
                    pe.wait_ge(S["rstd"], n)
                for c in range(c0, c0 + 4):
                    g = c % 4
                    m = mm(ps[32 * g:32 * g + 32, VAR, :], K("var_sel")[:, 32 * (c // 4):32 * (c // 4) + 32], sq[:, c * CH:(c + 1) * CH],
                           start=(c < 4), stop=(c >= 4))
                if c0:
                    m.then_inc(S["var"], 1)

            pe.wait_ge(x_in[s], x_loads)
            for c in range(NCH):
                if c == 0:
                    pe.wait_ge(S["qs"], n)
                elif c == 1 and not first:
                    pe.wait_ge(S["tok"], past(n - 1))
                elif c >= 2:
                    pe.wait_ge(S["sq"], n * NCH + c - 1)
                pixel_mm(ps[:, c % 2, :], K("centre"), s, c).then_inc(S["cx"], 1)
                if c == 5:
                    var_mm(0)
            pe.wait_ge(S["pooled"], n + 1)
            pe.wait_ge(S["sq"], n * NCH + 7)
            mm(ps[:, 0, 0:TOK], K("centre"), pooled[:, (s % 2) * TOK:(s % 2 + 1) * TOK]).then_inc(S["qc"], 1)
            var_mm(4)
            pe.wait_ge(S["qsq"], n + 1)
            mm(ps[:, 1, 0:TOK], K("mean"), qsq[:, :]).then_inc(S["qv"], 1)
            pe.wait_ge(S["qa"], n + 1)
            mm(ps[:, 0, 0:TOK], W("tok_wq"), qa[:, :]).then_inc(S["qq"], 1)

        def stage_b(n, s):
            def score_mm(c0):
                pe.wait_ge(S["kq"], n * NCH + c0 + 4)
                if c0 == 0:
                    pe.wait_ge(S["s1"], n)
                for c in range(c0, c0 + 4):
                    g = c % 4
                    m = mm(ps[32 * g:32 * g + 32, SCORE, :], K("head_sel")[:, 32 * (c // 4):32 * (c // 4) + 32], kq[:, c * CH:(c + 1) * CH],
                           start=(c < 4), stop=(c >= 4))
                if c0:
                    m.then_inc(S["scored"], 1)

            for c in range(NCH):
                pe.wait_ge(S["zmul"], n * NCH) if c < 2 else pe.wait_ge(S["kq"], n * NCH + c - 1)
                pixel_mm(ps[:, 2 + c % 2, :], wkc[:, :], s, c).then_inc(S["kx"], 1)
                if c == 5:
                    score_mm(0)
            score_mm(4)

        def stage_c(n, s, last):
            pe.wait_ge(S["attn"], n + 1)
            for c in range(NCH):
                pe.wait_ge(S["wide"], n * NCH + max(c - 1, 0))
                mm(ps[:, 6 + c % 2, :], K("spread")[:, c * P:(c + 1) * P], attn[:, :]).then_inc(S["wide_mm"], 1)
                if c >= 2:
                    pe.wait_ge(S["zmul"], n * NCH + c - 1)
                pixel_mm(ps[:, 2 + c % 2, :], wvc[:, :], s, c).then_inc(S["vx"], 1)
            pe.wait_ge(S["zred"], n * NCH + NCH)
            pe.wait_ge(S["qr"], n + (1 if last else 2))
            mm(ps[:, 1, 0:TOK], W("tok_wp"), z[:, :]).then_inc(S["pj"], 1)

        stage_a(0, 0, 16, first=True)

        def step(i, s, last):
            n = i * NX + s
            stage_b(n, s)
            end = last and s == NX - 1
            if not end:
                stage_a(n + 1, (s + 1) % NX, i * 16 + 16 * ((s + 1) // NX + 1))
            stage_c(n, s, end)

        for s in range(NX):
            step(0, s, False)
        with pe.Fori(1, NP // NX - 1) as i:
            for s in range(NX):
                step(i, s, False)
        for s in range(NX):
            step(NP // NX - 1, s, True)

    @block.scalar
    def _(act):
        A = nc.scalar.activation
        act.wait_ge(S["prep_pe"], 1)
        A(wkc[:, :], ps[:, 0, 0:P], ACT.Copy).then_inc(S["prep_act"], 1)
        A(wvc[:, :], ps[:, 0, P:2 * P], ACT.Copy).then_inc(S["prep_act"], 1)
        A(bv, ps[:, 1, 0:1], ACT.Copy).then_inc(S["prep_act"], 1)
        act.wait_ge(S["prep2_pe"], 1)
        A(pbz, ps[:, 1, 1:2], ACT.Identity, bias=W("L0_tok_proj_b")).then_inc(S["prep2_act"], 1)
        act.wait_ge(S["prep2_act"], 1)

        def stage_a(n, s, exp=None):
            def square(c):
                act.wait_ge(S["cx"], n * NCH + c + 1)
                if c == 0:
                    act.wait_ge(S["var"], n)
                A(sq[:, c * CH:(c + 1) * CH], ps[:, c % 2, :], ACT.Square).then_inc(S["sq"], 1)

            for c in range(4):
                square(c)
            if exp is not None:
                exp()
            for c in range(4, NCH):
                square(c)
            act.wait_ge(S["qc"], n + 1)
            act.wait_ge(S["qv"], n)
            A(qsq[:, :], ps[:, 0, 0:TOK], ACT.Square, scale=1.0 / PX).then_inc(S["qsq"], 1)
            act.wait_ge(S["var"], n + 1)
            if exp is not None:
                act.wait_ge(S["er"], past(n - 1))
                act.wait_ge(S["s1"], past(n - 1))
            A(rstd[:, (s % 2) * CH:(s % 2 + 1) * CH], ps[:, VAR, :], ACT.Abs_reciprocal_sqrt, bias=K("eps")).then_inc(S["rstd"], 1)
            act.wait_ge(S["qv"], n + 1)
            act.wait_ge(S["qn"], n)
            A(qr[:, :], ps[:, 1, 0:TOK], ACT.Abs_reciprocal_sqrt, bias=K("eps")).then_inc(S["qr"], 1)
            act.wait_ge(S["qn"], n + 1)
            act.wait_ge(S["qq"], n)
            A(qa[:, :], qn[:, :], ACT.Identity, bias=W("L0_tok_ln_q_b"), scale=lnq16).then_inc(S["qa"], 1)
            if exp is not None:
                act.wait_ge(S["tok"], past(n - 1))
            A(base[:, (s % 2) * TOK:(s % 2 + 1) * TOK], pooled[:, (s % 2) * TOK:(s % 2 + 1) * TOK], ACT.Identity,
              bias=pbz, scale=1.0 / PX).then_inc(S["base"], 1)
            act.wait_ge(S["qq"], n + 1)
            if exp is not None:
                act.wait_ge(S["kq"], past((n - 1) * NCH))
            A(qs[:, (s % 2) * TOK:(s % 2 + 1) * TOK], ps[:, 0, 0:TOK], ACT.Copy, scale=float(C) ** -0.5).then_inc(S["qs"], 1)

        def exp_pair(n):
            act.wait_ge(S["shifted"], n + 1)
            act.wait_ge(S["er"], n)
            act.wait_ge(S["den"], n)
            A(expd[:, :], shifted[:, :], ACT.Exp).then_inc(S["exp"], 1)

        act.wait_ge(S["prep_dve"], 3)
        stage_a(0, 0)

        def step(i, s, last):
            n = i * NX + s
            if last and s == NX - 1:
                exp_pair(n)
            else:
                stage_a(n + 1, (s + 1) % NX, lambda: exp_pair(n))
            for c in range(NCH):
                act.wait_ge(S["wide_mm"], n * NCH + c + 1)
                act.wait_ge(S["zmul"], n * NCH + max(c - 3, 0))
                A(wide[:, (c % 4) * CH:(c % 4 + 1) * CH], ps[:, 6 + c % 2, :], ACT.Copy).then_inc(S["wide"], 1)

        for s in range(NX):
            step(0, s, False)
        with act.Fori(1, NP // NX - 1) as i:
            for s in range(NX):
                step(i, s, False)
        for s in range(NX):
            step(NP // NX - 1, s, True)

    @block.vector
    def _(dve):
        V = nc.vector
        V.tensor_scalar(wks[:, :], W("tok_wk"), W("L0_tok_ln_kv_w"), None, ALU.mult).then_inc(S["prep_dve"], 1)
        V.tensor_scalar(wvs[:, :], W("tok_wv"), W("L0_tok_ln_kv_w"), None, ALU.mult).then_inc(S["prep_dve"], 1)
        V.tensor_scalar(lnq16, W("L0_tok_ln_q_w"), 1.0 / PX, None, ALU.mult).then_inc(S["prep_dve"], 1)

        def query_norm(n):
            dve.wait_ge(S["qr"], n + 1)
            dve.wait_ge(S["qa"], n)
            V.tensor_tensor(qn[:, :], ps[:, 0, 0:TOK], qr[:, :], ALU.mult).then_inc(S["qn"], 1)

        query_norm(0)

        def step(i, s, last):
            n = i * NX + s
            q = qs[:, (s % 2) * TOK:(s % 2 + 1) * TOK]
            dve.wait_ge(S["qs"], n + 1)
            dve.wait_ge(S["scored"], n)
            for c in range(NCH):
                dve.wait_ge(S["kx"], n * NCH + c + 1)
                V.tensor_tensor(patches(kq[:, c * CH:(c + 1) * CH]), patches(ps[:, 2 + c % 2, :]),
                                over_pixels(q[:, c * CP:(c + 1) * CP], CP), ALU.mult).then_inc(S["kq"], 1)
            dve.wait_ge(S["scored"], n + 1)
            dve.wait_ge(S["rstd"], n + 1)
            dve.wait_ge(S["shifted"], n)
            V.tensor_tensor(score[:, :], ps[:, SCORE, :], rstd[:, (s % 2) * CH:(s % 2 + 1) * CH], ALU.mult).then_inc(S["s1"], 1)
            dve.wait_ge(S["s1"], n + 1)
            V.tensor_reduce(top[:, :], patches(score[:, :]), AX.X, ALU.max).then_inc(S["top"], 1)
            dve.wait_ge(S["top"], n + 1)
            dve.wait_ge(S["exp"], n)
            V.tensor_tensor(patches(shifted[:, :]), patches(score[:, :]), over_pixels(top[:, :], CP), ALU.subtract).then_inc(S["shifted"], 1)
            dve.wait_ge(S["exp"], n + 1)
            dve.wait_ge(S["rden"], n)
            V.tensor_reduce(den[:, :], patches(expd[:, :]), AX.X, ALU.add).then_inc(S["den"], 1)
            dve.wait_ge(S["den"], n + 1)
            dve.wait_ge(S["attn"], n)
            V.reciprocal(rden[:, :], den[:, :]).then_inc(S["rden"], 1)
            if not (last and s == NX - 1):
                query_norm(n + 1)

            def reduce(c):
                dve.wait_ge(S["zmul"], n * NCH + c + 1)
                if c == 0:
                    dve.wait_ge(S["pj"], n)
                V.tensor_reduce(z[:, c * CP:(c + 1) * CP], patches(zp[:, (c % 2) * CH:(c % 2 + 1) * CH]), AX.X, ALU.add).then_inc(S["zred"], 1)

            for c in range(NCH):
                dve.wait_ge(S["vx"], n * NCH + c + 1)
                dve.wait_ge(S["wide"], n * NCH + c + 1)
                dve.wait_ge(S["zred"], n * NCH + max(c - 1, 0))
                V.tensor_tensor(zp[:, (c % 2) * CH:(c % 2 + 1) * CH], ps[:, 2 + c % 2, :],
                                wide[:, (c % 4) * CH:(c % 4 + 1) * CH], ALU.mult).then_inc(S["zmul"], 1)
                if c:
                    reduce(c - 1)
            reduce(NCH - 1)
            dve.wait_ge(S["pj"], n + 1)
            dve.wait_ge(S["base"], n + 1)
            o = H[:, bass.ds(i * (NX * TOK) + s * TOK, TOK)]
            V.tensor_tensor(o, ps[:, 1, 0:TOK], base[:, (s % 2) * TOK:(s % 2 + 1) * TOK], ALU.add).then_inc(S["tok"], 1)

        for s in range(NX):
            step(0, s, False)
        with dve.Fori(1, NP // NX - 1) as i:
            for s in range(NX):
                step(i, s, False)
        for s in range(NX):
            step(NP // NX - 1, s, True)


U = 2
UT = U * TOK
NU = NP // U
QT = UT // P
NT = 2 * QT


def rounds(eng, body):
    body(0)
    with eng.Fori(1, NU // 2) as i:
        body(i)


class Norm:
    PARTS = "c sq v r x"

    def __init__(self, nc, S, K, name, ps, mean_bank, var_bank, sq, r):
        self.nc, self.S, self.K, self.name, self.ps = nc, S, K, name, ps
        self.mb, self.vb, self.sq, self.r = mean_bank, var_bank, sq, r

    @staticmethod
    def names(*norms):
        return " ".join(f"{n}_{p}" for n in norms for p in Norm.PARTS.split())

    def centre(self, src, s):
        self.nc.tensor.matmul(self.ps[:, 4 * s + self.mb, :], self.K("centre"), src, start=True, stop=True)\
            .then_inc(self.S[self.name + "_c"], 1)

    def square(self, act, n, s):
        act.wait_ge(self.S[self.name + "_c"], n + 1)
        self.nc.scalar.activation(self.sq[s], self.ps[:, 4 * s + self.mb, :], ACT.Square).then_inc(self.S[self.name + "_sq"], 1)

    def variance(self, pe, n, s):
        pe.wait_ge(self.S[self.name + "_sq"], n + 1)
        self.nc.tensor.matmul(self.ps[:, 4 * s + self.vb, :], self.K("mean"), self.sq[s], start=True, stop=True)\
            .then_inc(self.S[self.name + "_v"], 1)

    def rstd(self, act, n, s):
        act.wait_ge(self.S[self.name + "_v"], n + 1)
        self.nc.scalar.activation(self.r[s], self.ps[:, 4 * s + self.vb, :], ACT.Abs_reciprocal_sqrt, bias=self.K("eps"))\
            .then_inc(self.S[self.name + "_r"], 1)

    def scale(self, dve, n, s, out):
        dve.wait_ge(self.S[self.name + "_r"], n + 1)
        self.nc.vector.tensor_tensor(out, self.ps[:, 4 * s + self.mb, :], self.r[s], ALU.mult).then_inc(self.S[self.name + "_x"], 1)


def attention(nc, ctx, K, W, H, psum):
    NB = TOK // 128
    BK = 64
    S = Sems(nc, ctx, "at", "sp0 sp1 sp2 sp3 sp4 sp5 sp6 "
             + Norm.names("n1", "n2", "n3") +
             " tn q kv qsq qv qm qr qn ksq kss ksm kr kn v kpvp kpt vp sc mx sh ex den rden w wt wts ao aos wo o1 o2 o3")

    def sb(name, cols):
        t = ctx.enter_context(nc.sbuf_tensor("at_" + name, [P, 2, cols], F32))
        return [t[:, s, :] for s in range(2)]

    sq, r, xn, tn = sb("sq", UT), sb("r", UT), sb("xn", UT), sb("tn", UT)
    qm, qr, qn = sb("qm", UT), sb("qr", UT), sb("qn", UT)
    ksq, kn, v = sb("ksq", UT), sb("kn", UT), sb("v", UT)
    kss, ksm, kr = sb("kss", NT), sb("ksm", NT), sb("kr", NT)
    kpt, vp = sb("kpt", U * P), sb("vp", U * P)
    sh, ex, wts = sb("sh", NT * P), sb("ex", NT * P), sb("wts", NT * P)
    mx, den, rden = sb("mx", NT), sb("den", NT), sb("rden", NT)
    ao, o1, o2, o3 = sb("ao", UT), sb("o1", UT), sb("o2", UT), sb("o3", UT)
    sp_ = ctx.enter_context(nc.sbuf_tensor("at_softplus", [P, 8], F32))
    neg, low, el, onep, ln1, pos, sc = (sp_[:, k:k + 1] for k in range(7))
    ps = psum
    n1 = Norm(nc, S, K, "n1", ps, 0, 1, sq, r)
    n2 = Norm(nc, S, K, "n2", ps, 0, 1, sq, r)
    n3 = Norm(nc, S, K, "n3", ps, 2, 3, sq, r)

    def h(i, s):
        return H[:, bass.ds(i * (2 * UT) + s * UT, UT)]

    def bank(s, b, n=1):
        return ps[:, 4 * s + b:4 * s + b + n, :].rearrange("p a b -> p (a b)")

    def kv(s):
        return bank(s, 2, 2).rearrange("p (t m c) -> p t m c", t=QT, m=2)

    def tiles(v, n=NT):
        return v.rearrange("p (t k) -> p t k", t=n)

    def over(v, k):
        return v.unsqueeze(2).broadcast_to([P, v.shape[1], k])

    block = ctx.enter_context(nc.Block())

    @block.tensor
    def _(pe):
        mm = nc.tensor.matmul

        def body(i):
            for s in (0, 1):
                pe.wait_ge(S["n3_x"], past(2 * i + s - 1))
                n1.centre(h(i, s), s)
            for s in (0, 1):
                n1.variance(pe, 2 * i + s, s)
            for s in (0, 1):
                pe.wait_ge(S["tn"], 2 * i + s + 1)
                mm(ps[:, 4 * s, :], W("at_wq"), tn[s], start=True, stop=True).then_inc(S["q"], 1)
                for t in range(QT):
                    m = mm(bank(s, 2, 2)[:, 256 * t:256 * t + 256], tn[s][:, P * t:P * t + P], W("at_wkv"), start=True, stop=True)
                m.then_inc(S["kv"], 1)
            for s in (0, 1):
                pe.wait_ge(S["qsq"], 2 * i + s + 1)
                mm(ps[:, 4 * s + 1, :], K("mean"), sq[s], start=True, stop=True).then_inc(S["qv"], 1)
            for s in (0, 1):
                pe.wait_ge(S["kn"], 2 * i + s + 1)
                pe.wait_ge(S["v"], 2 * i + s + 1)
                pe.wait_ge(S["qn"], 2 * i + s + 1)
                for j in range(U):
                    for t in range(NB):
                        c = P * (NB * j + t)
                        mm(bank(s, 0)[:, P * j + BK * t:P * j + BK * t + BK], kn[s][:, c:c + P], W("at_e"), start=True, stop=True)
                        m = mm(ps[BK * t:BK * t + BK, 4 * s, 256 + P * j:256 + P * j + P], W("at_f"), v[s][:, c:c + P], start=True, stop=True)
                m.then_inc(S["kpvp"], 1)
            for s in (0, 1):
                pe.wait_ge(S["kpt"], 2 * i + s + 1)
                for j in range(U):
                    for img in range(2):
                        lo = 64 * img
                        for t in range(NB):
                            k = (img * U + j) * NB + t
                            m = mm(bank(s, 2, 2)[:, P * k:P * k + P], qn[s][lo:lo + 64, P * (NB * j + t):P * (NB * j + t) + P],
                                   kpt[s][lo:lo + 64, P * j:P * j + P], start=True, stop=True)
                m.then_inc(S["sc"], 1)
            for s in (0, 1):
                pe.wait_ge(S["w"], 2 * i + s + 1)
                pe.wait_ge(S["vp"], 2 * i + s + 1)
                for k in range(NT):
                    m = nc.tensor.transpose(bank(s, 0, 2)[:, P * k:P * k + P], ex[s][:, P * k:P * k + P], K("ident"))
                m.then_inc(S["wt"], 1)
            for s in (0, 1):
                pe.wait_ge(S["wts"], 2 * i + s + 1)
                for j in range(U):
                    for img in range(2):
                        k = (img * U + j) * TOK
                        m = mm(ps[64 * img:64 * img + 64, 4 * s + 2, TOK * j:TOK * j + TOK], vp[s][:, P * j + 64 * img:P * j + 64 * img + 64],
                               wts[s][:, k:k + TOK], start=True, stop=True)
                m.then_inc(S["ao"], 1)
            for s in (0, 1):
                pe.wait_ge(S["aos"], 2 * i + s + 1)
                mm(ps[:, 4 * s + 3, :], W("at_wo"), ao[s], start=True, stop=True).then_inc(S["wo"], 1)
            for s in (0, 1):
                pe.wait_ge(S["o1"], 2 * i + s + 1)
                n2.centre(o1[s], s)
            for s in (0, 1):
                n2.variance(pe, 2 * i + s, s)
            for s in (0, 1):
                pe.wait_ge(S["o3"], 2 * i + s + 1)
                n3.centre(o3[s], s)
            for s in (0, 1):
                n3.variance(pe, 2 * i + s, s)

        rounds(pe, body)

    @block.scalar
    def _(act):
        A = nc.scalar.activation
        act.wait_ge(S["sp1"], 1)
        A(el, low, ACT.Exp).then_inc(S["sp2"], 1)
        act.wait_ge(S["sp3"], 1)
        A(ln1, onep, ACT.Ln).then_inc(S["sp4"], 1)
        act.wait_ge(S["sp6"], 1)

        def body(i):
            for s in (0, 1):
                n1.square(act, 2 * i + s, s)
            for s in (0, 1):
                n1.rstd(act, 2 * i + s, s)
            for s in (0, 1):
                act.wait_ge(S["n1_x"], 2 * i + s + 1)
                A(tn[s], xn[s], ACT.Identity, bias=W("L0_attn_b1"), scale=W("L0_attn_g1")).then_inc(S["tn"], 1)
            for s in (0, 1):
                act.wait_ge(S["q"], 2 * i + s + 1)
                A(sq[s], ps[:, 4 * s, :], ACT.Square).then_inc(S["qsq"], 1)
                act.wait_ge(S["kv"], 2 * i + s + 1)
                A(tiles(ksq[s], QT), kv(s)[:, :, 0, :], ACT.Square).then_inc(S["ksq"], 1)
                A(tiles(v[s], QT), kv(s)[:, :, 1, :], ACT.Copy).then_inc(S["v"], 1)
            for s in (0, 1):
                act.wait_ge(S["qm"], 2 * i + s + 1)
                A(qr[s], qm[s], ACT.Abs_reciprocal_sqrt).then_inc(S["qr"], 1)
                act.wait_ge(S["ksm"], 2 * i + s + 1)
                A(kr[s], ksm[s], ACT.Abs_reciprocal_sqrt).then_inc(S["kr"], 1)
            for s in (0, 1):
                act.wait_ge(S["kpvp"], 2 * i + s + 1)
                A(kpt[s], bank(s, 0)[:, 0:U * P], ACT.Copy).then_inc(S["kpt"], 1)
                A(vp[s], bank(s, 0)[:, U * P:2 * U * P], ACT.Copy).then_inc(S["vp"], 1)
            for s in (0, 1):
                act.wait_ge(S["sh"], 2 * i + s + 1)
                A(sh[s], sh[s], ACT.Exp, scale=sc).then_inc(S["ex"], 1)
            for s in (0, 1):
                act.wait_ge(S["wt"], 2 * i + s + 1)
                A(wts[s], bank(s, 0, 2), ACT.Copy).then_inc(S["wts"], 1)
            for s in (0, 1):
                act.wait_ge(S["ao"], 2 * i + s + 1)
                A(ao[s], ps[:, 4 * s + 2, :], ACT.Copy).then_inc(S["aos"], 1)
            for s in (0, 1):
                n2.square(act, 2 * i + s, s)
            for s in (0, 1):
                n2.rstd(act, 2 * i + s, s)
            for s in (0, 1):
                act.wait_ge(S["n2_x"], 2 * i + s + 1)
                A(o2[s], xn[s], ACT.Identity, bias=W("L0_attn_b2"), scale=W("L0_attn_g2")).then_inc(S["o2"], 1)
            for s in (0, 1):
                n3.square(act, 2 * i + s, s)
            for s in (0, 1):
                n3.rstd(act, 2 * i + s, s)

        rounds(act, body)

    @block.vector
    def _(dve):
        V = nc.vector
        x = W("L0_attn_scale")
        V.tensor_scalar(neg, x, -1.0, None, ALU.mult).then_inc(S["sp0"], 1)
        dve.wait_ge(S["sp0"], 1)
        V.tensor_tensor(low, x, neg, ALU.min).then_inc(S["sp1"], 1)
        dve.wait_ge(S["sp2"], 1)
        V.tensor_scalar(onep, el, 1.0, None, ALU.add).then_inc(S["sp3"], 1)
        dve.wait_ge(S["sp4"], 1)
        V.scalar_tensor_tensor(pos, x, 0.0, ln1, ALU.max, ALU.add).then_inc(S["sp5"], 1)
        dve.wait_ge(S["sp5"], 1)
        V.tensor_scalar(sc, pos, float(C) ** -0.5, None, ALU.mult).then_inc(S["sp6"], 1)

        def body(i):
            for s in (0, 1):
                n1.scale(dve, 2 * i + s, s, xn[s])
            for s in (0, 1):
                dve.wait_ge(S["ksq"], 2 * i + s + 1)
                V.tensor_reduce(kss[s], tiles(ksq[s]), AX.X, ALU.add).then_inc(S["kss"], 1)
                dve.wait_ge(S["qv"], 2 * i + s + 1)
                V.tensor_scalar(qm[s], ps[:, 4 * s + 1, :], float(C), 1e-24, ALU.mult, ALU.max).then_inc(S["qm"], 1)
                dve.wait_ge(S["kss"], 2 * i + s + 1)
                V.tensor_scalar(ksm[s], kss[s], 1e-24, None, ALU.max).then_inc(S["ksm"], 1)
            for s in (0, 1):
                dve.wait_ge(S["qr"], 2 * i + s + 1)
                V.tensor_tensor(qn[s], ps[:, 4 * s, :], qr[s], ALU.mult).then_inc(S["qn"], 1)
                dve.wait_ge(S["kr"], 2 * i + s + 1)
                for m in range(2):
                    o = kn[s].rearrange("p (t m c) -> p t m c", t=QT, m=2)[:, :, m, :]
                    k = kr[s].rearrange("p (t m) -> p t m", m=2)[:, :, m]
                    last = V.tensor_tensor(o, kv(s)[:, :, 0, 64 * m:64 * m + 64], over(k, 64), ALU.mult)
                last.then_inc(S["kn"], 1)
            for s in (0, 1):
                dve.wait_ge(S["sc"], 2 * i + s + 1)
                V.tensor_reduce(mx[s], tiles(bank(s, 2, 2)), AX.X, ALU.max).then_inc(S["mx"], 1)
                dve.wait_ge(S["mx"], 2 * i + s + 1)
                V.tensor_tensor(tiles(sh[s]), tiles(bank(s, 2, 2)), over(mx[s], P), ALU.subtract).then_inc(S["sh"], 1)
            for s in (0, 1):
                dve.wait_ge(S["ex"], 2 * i + s + 1)
                V.tensor_reduce(den[s], tiles(sh[s]), AX.X, ALU.add).then_inc(S["den"], 1)
                dve.wait_ge(S["den"], 2 * i + s + 1)
                V.reciprocal(rden[s], den[s]).then_inc(S["rden"], 1)
                dve.wait_ge(S["rden"], 2 * i + s + 1)
                V.tensor_tensor(tiles(ex[s]), tiles(sh[s]), over(rden[s], P), ALU.mult).then_inc(S["w"], 1)
            for s in (0, 1):
                dve.wait_ge(S["wo"], 2 * i + s + 1)
                V.scalar_tensor_tensor(o1[s], ps[:, 4 * s + 3, :], 0.1, h(i, s), ALU.mult, ALU.add).then_inc(S["o1"], 1)
            for s in (0, 1):
                n2.scale(dve, 2 * i + s, s, xn[s])
            for s in (0, 1):
                dve.wait_ge(S["o2"], 2 * i + s + 1)
                V.tensor_tensor(o3[s], o2[s], h(i, s), ALU.add).then_inc(S["o3"], 1)
            for s in (0, 1):
                n3.scale(dve, 2 * i + s, s, h(i, s))

        rounds(dve, body)


def routed_ffn(nc, ctx, K, W, H, psum):
    KEPT = max(1, TOK // 2) - 1
    MH = 2
    S = Sems(nc, ctx, "ff", Norm.names("n1") + " hs wb wbs dg wc gt eq cnt f fr ft fts hid g0 g1 y yf o")

    def sb(name, cols):
        t = ctx.enter_context(nc.sbuf_tensor("ff_" + name, [P, 2, cols], F32))
        return [t[:, s, :] for s in range(2)]

    sq, r, hs, wbs, dg = sb("sq", UT), sb("r", UT), sb("hs", UT), sb("wbs", 2 * UT), sb("dg", 2 * UT)
    wc, gt, eq, cnt, f = (sb(n, NT) for n in ("wc", "gt", "eq", "cnt", "f"))
    fr, fts, yf, o = sb("fr", UT), sb("fts", UT), sb("yf", UT), sb("o", UT)
    g = sb("g", 2 * MH * UT)
    junk = ctx.enter_context(nc.sbuf_tensor("ff_junk", [P, NT, TOK], BF16))
    junk2 = ctx.enter_context(nc.sbuf_tensor("ff_junk2", [P, NT, TOK], BF16))
    ps = psum
    n1 = Norm(nc, S, K, "n1", ps, 2, 3, sq, r)

    def h(i, s):
        return H[:, bass.ds(i * (2 * UT) + s * UT, UT)]

    def bank(s, b, n=1):
        return ps[:, 4 * s + b:4 * s + b + n, :].rearrange("p a b -> p (a b)")

    def tiles(v, n=NT):
        return v.rearrange("p (t k) -> p t k", t=n)

    block = ctx.enter_context(nc.Block())

    @block.tensor
    def _(pe):
        mm = nc.tensor.matmul

        def body(i):
            for s in (0, 1):
                pe.wait_ge(S["hs"], 2 * i + s + 1)
                pe.wait_ge(S[f"g{s}"], i * (2 * MH))
                for img in range(2):
                    m = mm(ps[:, 4 * s + img, :], W("ff_wr")[64 * img:64 * img + 64, :], hs[s][64 * img:64 * img + 64, :], start=True, stop=True)
                m.then_inc(S["wb"], 1)
            for k in range(2 * MH):
                img, half = k % 2, k // 2
                lo = 64 * img
                for s in (0, 1):
                    n = 2 * i + s
                    pe.wait_ge(S["wbs"], n + 1)
                    if k >= 2:
                        pe.wait_ge(S[f"g{s}"], i * (2 * MH) + k - 1)
                    mm(ps[:, 4 * s + img, :], W("ff_w1")[lo:lo + 64, P * half:P * half + P], hs[s][lo:lo + 64, :],
                       start=True, stop=True).then_inc(S["hid"], 1)
            for s in (0, 1):
                pe.wait_ge(S["fr"], 2 * i + s + 1)
                pe.wait_ge(S["n1_x"], past(2 * i + s - 1))
                for t in range(QT):
                    m = mm(ps[:, 4 * s + 2, P * t:P * t + P], fr[s][:, P * t:P * t + P], K("ident"), start=True, stop=True)
                m.then_inc(S["ft"], 1)
            for s in (0, 1):
                pe.wait_ge(S[f"g{s}"], i * (2 * MH) + 2 * MH)
                for half in range(MH):
                    for img in range(2):
                        k = 2 * half + img
                        m = mm(ps[64 * img:64 * img + 64, 4 * s + 3, :], W("ff_w2")[:, 64 * half:64 * half + 64], g[s][:, UT * k:UT * k + UT],
                               start=(half == 0), stop=(half == MH - 1))
                m.then_inc(S["y"], 1)
            for s in (0, 1):
                pe.wait_ge(S["o"], 2 * i + s + 1)
                n1.centre(o[s], s)
            for s in (0, 1):
                n1.variance(pe, 2 * i + s, s)

        rounds(pe, body)

    @block.scalar
    def _(act):
        A = nc.scalar.activation

        def body(i):
            for s in (0, 1):
                n = 2 * i + s
                act.wait_ge(S["n1_c"], past(n - 1))
                act.wait_ge(S["o"], past(n - 1))
                A(hs[s], h(i, s), ACT.Copy).then_inc(S["hs"], 1)
            for s in (0, 1):
                act.wait_ge(S["wb"], 2 * i + s + 1)
                A(wbs[s], bank(s, 0, 2), ACT.Identity, bias=W("L0_ffn_br")).then_inc(S["wbs"], 1)
            for k in range(2 * MH):
                for s in (0, 1):
                    n = 2 * i + s
                    act.wait_ge(S["hid"], i * (4 * MH) + 2 * k + s + 1)
                    A(g[s][:, UT * k:UT * k + UT], ps[:, 4 * s + k % 2, :], ACT.Gelu_apprx_tanh, bias=W("ff_b1")[:, k // 2:k // 2 + 1]).then_inc(S[f"g{s}"], 1)
            for s in (0, 1):
                act.wait_ge(S["ft"], 2 * i + s + 1)
                A(fts[s], ps[:, 4 * s + 2, :], ACT.Copy).then_inc(S["fts"], 1)
            for s in (0, 1):
                n1.square(act, 2 * i + s, s)
            for s in (0, 1):
                n1.rstd(act, 2 * i + s, s)

        rounds(act, body)

    @block.vector
    def _(dve):
        V = nc.vector

        def body(i):
            for s in (0, 1):
                n = 2 * i + s
                dve.wait_ge(S["wbs"], n + 1)
                dve.wait_ge(S["wc"], past(n - 1))
                V.tensor_tensor(tiles(dg[s]), tiles(wbs[s]), K("ident").unsqueeze(1).broadcast_to([P, NT, P]), ALU.mult).then_inc(S["dg"], 1)
            for s in (0, 1):
                n = 2 * i + s
                dve.wait_ge(S["dg"], n + 1)
                V.tensor_reduce(wc[s], tiles(dg[s]), AX.X, ALU.add).then_inc(S["wc"], 1)
            for s in (0, 1):
                n = 2 * i + s
                dve.wait_ge(S["wc"], n + 1)
                dve.wait_ge(S["cnt"], n)
                for k in range(NT):
                    row = wbs[s][:, TOK * (k // 2):TOK * (k // 2) + TOK]
                    a = V.tensor_scalar(junk[:, k, :], row, wc[s][:, k:k + 1], None, ALU.is_gt, ALU.add, accum_out=gt[s][:, k:k + 1])
                    b = V.scalar_tensor_tensor(junk2[:, k, :], row, wc[s][:, k:k + 1], K("earlier")[:, TOK * (k % 2):TOK * (k % 2) + TOK],
                                               ALU.is_equal, ALU.mult, accum_out=eq[s][:, k:k + 1])
                a.then_inc(S["gt"], 1)
                b.then_inc(S["eq"], 1)
                dve.wait_ge(S["gt"], n + 1)
                dve.wait_ge(S["eq"], n + 1)
                V.tensor_tensor(cnt[s], gt[s], eq[s], ALU.add).then_inc(S["cnt"], 1)
                dve.wait_ge(S["cnt"], n + 1)
                V.scalar_tensor_tensor(f[s], cnt[s], KEPT - 0.5, wc[s], ALU.is_lt, ALU.mult).then_inc(S["f"], 1)
                dve.wait_ge(S["f"], n + 1)
                for img in range(2):
                    d = fr[s].rearrange("p (t m c) -> p t m c", t=QT, m=2)[:, :, img, :]
                    last = V.tensor_copy(d, f[s][:, QT * img:QT * img + QT].unsqueeze(2).broadcast_to([P, QT, 64]))
                last.then_inc(S["fr"], 1)
            for s in (0, 1):
                n = 2 * i + s
                dve.wait_ge(S["y"], n + 1)
                dve.wait_ge(S["fts"], n + 1)
                V.scalar_tensor_tensor(yf[s], ps[:, 4 * s + 3, :], W("ff_b2"), fts[s], ALU.add, ALU.mult).then_inc(S["yf"], 1)
                dve.wait_ge(S["yf"], n + 1)
                V.scalar_tensor_tensor(o[s], hs[s], 2.0, yf[s], ALU.mult, ALU.add).then_inc(S["o"], 1)
            for s in (0, 1):
                n1.scale(dve, 2 * i + s, s, h(i, s))

        rounds(dve, body)


PI = 3.1415925


def holographic(nc, ctx, K, W, H, psum):
    S = Sems(nc, ctx, "ho", Norm.names("n1", "n2") +
             " pr0 pr1 pr2 pr3 pr4 pr5 pr6 pr7 pr8 sn0 sn1 wg gb hs t1 a1 t2 a2 vp vps g1 g1s vt vts k2 tk uk kf q2 tq uq qf sa sb sas sbs"
             " ct cts gd gt gg mr mi mrs mis rr ri pos df dg cb nb wo wos o")

    def sb(name, cols, n=2):
        t = ctx.enter_context(nc.sbuf_tensor("ho_" + name, [P, n, cols], F32))
        return [t[:, s, :] for s in range(n)]

    sq, r, hs = sb("sq", UT), sb("r", UT), sb("hs", UT)
    a1, a2, vps, vts = sb("a1", UT), sb("a2", UT), sb("vps", UT), sb("vts", UT)
    g1s = sb("g1s", UT)
    tk, uk, kf, tq, uq, qf = (sb(n, UT) for n in ("tk", "uk", "kf", "tq", "uq", "qf"))
    sa, sc_ = sb("sa", 2 * UT), sb("sc", UT)
    cts, gt, gg = sb("cts", UT), sb("gt", UT), sb("gg", UT)
    mr, mi, mrs, mis = (sb(n, UT) for n in ("mr", "mi", "mrs", "mis"))
    pos, df, cb, nb, wos, o = (sb(n, UT) for n in ("pos", "df", "cb", "nb", "wos", "o"))
    rr, ri = mr, mi
    tab = ctx.enter_context(nc.sbuf_tensor("ho_tab", [P, 14, TOK], F32))
    turns, whole, red1, red2, red3, red, mag, low, sinp, cosp, sinn, cosn = (tab[:, k, :] for k in range(12))
    wgd = ctx.enter_context(nc.sbuf_tensor("ho_wgd", [32, P], F32))
    gb = ctx.enter_context(nc.sbuf_tensor("ho_gb", [P, 2], F32))
    ps = psum
    n1 = Norm(nc, S, K, "n1", ps, 1, 2, sq, r)
    n2 = Norm(nc, S, K, "n2", ps, 1, 2, sq, r)

    def h(i, s):
        return H[:, bass.ds(i * (2 * UT) + s * UT, UT)]

    def bank(s, b, n=1):
        return ps[:, 4 * s + b:4 * s + b + n, :].rearrange("p a b -> p (a b)")

    def tiles(v, n):
        return v.rearrange("p (t k) -> p t k", t=n)

    def each(v, n):
        return v.unsqueeze(1).broadcast_to([P, n, v.shape[1]])

    block = ctx.enter_context(nc.Block())

    @block.tensor
    def _(pe):
        mm = nc.tensor.matmul
        pe.wait_ge(S["wg"], 1)

        def body(i):
            for s in (0, 1):
                n = 2 * i + s
                pe.wait_ge(S["hs"], n + 1)
                pe.wait_ge(S["n2_x"], past(n - 1))
                mm(ps[:, 4 * s, :], W("ho_wk1"), hs[s], start=True, stop=True).then_inc(S["t1"], 1)
                mm(ps[:, 4 * s + 1, :], W("ho_wq1"), hs[s], start=True, stop=True).then_inc(S["t2"], 1)
                mm(ps[:, 4 * s + 2, :], W("ho_wvp"), hs[s], start=True, stop=True).then_inc(S["vp"], 1)
                for t in range(QT):
                    m = mm(ps[:, 4 * s + 3, P * t:P * t + P], hs[s][:, P * t:P * t + P], W("ho_wvc"), start=True, stop=True)
                m.then_inc(S["vt"], 1)
            for s in (0, 1):
                n = 2 * i + s
                pe.wait_ge(S["a1"], n + 1)
                mm(ps[:, 4 * s, :], W("ho_wk2"), a1[s], start=True, stop=True).then_inc(S["k2"], 1)
                pe.wait_ge(S["a2"], n + 1)
                mm(ps[:, 4 * s + 1, :], W("ho_wq2"), a2[s], start=True, stop=True).then_inc(S["q2"], 1)
                pe.wait_ge(S["vps"], n + 1)
                mm(ps[0:32, 4 * s + 2, :], W("ho_wg1"), hs[s], start=True, stop=True).then_inc(S["g1"], 1)
                pe.wait_ge(S["vts"], n + 1)
                pe.wait_ge(S["g1s"], n + 1)
                mm(ps[:, 4 * s + 3, :], wgd[:, :], g1s[s][0:32, :], start=True, stop=True).then_inc(S["gd"], 1)
            for s in (0, 1):
                n = 2 * i + s
                pe.wait_ge(S["kf"], n + 1)
                pe.wait_ge(S["qf"], n + 1)
                for img in range(2):
                    lo = 64 * img
                    for j in range(U):
                        c = TOK * j
                        m = mm(ps[:, 4 * s + img, TOK * j:TOK * j + TOK], kf[s][lo:lo + 64, c:c + P], qf[s][lo:lo + 64, c:c + TOK], start=True, stop=True)
                m.then_inc(S["sa"], 1)
                pe.wait_ge(S["gt"], n + 1)
                for img in range(2):
                    lo = 64 * img
                    for j in range(U):
                        c = TOK * j + P
                        k = img * U + j
                        m = mm(ps[:, 4 * s + 2 + img, P * j:P * j + P], kf[s][lo:lo + 64, c:c + P], qf[s][lo:lo + 64, c:c + P], start=True, stop=True)
                m.then_inc(S["sb"], 1)
            for s in (0, 1):
                n = 2 * i + s
                pe.wait_ge(S["sas"], n + 1)
                pe.wait_ge(S["sbs"], n + 1)
                for j in range(U):
                    for img in range(2):
                        k = img * U + j
                        o_ = ps[64 * img:64 * img + 64, 4 * s, TOK * j:TOK * j + TOK]
                        v0 = vts[s][:, 2 * P * j + 64 * img:2 * P * j + 64 * img + 64]
                        v1 = vts[s][:, 2 * P * j + P + 64 * img:2 * P * j + P + 64 * img + 64]
                        mm(o_, v0, sa[s][:, TOK * k:TOK * k + TOK], start=True, stop=False, skip_group_check=True)
                        m = mm(o_[:, P:], v1, sc_[s][:, P * k:P * k + P], start=False, stop=True, skip_group_check=True)
                m.then_inc(S["ct"], 1)
            for s in (0, 1):
                pe.wait_ge(S["cb"], 2 * i + s + 1)
                n1.centre(cb[s], s)
            for s in (0, 1):
                n1.variance(pe, 2 * i + s, s)
            for s in (0, 1):
                pe.wait_ge(S["nb"], 2 * i + s + 1)
                mm(ps[:, 4 * s + 3, :], W("ho_wo"), nb[s], start=True, stop=True).then_inc(S["wo"], 1)
            for s in (0, 1):
                pe.wait_ge(S["o"], 2 * i + s + 1)
                n2.centre(o[s], s)
            for s in (0, 1):
                n2.variance(pe, 2 * i + s, s)

        rounds(pe, body)

    @block.scalar
    def _(act):
        A = nc.scalar.activation
        act.wait_ge(S["pr6"], 1)
        A(sinp, red, ACT.Sin).then_inc(S["sn0"], 1)
        act.wait_ge(S["pr8"], 1)
        A(cosp, low, ACT.Sin).then_inc(S["sn1"], 1)
        act.wait_ge(S["gb"], 1)

        def body(i):
            for s in (0, 1):
                act.wait_ge(S["o"], past(2 * i + s - 1))
                A(hs[s], h(i, s), ACT.Copy).then_inc(S["hs"], 1)
            for s in (0, 1):
                n = 2 * i + s
                act.wait_ge(S["t1"], n + 1)
                A(a1[s], ps[:, 4 * s, :], ACT.Tanh, bias=W("L1_attn_bk1")).then_inc(S["a1"], 1)
                act.wait_ge(S["t2"], n + 1)
                A(a2[s], ps[:, 4 * s + 1, :], ACT.Tanh, bias=W("L1_attn_bq1")).then_inc(S["a2"], 1)
                act.wait_ge(S["vp"], n + 1)
                A(vps[s], ps[:, 4 * s + 2, :], ACT.Identity, bias=W("L1_attn_bvp")).then_inc(S["vps"], 1)
            for s in (0, 1):
                n = 2 * i + s
                act.wait_ge(S["g1"], n + 1)
                A(g1s[s][0:32, :], ps[0:32, 4 * s + 2, :], ACT.Relu, bias=W("ho_bg1")).then_inc(S["g1s"], 1)
                act.wait_ge(S["k2"], n + 1)
                A(tk[s], ps[:, 4 * s, :], ACT.Tanh, bias=W("ho_bk2")).then_inc(S["tk"], 1)
                act.wait_ge(S["q2"], n + 1)
                A(tq[s], ps[:, 4 * s + 1, :], ACT.Tanh, bias=W("ho_bq2")).then_inc(S["tq"], 1)
                act.wait_ge(S["gd"], n + 1)
                A(gt[s], ps[:, 4 * s + 3, :], ACT.Tanh, bias=gb[:, 1:2], scale=0.5).then_inc(S["gt"], 1)
            for s in (0, 1):
                n = 2 * i + s
                act.wait_ge(S["uk"], n + 1)
                A(kf[s], uk[s], ACT.Sin, bias=K("turn_bias"), scale=K("turn_scale")).then_inc(S["kf"], 1)
                act.wait_ge(S["uq"], n + 1)
                A(qf[s], uq[s], ACT.Sin, bias=K("turn_bias"), scale=K("turn_scale")).then_inc(S["qf"], 1)
            for s in (0, 1):
                n1.square(act, 2 * i + s, s)
            for s in (0, 1):
                n1.rstd(act, 2 * i + s, s)
            for s in (0, 1):
                act.wait_ge(S["n1_x"], 2 * i + s + 1)
                A(nb[s], df[s], ACT.Identity, bias=W("L1_attn_ln_b"), scale=W("L1_attn_ln_g")).then_inc(S["nb"], 1)
            for s in (0, 1):
                act.wait_ge(S["wo"], 2 * i + s + 1)
                A(wos[s], ps[:, 4 * s + 3, :], ACT.Identity, bias=W("L1_attn_bo")).then_inc(S["wos"], 1)
            for s in (0, 1):
                n2.square(act, 2 * i + s, s)
            for s in (0, 1):
                n2.rstd(act, 2 * i + s, s)

        rounds(act, body)

    @block.gpsimd
    def _(pool):
        G = nc.gpsimd
        pool.wait_ge(S["sn1"], 1)

        def body(i):
            for s in (0, 1):
                n = 2 * i + s
                pool.wait_ge(S["vps"], n + 1)
                pool.wait_ge(S["pos"], past(n - 1))
                G.tensor_tensor(tiles(mr[s], U), tiles(vps[s], U), each(cosp, U), ALU.mult).then_inc(S["mr"], 1)
                G.tensor_tensor(tiles(mi[s], U), tiles(vps[s], U), each(sinp, U), ALU.mult).then_inc(S["mi"], 1)

        rounds(pool, body)

    @block.vector
    def _(dve):
        V = nc.vector
        V.tensor_tensor(wgd[:, :], W("ho_wg2a"), W("ho_wg2b"), ALU.subtract).then_inc(S["wg"], 1)
        V.tensor_tensor(gb[:, 0:1], W("ho_bg2a"), W("ho_bg2b"), ALU.subtract).then_inc(S["pr0"], 1)
        dve.wait_ge(S["pr0"], 1)
        V.tensor_scalar(gb[:, 1:2], gb[:, 0:1], 0.5, None, ALU.mult).then_inc(S["gb"], 1)
        C1, C2 = 6.28125, 0.0019350051879882812
        C3 = 2 * np.pi - C1 - C2
        MAGIC = 1.5 * 2.0 ** 23
        ph = W("ho_phases")
        V.tensor_scalar(turns, ph, 1 / (2 * np.pi), MAGIC, ALU.mult, ALU.add).then_inc(S["pr1"], 1)
        dve.wait_ge(S["pr1"], 1)
        V.tensor_scalar(whole, turns, -MAGIC, None, ALU.add).then_inc(S["pr2"], 1)
        dve.wait_ge(S["pr2"], 1)
        V.scalar_tensor_tensor(red1, whole, -C1, ph, ALU.mult, ALU.add).then_inc(S["pr3"], 1)
        dve.wait_ge(S["pr3"], 1)
        V.scalar_tensor_tensor(red2, whole, -C2, red1, ALU.mult, ALU.add).then_inc(S["pr4"], 1)
        dve.wait_ge(S["pr4"], 1)
        V.scalar_tensor_tensor(red3, whole, -float(C3), red2, ALU.mult, ALU.add).then_inc(S["pr5"], 1)
        dve.wait_ge(S["pr5"], 1)
        V.tensor_scalar(red, red3, PI, -PI, ALU.min, ALU.max).then_inc(S["pr6"], 1)
        dve.wait_ge(S["pr6"], 1)
        V.scalar_tensor_tensor(mag, red, -1.0, red, ALU.mult, ALU.max).then_inc(S["pr7"], 1)
        dve.wait_ge(S["pr7"], 1)
        V.tensor_scalar(low, mag, -1.0, PI / 2, ALU.mult, ALU.add).then_inc(S["pr8"], 1)
        dve.wait_ge(S["sn1"], 1)
        dve.wait_ge(S["sn0"], 1)
        V.tensor_tensor(cosn, cosp, K("root"), ALU.mult)
        V.tensor_tensor(sinn, sinp, K("root"), ALU.mult).then_inc(S["pr0"], 1)
        dve.wait_ge(S["pr0"], 2)

        def body(i):
            for s in (0, 1):
                n = 2 * i + s
                dve.wait_ge(S["vt"], n + 1)
                V.tensor_tensor(tiles(vts[s], QT), tiles(ps[:, 4 * s + 3, :], QT), each(W("ho_bvc"), QT), ALU.add).then_inc(S["vts"], 1)
            for s in (0, 1):
                n = 2 * i + s
                dve.wait_ge(S["tk"], n + 1)
                V.scalar_tensor_tensor(uk[s], tk[s], K("turn_sign"), tk[s], ALU.mult, ALU.max).then_inc(S["uk"], 1)
                dve.wait_ge(S["tq"], n + 1)
                V.scalar_tensor_tensor(uq[s], tq[s], K("turn_sign"), tq[s], ALU.mult, ALU.max).then_inc(S["uq"], 1)
            for s in (0, 1):
                n = 2 * i + s
                dve.wait_ge(S["mr"], n + 1)
                for j in range(U):
                    m = V.tensor_tensor_scan(mrs[s][:, TOK * j:TOK * j + TOK], K("ones"), mr[s][:, TOK * j:TOK * j + TOK], 0.0, ALU.mult, ALU.add)
                m.then_inc(S["mrs"], 1)
                dve.wait_ge(S["mi"], n + 1)
                for j in range(U):
                    m = V.tensor_tensor_scan(mis[s][:, TOK * j:TOK * j + TOK], K("ones"), mi[s][:, TOK * j:TOK * j + TOK], 0.0, ALU.mult, ALU.add)
                m.then_inc(S["mis"], 1)
            for s in (0, 1):
                n = 2 * i + s
                dve.wait_ge(S["sa"], n + 1)
                V.tensor_tensor(tiles(sa[s], 2 * U), tiles(bank(s, 0, 2), 2 * U), each(K("causal"), 2 * U), ALU.mult).then_inc(S["sas"], 1)
                dve.wait_ge(S["sb"], n + 1)
                for img in range(2):
                    m = V.tensor_tensor(tiles(sc_[s][:, P * U * img:P * U * (img + 1)], U), tiles(ps[:, 4 * s + 2 + img, 0:U * P], U),
                                        each(K("causal")[:, 0:P], U), ALU.mult)
                m.then_inc(S["sbs"], 1)
            for s in (0, 1):
                n = 2 * i + s
                dve.wait_ge(S["mrs"], n + 1)
                V.tensor_tensor(tiles(rr[s], U), tiles(mrs[s], U), each(cosn, U), ALU.mult).then_inc(S["rr"], 1)
                dve.wait_ge(S["mis"], n + 1)
                V.tensor_tensor(tiles(ri[s], U), tiles(mis[s], U), each(sinn, U), ALU.mult).then_inc(S["ri"], 1)
                dve.wait_ge(S["gt"], n + 1)
                V.tensor_scalar(gg[s], gt[s], 0.5, 0.5, ALU.mult, ALU.add).then_inc(S["gg"], 1)
                dve.wait_ge(S["rr"], n + 1)
                dve.wait_ge(S["ri"], n + 1)
                V.tensor_tensor(pos[s], rr[s], ri[s], ALU.add).then_inc(S["pos"], 1)
            for s in (0, 1):
                n = 2 * i + s
                dve.wait_ge(S["ct"], n + 1)
                V.tensor_tensor(tiles(cts[s], U), tiles(ps[:, 4 * s, :], U), each(K("root32"), U), ALU.mult).then_inc(S["cts"], 1)
                dve.wait_ge(S["cts"], n + 1)
                dve.wait_ge(S["pos"], n + 1)
                V.tensor_tensor(df[s], pos[s], cts[s], ALU.subtract).then_inc(S["df"], 1)
                dve.wait_ge(S["df"], n + 1)
                dve.wait_ge(S["gg"], n + 1)
                V.tensor_tensor(gg[s], df[s], gg[s], ALU.mult).then_inc(S["dg"], 1)
                dve.wait_ge(S["dg"], n + 1)
                V.tensor_tensor(cb[s], gg[s], cts[s], ALU.add).then_inc(S["cb"], 1)
            for s in (0, 1):
                n1.scale(dve, 2 * i + s, s, df[s])
            for s in (0, 1):
                n = 2 * i + s
                dve.wait_ge(S["wos"], n + 1)
                V.scalar_tensor_tensor(o[s], hs[s], 2.0, wos[s], ALU.mult, ALU.add).then_inc(S["o"], 1)
            for s in (0, 1):
                n2.scale(dve, 2 * i + s, s, h(i, s))

        rounds(dve, body)


NE, FF = 16, 128
FAR = 3.0e38


def experts(nc, ctx, K, W, H, psum, w1_dram, w2_dram, out):
    S = Sems(nc, ctx, "mo", "win hs lgp lg m1 e1 p1 q1 b1 l2 m2 e2 p2 q2 b2 dd ex s1 w1 w2 g1 g2 g gtp gts xb ht acc hts"
             " hid rel y gm add sa ma xa sqa va ra na ga ba ha sz mz xz sqz vz rz o st0 st1")

    def sb(name, cols, dt=F32):
        t = ctx.enter_context(nc.sbuf_tensor("mo_" + name, [P, 2, cols], dt))
        return [t[:, s, :] for s in range(2)]

    w1 = ctx.enter_context(nc.sbuf_tensor("mo_wup", [P, NE * FF], F32))
    w2 = ctx.enter_context(nc.sbuf_tensor("mo_wdown", [FF, NE * C], F32))
    hs = sb("hs", UT)
    lg, e1, p1, b1, l2, e2, p2, b2, g1, g2, gate = (sb(n, NT * NE) for n in "lg e1 p1 b1 l2 e2 p2 b2 g1 g2 gate".split())
    m1, q1, m2, q2, dd, ex, s1, v1, v2 = (sb(n, NT) for n in "m1 q1 m2 q2 dd ex s1 v1 v2".split())
    gts = sb("gts", P)
    hid = sb("hid", 2 * UT)
    tmp = sb("tmp", UT)
    acc, hts = sb("acc", UT), sb("hts", UT)
    xc, sq, ya, yb = sb("xc", UT), sb("sq", UT), sb("ya", UT), sb("yb", UT)
    sm, mn, vs, rs = (sb(n, NT) for n in "sm mn vs rs".split())
    ps = psum

    def h(i, s):
        return H[:, bass.ds(i * (2 * UT) + s * UT, UT)]

    def tiles(v, n=NT):
        return v.rearrange("p (t k) -> p t k", t=n)

    def over(v, k):
        return v.unsqueeze(2).broadcast_to([P, v.shape[1], k])

    def each(v, n=NT):
        return v.unsqueeze(1).broadcast_to([P, n, v.shape[1]])

    out_v = out.rearrange("(u j m) (t p) c -> u p j t m c", j=U, m=2, p=P)
    block = ctx.enter_context(nc.Block())

    @block.sync
    def _(sp):
        sp.dma_start(w1[0:64, :].rearrange("h (e f) -> h e f", e=NE), w1_dram.rearrange("e h f -> h e f")).then_inc(S["win"], 16)
        sp.dma_start(w1[64:128, :].rearrange("h (e f) -> h e f", e=NE), w1_dram.rearrange("e h f -> h e f")).then_inc(S["win"], 16)
        sp.dma_start(w2[:, :].rearrange("f (e h) -> f e h", e=NE), w2_dram.rearrange("e f h -> f e h")).then_inc(S["win"], 16)

        def body(i):
            for s in (0, 1):
                sp.wait_ge(S["o"], 2 * i + s + 1)
                src = yb[s].rearrange("p (j t m c) -> p j t m c", j=U, t=2, m=2)
                for j in range(U):
                    for m in range(2):
                        sp.dma_start(out_v[bass.ds(2 * i + s, 1), :, j, :, m, :].rearrange("a p t c -> (a p) t c"), src[:, j, :, m, :])\
                          .then_inc(S[f"st{s}"], 16)

        rounds(sp, body)
        sp.wait_ge(S["st0"], 16 * 2 * U * (NU // 2))
        sp.wait_ge(S["st1"], 16 * 2 * U * (NU // 2))

    @block.tensor
    def _(pe):
        mm = nc.tensor.matmul
        pe.wait_ge(S["win"], 48)

        def body(i):
            for s in (0, 1):
                n = 2 * i + s
                pe.wait_ge(S["hs"], n + 1)
                for t in range(QT):
                    m = mm(ps[:, 4 * s, 32 * t:32 * t + 32], hs[s][:, P * t:P * t + P], W("mo_gate"), start=True, stop=True)
                m.then_inc(S["lgp"], 1)
                pe.wait_ge(S["gm"], past((n - 1) * NE))
                for t in range(QT):
                    m = nc.tensor.transpose(ps[:, 4 * s + 3, P * t:P * t + P], hs[s][:, P * t:P * t + P], K("ident"))
                m.then_inc(S["ht"], 1)
            for s in (0, 1):
                n = 2 * i + s
                pe.wait_ge(S["g"], n + 1)
                nc.tensor.transpose(ps[:, 4 * s + 1, 0:P], gate[s], K("ident")).then_inc(S["gtp"], 1)
            for s in (0, 1):
                n = 2 * i + s
                pe.wait_ge(S["gts"], n + 1)
                for t in range(QT):
                    o = ps[:, 4 * s + 2, P * t:P * t + P]
                    mm(o, hs[s][:, P * t:P * t + P], K("ident"), start=True, stop=False)
                    m = mm(o, gts[s], W("mo_b2")[:, P * t:P * t + P], start=False, stop=True)
                m.then_inc(S["xb"], 1)
            for s in (0, 1):
                n = 2 * i + s

                def up(e):
                    if e == 0:
                        pe.wait_ge(S["gtp"], n + 1)
                    else:
                        pe.wait_ge(S["rel"], n * 2 * NE + 2 * e)
                    for img in range(2):
                        lo = 64 * img
                        mm(ps[:, 4 * s + img, :], w1[lo:lo + 64, FF * e:FF * e + FF], hs[s][lo:lo + 64, :], start=True, stop=True).then_inc(S["hid"], 1)

                def down(e):
                    pe.wait_ge(S["rel"], n * 2 * NE + 2 * e + 2)
                    if e == 0:
                        pe.wait_ge(S["acc"], n + 1)
                    elif e == 1:
                        pe.wait_ge(S["hts"], n + 1)
                    else:
                        pe.wait_ge(S["gm"], n * NE + e - 1)
                    for t in range(QT):
                        for img in range(2):
                            k = 2 * t + img
                            m = mm(ps[:, 4 * s + 2 + e % 2, C * k:C * k + C], hid[e % 2][:, UT * img + P * t:UT * img + P * t + P],
                                   w2[:, C * e:C * e + C], start=True, stop=True)
                    m.then_inc(S["y"], 1)

                up(0)
                for e in range(NE):
                    if e + 1 < NE:
                        up(e + 1)
                    down(e)

        rounds(pe, body)

    @block.scalar
    def _(act):
        A = nc.scalar.activation

        def body(i):
            for s in (0, 1):
                n = 2 * i + s
                act.wait_ge(S["y"], past((n - 1) * NE))
                A(hs[s], h(i, s), ACT.Copy).then_inc(S["hs"], 1)
                act.wait_ge(S["ht"], n + 1)
                act.wait_ge(S["ha"], past(n - 1))
                A(hts[s], ps[:, 4 * s + 3, :], ACT.Copy).then_inc(S["hts"], 1)
            for s in (0, 1):
                n = 2 * i + s
                act.wait_ge(S["dd"], n + 1)
                A(ex[s], dd[s], ACT.Exp).then_inc(S["ex"], 1)
            for s in (0, 1):
                n = 2 * i + s
                act.wait_ge(S["gtp"], n + 1)
                A(gts[s], ps[:, 4 * s + 1, 0:P], ACT.Copy).then_inc(S["gts"], 1)
            for s in (0, 1):
                n = 2 * i + s
                act.wait_ge(S["xb"], n + 1)
                act.wait_ge(S["xa"], past(n - 1))
                A(acc[s], ps[:, 4 * s + 2, :], ACT.Copy).then_inc(S["acc"], 1)
            for s in (0, 1):
                n = 2 * i + s
                for e in range(NE):
                    for img in range(2):
                        act.wait_ge(S["hid"], n * 2 * NE + 2 * e + img + 1)
                        if e >= 2:
                            act.wait_ge(S["y"], n * NE + e - 1)
                        else:
                            act.wait_ge(S["y"], n * NE)
                        A(hid[e % 2][:, UT * img:UT * img + UT], ps[:, 4 * s + img, :], ACT.Relu, bias=W("mo_b1")[:, e:e + 1]).then_inc(S["rel"], 1)
            for s in (0, 1):
                n = 2 * i + s
                act.wait_ge(S["xa"], n + 1)
                A(sq[s], xc[s], ACT.Square).then_inc(S["sqa"], 1)
            for s in (0, 1):
                n = 2 * i + s
                act.wait_ge(S["va"], n + 1)
                A(rs[s], vs[s], ACT.Abs_reciprocal_sqrt, bias=K("eps"), scale=1.0 / C).then_inc(S["ra"], 1)
            for s in (0, 1):
                n = 2 * i + s
                act.wait_ge(S["xz"], n + 1)
                A(sq[s], xc[s], ACT.Square).then_inc(S["sqz"], 1)
            for s in (0, 1):
                n = 2 * i + s
                act.wait_ge(S["vz"], n + 1)
                A(rs[s], vs[s], ACT.Abs_reciprocal_sqrt, bias=K("eps"), scale=1.0 / C).then_inc(S["rz"], 1)

        rounds(act, body)

    @block.gpsimd
    def _(pool):
        G = nc.gpsimd

        def body(i):
            for s in (0, 1):
                n = 2 * i + s
                for e in range(NE):
                    pool.wait_ge(S["gm"], n * NE + e + 1)
                    pool.wait_ge(S["add"], n * NE + e)
                    if e == 0:
                        pool.wait_ge(S["acc"], n + 1)
                    G.tensor_tensor(acc[s], acc[s], tmp[e % 2], ALU.add).then_inc(S["add"], 1)
            for s in (0, 1):
                n = 2 * i + s
                pool.wait_ge(S["na"], n + 1)
                G.tensor_tensor(tiles(ya[s]), tiles(ya[s]), each(W("mo_gamma")), ALU.mult).then_inc(S["ga"], 1)
                pool.wait_ge(S["ga"], n + 1)
                G.tensor_tensor(tiles(ya[s]), tiles(ya[s]), each(W("mo_beta")), ALU.add).then_inc(S["ba"], 1)
                pool.wait_ge(S["ba"], n + 1)
                G.tensor_tensor(ya[s], ya[s], hts[s], ALU.add).then_inc(S["ha"], 1)

        rounds(pool, body)

    @block.vector
    def _(dve):
        V = nc.vector

        def body(i):
            def both(step):
                for s in (0, 1):
                    step(s, 2 * i + s)

            def best(src, mx, eq, pr, pm, oh, names, after):
                k_m, k_e, k_p, k_q, k_o = names

                def a(s, n):
                    dve.wait_ge(S[after], n + 1)
                    V.tensor_reduce(mx[s], tiles(src[s]), AX.X, ALU.max).then_inc(S[k_m], 1)

                def b(s, n):
                    dve.wait_ge(S[k_m], n + 1)
                    V.tensor_tensor(tiles(eq[s]), tiles(src[s]), over(mx[s], NE), ALU.is_equal).then_inc(S[k_e], 1)

                def c(s, n):
                    dve.wait_ge(S[k_e], n + 1)
                    V.tensor_tensor(tiles(pr[s]), tiles(eq[s]), each(K("priority")), ALU.mult).then_inc(S[k_p], 1)

                def d(s, n):
                    dve.wait_ge(S[k_p], n + 1)
                    V.tensor_reduce(pm[s], tiles(pr[s]), AX.X, ALU.max).then_inc(S[k_q], 1)

                def e(s, n):
                    dve.wait_ge(S[k_q], n + 1)
                    V.tensor_tensor(tiles(oh[s]), tiles(pr[s]), over(pm[s], NE), ALU.is_equal).then_inc(S[k_o], 1)

                for f in (a, b, c, d, e):
                    both(f)

            def logits(s, n):
                dve.wait_ge(S["lgp"], n + 1)
                V.tensor_tensor(tiles(lg[s]), tiles(ps[:, 4 * s, 0:P]), each(W("mo_gate_b")), ALU.add).then_inc(S["lg"], 1)

            both(logits)
            best(lg, m1, e1, p1, q1, b1, ("m1", "e1", "p1", "q1", "b1"), "lg")

            def rest(s, n):
                dve.wait_ge(S["b1"], n + 1)
                V.scalar_tensor_tensor(l2[s], b1[s], -FAR, lg[s], ALU.mult, ALU.add).then_inc(S["l2"], 1)

            both(rest)
            best(l2, m2, e2, p2, q2, b2, ("m2", "e2", "p2", "q2", "b2"), "l2")

            def step(name, after, emit):
                def f(s, n):
                    for a in after.split():
                        dve.wait_ge(S[a], n + 1)
                    emit(s).then_inc(S[name], 1)
                both(f)

            step("dd", "m2", lambda s: V.tensor_tensor(dd[s], m2[s], m1[s], ALU.subtract))
            step("s1", "ex", lambda s: V.tensor_scalar(s1[s], ex[s], 1.0, None, ALU.add))
            step("w1", "s1", lambda s: V.reciprocal(v1[s], s1[s]))
            step("w2", "w1", lambda s: V.tensor_tensor(v2[s], ex[s], v1[s], ALU.mult))
            step("g1", "b1", lambda s: V.tensor_tensor(tiles(g1[s]), tiles(b1[s]), over(v1[s], NE), ALU.mult))
            step("g2", "b2 w2", lambda s: V.tensor_tensor(tiles(g2[s]), tiles(b2[s]), over(v2[s], NE), ALU.mult))
            step("g", "g1 g2", lambda s: V.tensor_tensor(gate[s], g1[s], g2[s], ALU.add))

            for s in (0, 1):
                n = 2 * i + s
                for e in range(NE):
                    dve.wait_ge(S["y"], n * NE + e + 1)
                    if e >= 2:
                        dve.wait_ge(S["add"], n * NE + e - 1)
                    else:
                        dve.wait_ge(S["add"], n * NE)
                    g = tiles(gate[s])[:, :, e]
                    V.tensor_tensor(tiles(tmp[e % 2]), tiles(ps[:, 4 * s + 2 + e % 2, :]), over(g, C), ALU.mult).then_inc(S["gm"], 1)

            def norm(src, dst, src_ready, k):
                k_s, k_m, k_x, k_sq, k_v, k_r, k_o = k

                def a(s, n):
                    dve.wait_ge(S[src_ready], (n + 1) * (NE if src_ready == "add" else 1))
                    V.tensor_reduce(sm[s], tiles(src[s]), AX.X, ALU.add).then_inc(S[k_s], 1)

                def b(s, n):
                    dve.wait_ge(S[k_s], n + 1)
                    V.tensor_scalar(mn[s], sm[s], 1.0 / C, None, ALU.mult).then_inc(S[k_m], 1)

                def c(s, n):
                    dve.wait_ge(S[k_m], n + 1)
                    V.tensor_tensor(tiles(xc[s]), tiles(src[s]), over(mn[s], C), ALU.subtract).then_inc(S[k_x], 1)

                def d(s, n):
                    dve.wait_ge(S[k_sq], n + 1)
                    V.tensor_reduce(vs[s], tiles(sq[s]), AX.X, ALU.add).then_inc(S[k_v], 1)

                def e(s, n):
                    dve.wait_ge(S[k_r], n + 1)
                    if k_o == "o":
                        dve.wait_ge(S[f"st{s}"], i * (16 * 2 * U))
                    V.tensor_tensor(tiles(dst[s]), tiles(xc[s]), over(rs[s], C), ALU.mult).then_inc(S[k_o], 1)

                for f in (a, b, c, d, e):
                    both(f)

            norm(acc, ya, "add", ("sa", "ma", "xa", "sqa", "va", "ra", "na"))
            norm(ya, yb, "ha", ("sz", "mz", "xz", "sqz", "vz", "rz", "o"))

        rounds(dve, body)


class Phase(ExitStack):

    def __init__(self, nc):
        super().__init__()
        self.nc, self.held = nc, []

    def semaphore(self, name):
        self.held.append(self.nc.alloc_semaphore(name=name))
        return self.held[-1]

    def done(self):
        self.nc.clear_and_free_semaphores(self.held)
        self.nc.all_engine_barrier()


def program(nc, x, consts, wts, w1, w2, out, kat, wat, debug=None, debug_from=None, hin=None):
    with ExitStack() as ctx:
        def phase(build, *args):
            with Phase(nc) as p:
                build(nc, p, *args)
            p.done()

        kb = ctx.enter_context(nc.sbuf_tensor("consts_sb", [P, consts.shape[1]], F32))
        wb = ctx.enter_context(nc.sbuf_tensor("weights_sb", [P, wts.shape[1]], F32))
        H = ctx.enter_context(nc.sbuf_tensor("tokens", [P, NP * TOK], F32))
        loaded = ctx.enter_context(nc.semaphore("loaded"))
        stored = ctx.enter_context(nc.semaphore("stored"))

        def K(name):
            at, n, rows = kat[name]
            return kb[0:rows, at:at + n]

        def W(name):
            at, n, rows = wat[name]
            return wb[0:rows, at:at + n]

        with nc.Block() as block:
            @block.sync
            def _(sp):
                sp.dma_start(kb[:, :], consts).then_inc(loaded, 16)
                sp.dma_start(wb[:, :], wts).then_inc(loaded, 16)
                sp.wait_ge(loaded, 32)

        psum = ctx.enter_context(nc.psum_tensor("psum", [P, 8, CH], F32))
        if debug in (None, "tok") or debug_from is None:
            phase(tokenizer, x.rearrange("(n two) c h w -> n (two c) (h w)", two=2), K, W, H, psum)
        if debug_from is not None:
            with nc.Block() as block:
                @block.sync
                def _(sp):
                    sp.dma_start(H[:, :], hin).then_inc(stored, 16)
                    sp.wait_ge(stored, 16)
        todo = {"attn": attention, "ffn": routed_ffn, "holo": holographic}
        for name, build in todo.items():
            if debug is None or (list(todo).index(name) <= (list(todo).index(debug) if debug in todo else -1)
                                 and (debug_from is None or name == debug)):
                phase(build, K, W, H, psum)
        if debug in (None, "moe"):
            phase(experts, K, W, H, psum, w1, w2, out)
        elif debug:
            with nc.Block() as block:
                @block.sync
                def _(sp):
                    sp.dma_start(out.rearrange("b t c -> (b t c)").rearrange("(p n) -> p n", p=P), H[:, :]).then_inc(stored, 16)
                    sp.wait_ge(stored, 32 if debug_from is not None else 16)


def kernel(debug=None, hstart=None, **inputs):
    import concourse.bacc as bacc
    from concourse.bass_utils import run_bass_kernel_spmd as run

    nc = bacc.Bacc("TRN2", target_bir_lowering=False, num_devices=1)
    k, w = shape_constants(), weights(inputs)
    k.add("eps", np.full((P, 1), EPS))
    arrays = {"x": np.ascontiguousarray(inputs["x"]), "consts": k.array(), "weights_in": w.array(),
              "experts_up": np.ascontiguousarray(inputs["L1_ffn_w1"]), "experts_down": np.ascontiguousarray(inputs["L1_ffn_w2"])}
    aps = [nc.dram_tensor(n, a.shape, F32, kind="ExternalInput").ap() for n, a in arrays.items()]
    out = nc.dram_tensor("out", (B, TOK, C), F32, kind="ExternalOutput").ap()
    hin = None
    if hstart is not None:
        arrays["hin"] = hstart
        hin = nc.dram_tensor("hin", hstart.shape, F32, kind="ExternalInput").ap()
    program(nc, *aps, out, k.at, w.at, debug, None if hstart is None else 1, hin)
    r = run(nc, [arrays], core_ids=[0])
    return r.results[0]["out"]
```

```python
from contextlib import ExitStack

import numpy as np
import concourse.bass as bass
from concourse import mybir

F32 = mybir.dt.float32
BF16 = mybir.dt.bfloat16
ALU = mybir.AluOpType
ACT = mybir.ActivationFunctionType
AX = mybir.AxisListType

B, C, IMG = 64, 64, 64
STRIDE, HEADS = 4, 8
HD = C // HEADS
SIDE = IMG // STRIDE
TOK = SIDE * SIDE
PX = STRIDE * STRIDE
PIX = IMG * IMG
P = 128
NP = B // 2
CH = 512
NCH = PIX // CH
CP = CH // PX
EPS = 1e-5


class Pack:

    def __init__(self):
        self.parts, self.at, self.n = [], {}, 0

    def add(self, name, a):
        a = np.asarray(a, np.float32)
        full = np.zeros((P, a.shape[1]), np.float32)
        full[: a.shape[0]] = a
        self.at[name] = (self.n, a.shape[1], a.shape[0])
        self.parts.append(full)
        self.n += a.shape[1]

    def array(self):
        return np.ascontiguousarray(np.concatenate(self.parts, axis=1))


def twice(m):
    m = np.asarray(m, np.float32)
    out = np.zeros((2 * m.shape[0], 2 * m.shape[1]), np.float32)
    out[: m.shape[0], : m.shape[1]] = m
    out[m.shape[0]:, m.shape[1]:] = m
    return out


def column(v):
    v = np.asarray(v, np.float32).reshape(-1, 1)
    return np.concatenate([v, v], axis=0)


def shape_constants():
    k = Pack()
    eye = np.eye(P, dtype=np.float32)
    k.add("ident", eye)
    k.add("centre", twice(np.eye(C) - 1.0 / C))
    k.add("mean", twice(np.full((C, C), 1.0 / C)))
    var_sel = np.zeros((P, 2, 32), np.float32)
    head_sel = np.zeros((P, 2, 32), np.float32)
    spread = np.zeros((P, NCH, P), np.float32)
    for a in range(2):
        for img in range(2):
            for h in range(HEADS):
                row = 16 * a + 8 * img + h
                lo = 64 * img + HD * h
                var_sel[64 * img:64 * img + 64, a, row] = 1.0 / C
                head_sel[lo:lo + HD, a, row] = 1.0
                for g in range(4):
                    spread[32 * g + row, 4 * a + g, lo:lo + HD] = 1.0
    k.add("var_sel", var_sel.reshape(P, -1))
    k.add("head_sel", head_sel.reshape(P, -1))
    part, col = np.arange(P)[:, None], np.arange(TOK)[None]
    k.add("earlier", np.concatenate([col < part, col < part + P], axis=1))
    k.add("priority", np.broadcast_to(16.0 - np.arange(16)[None], (P, 16)))
    k.add("causal", part <= col)
    k.add("ones", np.ones((P, TOK)))
    k.add("root", np.broadcast_to(1 / np.sqrt(col + 1.0), (P, TOK)))
    k.add("root32", np.broadcast_to(1 / np.sqrt((col + 1.0) * 32), (P, TOK)))
    cosine = (np.arange(P)[:, None] // 32) % 2 == 0
    k.add("turn_sign", np.where(cosine, -1.0, 1.0))
    k.add("turn_scale", np.where(cosine, -PI, PI))
    k.add("turn_bias", np.where(cosine, PI / 2, 0.0))
    k.add("spread", spread.reshape(P, -1))
    return k


def gate_rows():
    sel = np.zeros((PARTS, 2, NE, NE, 2, C), np.float32)
    for e in range(NE):
        for img in range(2):
            sel[:, img, e, e, img] = 1.0
    return sel.reshape(PARTS * 2 * NE, NE * P)


def weights(x):
    w = Pack()
    wkv = np.asarray(x["L0_tok_Wkv"])
    w.add("tok_wq", twice(np.asarray(x["L0_tok_Wq"]).T))
    w.add("tok_wk", twice(wkv[:C].T))
    w.add("tok_wv", twice(wkv[C:].T))
    w.add("tok_wp", twice(np.asarray(x["L0_tok_proj_w"]).T))
    w.add("at_wq", twice(np.asarray(x["L0_attn_W_q"]).T))
    kv = [twice(np.asarray(x[n]).T) for n in ("L0_attn_W_k", "L0_attn_W_v")]
    w.add("at_wkv", np.concatenate(kv, axis=1))
    w.add("at_wo", twice(np.asarray(x["L0_attn_W_o"]).T))
    w.add("at_e", np.asarray(x["L0_attn_E_block"]).T)
    w.add("at_f", np.asarray(x["L0_attn_F_block"]).T)
    for name in ("L0_attn_g1", "L0_attn_b1", "L0_attn_g2", "L0_attn_b2"):
        w.add(name, column(x[name]))
    w.add("ff_wr", np.tile(np.broadcast_to(np.asarray(x["L0_ffn_wr"]), (C, P)), (2, 1)))
    w.add("L0_ffn_br", np.broadcast_to(np.asarray(x["L0_ffn_br"]).reshape(1, 1), (P, 1)))
    w.add("ff_w1", np.tile(np.asarray(x["L0_ffn_w1"]), (2, 1)))
    w.add("ff_b1", np.asarray(x["L0_ffn_b1"]).reshape(2, P).T)
    w.add("ff_w2", np.concatenate(np.split(np.asarray(x["L0_ffn_w2"]), 2), axis=1))
    w.add("ff_b2", column(x["L0_ffn_b2"]))

    def features(m):
        m = np.asarray(m)
        return np.concatenate([m, m], axis=1)

    for n in ("k", "q"):
        w.add(f"ho_w{n}1", twice(x[f"L1_attn_W{n}1"]))
        w.add(f"ho_w{n}2", twice(features(x[f"L1_attn_W{n}2"])))
        w.add(f"ho_b{n}2", column(features(np.asarray(x[f"L1_attn_b{n}2"])[None])))
        w.add(f"L1_attn_b{n}1", column(x[f"L1_attn_b{n}1"]))
    w.add("ho_wvp", twice(x["L1_attn_Wvp"]))
    w.add("ho_wvc", twice(x["L1_attn_Wvc"]))
    w.add("ho_bvc", np.broadcast_to(column(x["L1_attn_bvc"]).T, (P, P)))
    w.add("ho_wg1", twice(x["L1_attn_Wg1"]))
    w.add("ho_bg1", column(x["L1_attn_bg1"]))
    for k, n in enumerate("ab"):
        w.add(f"ho_wg2{n}", twice(np.broadcast_to(np.asarray(x["L1_attn_Wg2"])[:, k:k + 1], (C // 4, C))))
        w.add(f"ho_bg2{n}", np.broadcast_to(np.asarray(x["L1_attn_bg2"])[k:k + 1].reshape(1, 1), (P, 1)))
    w.add("ho_phases", np.tile(np.asarray(x["L1_attn_base_phases"])[:TOK].T, (2, 1)))
    w.add("mo_gate", twice(x["L1_ffn_gate_w"]))
    w.add("mo_gate_b", np.broadcast_to(np.asarray(x["L1_ffn_gate_b"])[None], (P, 16)))
    w.add("mo_b1", np.asarray(x["L1_ffn_b1"]).T)
    w.add("mo_b2", np.tile(twice(x["L1_ffn_b2"]), (3, 1)))
    w.add("mo_gamma", np.broadcast_to(np.asarray(x["L1_ffn_gamma"])[None], (P, C)))
    w.add("mo_beta", np.broadcast_to(np.asarray(x["L1_ffn_beta"])[None], (P, C)))
    w.add("ho_wo", twice(x["L1_attn_Wo"]))
    for name in ("L1_attn_bvp", "L1_attn_ln_g", "L1_attn_ln_b", "L1_attn_bo"):
        w.add(name, column(x[name]))
    w.add("L0_attn_scale", np.broadcast_to(np.asarray(x["L0_attn_scale"]).reshape(1, 1), (P, 1)))
    for name in ("L0_tok_ln_q_w", "L0_tok_ln_q_b", "L0_tok_ln_kv_w", "L0_tok_ln_kv_b", "L0_tok_proj_b"):
        w.add(name, column(x[name]))
    return w


class Sems:

    def __init__(self, nc, ctx, phase, names):
        self.s = {n: ctx.semaphore(f"{phase}_{n}") for n in names.split()}

    def __getitem__(self, n):
        return self.s[n]


def past(count):
    return max(count, 0) if isinstance(count, int) else count


def tokenizer(nc, ctx, x, K, W, H, psum):
    NX = 4

    def sb(name, cols, dt=F32):
        return ctx.enter_context(nc.sbuf_tensor(name, [P, cols], dt))

    def sem(name):
        return ctx.semaphore("tok_" + name)

    xt = sb("tok_x", NX * PIX)
    sq = sb("tok_sq", NCH * CH)
    kq = sb("tok_kq", NCH * CH)
    half = sb("tok_half", PIX // 2)
    quarter = sb("tok_quarter", PIX // 4)
    eighth = half[:, 0:PIX // 8]
    pooled = sb("tok_pooled", 2 * TOK)
    base = sb("tok_base", 2 * TOK)
    qsq = sb("tok_qsq", TOK)
    qr = sb("tok_qr", TOK)
    qn = sb("tok_qn", TOK)
    qa = sb("tok_qa", TOK)
    qs = sb("tok_qs", 2 * TOK)
    rstd = sb("tok_rstd", 2 * CH)
    score = sb("tok_score", CH)
    shifted = sb("tok_shifted", CH)
    top = sb("tok_top", CP)
    expd = sb("tok_exp", CH)
    den = sb("tok_den", CP)
    rden = sb("tok_rden", CP)
    er = sb("tok_er", CH)
    attn = sb("tok_attn", CH)
    wide = sb("tok_wide", 4 * CH)
    zp = sb("tok_zp", 2 * CH)
    z = sb("tok_z", TOK)
    wkc = sb("tok_wkc", P)
    wvc = sb("tok_wvc", P)
    wks, wvs = kq[:, 0:P], kq[:, P:2 * P]
    small = sb("tok_small", 4)
    lnq16, bv, pbz = small[:, 0:1], small[:, 1:2], small[:, 2:3]

    ps = psum
    VAR, SCORE = 4, 5

    x_in = [sem(f"x_in{s}") for s in range(NX)]
    names = ("prep_dve prep_pe prep_act prep2_pe prep2_act half quarter eighth pooled cx sq var rstd qc qsq qv qr qn qa qq qs base "
             "kx kq scored s1 top shifted exp den rden er attn wide_mm wide vx zmul zred pj tok")
    S = Sems(nc, ctx, "tok", names)

    def mm(out, lhsT, rhs, start=True, stop=True, **kw):
        return nc.tensor.matmul(out, lhsT, rhs, start=start, stop=stop, **kw)

    def pixel_mm(out, lhsT, slot, c):
        n = STRIDE * IMG
        for k in range(CH // n):
            at = slot * PIX + c * CH + k * n
            v = xt[:, at:at + n].rearrange("p (i w j) -> p w i j", i=STRIDE, w=SIDE, j=STRIDE)
            last = mm(out[:, k * n:(k + 1) * n], lhsT, v)
        return last

    def patches(v):
        return v.rearrange("p (a b) -> p a b", b=PX)

    def over_pixels(v, n):
        return v.unsqueeze(2).broadcast_to([P, n, PX])

    block = ctx.enter_context(nc.Block())

    @block.sync
    def _(sp):
        for s in range(NX):
            sp.dma_start(xt[:, s * PIX:(s + 1) * PIX], x[s]).then_inc(x_in[s], 16)
        with sp.Fori(0, NP // NX - 1) as i:
            for s in range(NX):
                sp.wait_ge(S["vx"], i * (NX * NCH) + NCH * (s + 1))
                sp.dma_start(xt[:, s * PIX:(s + 1) * PIX], x[i * NX + (NX + s)]).then_inc(x_in[s], 16)

    @block.gpsimd
    def _(pool):
        def pool_pair(n, s, x_loads):
            pool.wait_ge(x_in[s], x_loads)
            pool.wait_ge(S["base"], past(n - 1))
            pool.wait_ge(S["qc"], past(n - 1))
            pool.wait_ge(S["pooled"], n)
            v = xt[:, s * PIX:(s + 1) * PIX].rearrange("p (h i w) -> p h i w", i=STRIDE, w=IMG)
            h = half[:, :].rearrange("p (h i w) -> p h i w", i=2, w=IMG)
            nc.gpsimd.tensor_tensor(h, v[:, :, 0:2], v[:, :, 2:4], ALU.add).then_inc(S["half"], 1)
            pool.wait_ge(S["half"], n + 1)
            q = quarter[:, :].rearrange("p (h w) -> p h w", w=IMG)
            nc.gpsimd.tensor_tensor(q, h[:, :, 0], h[:, :, 1], ALU.add).then_inc(S["quarter"], 1)
            pool.wait_ge(S["quarter"], n + 1)
            q = quarter[:, :].rearrange("p (t j) -> p t j", j=4)
            e = eighth[:, :].rearrange("p (t j) -> p t j", j=2)
            nc.gpsimd.tensor_tensor(e, q[:, :, 0:2], q[:, :, 2:4], ALU.add).then_inc(S["eighth"], 1)
            pool.wait_ge(S["eighth"], n + 1)
            o = pooled[:, (s % 2) * TOK:(s % 2 + 1) * TOK]
            nc.gpsimd.tensor_tensor(o, e[:, :, 0], e[:, :, 1], ALU.add).then_inc(S["pooled"], 1)

        for s in range(2):
            pool_pair(s, s, 16)

        def step(i, s, last):
            n = i * NX + s
            pool.wait_ge(S["exp"], n + 1)
            pool.wait_ge(S["rstd"], n + 1)
            pool.wait_ge(S["attn"], n)
            nc.gpsimd.tensor_tensor(er[:, :], expd[:, :], rstd[:, (s % 2) * CH:(s % 2 + 1) * CH], ALU.mult).then_inc(S["er"], 1)
            pool.wait_ge(S["er"], n + 1)
            pool.wait_ge(S["rden"], n + 1)
            pool.wait_ge(S["wide_mm"], n * NCH)
            nc.gpsimd.tensor_tensor(patches(attn[:, :]), patches(er[:, :]), over_pixels(rden[:, :], CP), ALU.mult).then_inc(S["attn"], 1)
            if not (last and s >= NX - 2):
                t = (s + 2) % NX
                pool_pair(n + 2, t, 16 * i + 16 * ((s + 2) // NX + 1))

        for s in range(NX):
            step(0, s, False)
        with pool.Fori(1, NP // NX - 1) as i:
            for s in range(NX):
                step(i, s, False)
        for s in range(NX):
            step(NP // NX - 1, s, True)

    @block.tensor
    def _(pe):
        pe.wait_ge(S["prep_dve"], 3)
        mm(ps[:, 0, 0:P], K("centre"), wks[:, :])
        mm(ps[:, 0, P:2 * P], K("centre"), wvs[:, :])
        mm(ps[:, 1, 0:1], W("tok_wv"), W("L0_tok_ln_kv_b")).then_inc(S["prep_pe"], 1)
        pe.wait_ge(S["prep_act"], 3)
        mm(ps[:, 1, 1:2], W("tok_wp"), bv).then_inc(S["prep2_pe"], 1)
        pe.wait_ge(S["prep2_act"], 1)

        def stage_a(n, s, x_loads, first=False):
            def var_mm(c0):
                pe.wait_ge(S["sq"], n * NCH + c0 + 4)
                if c0 == 0:
                    pe.wait_ge(S["rstd"], n)
                for c in range(c0, c0 + 4):
                    g = c % 4
                    m = mm(ps[32 * g:32 * g + 32, VAR, :], K("var_sel")[:, 32 * (c // 4):32 * (c // 4) + 32], sq[:, c * CH:(c + 1) * CH],
                           start=(c < 4), stop=(c >= 4))
                if c0:
                    m.then_inc(S["var"], 1)

            pe.wait_ge(x_in[s], x_loads)
            for c in range(NCH):
                if c == 0:
                    pe.wait_ge(S["qs"], n)
                elif c == 1 and not first:
                    pe.wait_ge(S["tok"], past(n - 1))
                elif c >= 2:
                    pe.wait_ge(S["sq"], n * NCH + c - 1)
                pixel_mm(ps[:, c % 2, :], K("centre"), s, c).then_inc(S["cx"], 1)
                if c == 5:
                    var_mm(0)
            pe.wait_ge(S["pooled"], n + 1)
            pe.wait_ge(S["sq"], n * NCH + 7)
            mm(ps[:, 0, 0:TOK], K("centre"), pooled[:, (s % 2) * TOK:(s % 2 + 1) * TOK]).then_inc(S["qc"], 1)
            var_mm(4)
            pe.wait_ge(S["qsq"], n + 1)
            mm(ps[:, 1, 0:TOK], K("mean"), qsq[:, :]).then_inc(S["qv"], 1)
            pe.wait_ge(S["qa"], n + 1)
            mm(ps[:, 0, 0:TOK], W("tok_wq"), qa[:, :]).then_inc(S["qq"], 1)

        def stage_b(n, s):
            def score_mm(c0):
                pe.wait_ge(S["kq"], n * NCH + c0 + 4)
                if c0 == 0:
                    pe.wait_ge(S["s1"], n)
                for c in range(c0, c0 + 4):
                    g = c % 4
                    m = mm(ps[32 * g:32 * g + 32, SCORE, :], K("head_sel")[:, 32 * (c // 4):32 * (c // 4) + 32], kq[:, c * CH:(c + 1) * CH],
                           start=(c < 4), stop=(c >= 4))
                if c0:
                    m.then_inc(S["scored"], 1)

            for c in range(NCH):
                pe.wait_ge(S["zmul"], n * NCH) if c < 2 else pe.wait_ge(S["kq"], n * NCH + c - 1)
                pixel_mm(ps[:, 2 + c % 2, :], wkc[:, :], s, c).then_inc(S["kx"], 1)
                if c == 5:
                    score_mm(0)
            score_mm(4)

        def stage_c(n, s, last):
            pe.wait_ge(S["attn"], n + 1)
            for c in range(NCH):
                pe.wait_ge(S["wide"], n * NCH + max(c - 1, 0))
                mm(ps[:, 6 + c % 2, :], K("spread")[:, c * P:(c + 1) * P], attn[:, :]).then_inc(S["wide_mm"], 1)
                if c >= 2:
                    pe.wait_ge(S["zmul"], n * NCH + c - 1)
                pixel_mm(ps[:, 2 + c % 2, :], wvc[:, :], s, c).then_inc(S["vx"], 1)
            pe.wait_ge(S["zred"], n * NCH + NCH)
            pe.wait_ge(S["qr"], n + (1 if last else 2))
            mm(ps[:, 1, 0:TOK], W("tok_wp"), z[:, :]).then_inc(S["pj"], 1)

        stage_a(0, 0, 16, first=True)

        def step(i, s, last):
            n = i * NX + s
            stage_b(n, s)
            end = last and s == NX - 1
            if not end:
                stage_a(n + 1, (s + 1) % NX, i * 16 + 16 * ((s + 1) // NX + 1))
            stage_c(n, s, end)

        for s in range(NX):
            step(0, s, False)
        with pe.Fori(1, NP // NX - 1) as i:
            for s in range(NX):
                step(i, s, False)
        for s in range(NX):
            step(NP // NX - 1, s, True)

    @block.scalar
    def _(act):
        A = nc.scalar.activation
        act.wait_ge(S["prep_pe"], 1)
        A(wkc[:, :], ps[:, 0, 0:P], ACT.Copy).then_inc(S["prep_act"], 1)
        A(wvc[:, :], ps[:, 0, P:2 * P], ACT.Copy).then_inc(S["prep_act"], 1)
        A(bv, ps[:, 1, 0:1], ACT.Copy).then_inc(S["prep_act"], 1)
        act.wait_ge(S["prep2_pe"], 1)
        A(pbz, ps[:, 1, 1:2], ACT.Identity, bias=W("L0_tok_proj_b")).then_inc(S["prep2_act"], 1)
        act.wait_ge(S["prep2_act"], 1)

        def stage_a(n, s, exp=None):
            def square(c):
                act.wait_ge(S["cx"], n * NCH + c + 1)
                if c == 0:
                    act.wait_ge(S["var"], n)
                A(sq[:, c * CH:(c + 1) * CH], ps[:, c % 2, :], ACT.Square).then_inc(S["sq"], 1)

            for c in range(4):
                square(c)
            if exp is not None:
                exp()
            for c in range(4, NCH):
                square(c)
            act.wait_ge(S["qc"], n + 1)
            act.wait_ge(S["qv"], n)
            A(qsq[:, :], ps[:, 0, 0:TOK], ACT.Square, scale=1.0 / PX).then_inc(S["qsq"], 1)
            act.wait_ge(S["var"], n + 1)
            if exp is not None:
                act.wait_ge(S["er"], past(n - 1))
                act.wait_ge(S["s1"], past(n - 1))
            A(rstd[:, (s % 2) * CH:(s % 2 + 1) * CH], ps[:, VAR, :], ACT.Abs_reciprocal_sqrt, bias=K("eps")).then_inc(S["rstd"], 1)
            act.wait_ge(S["qv"], n + 1)
            act.wait_ge(S["qn"], n)
            A(qr[:, :], ps[:, 1, 0:TOK], ACT.Abs_reciprocal_sqrt, bias=K("eps")).then_inc(S["qr"], 1)
            act.wait_ge(S["qn"], n + 1)
            act.wait_ge(S["qq"], n)
            A(qa[:, :], qn[:, :], ACT.Identity, bias=W("L0_tok_ln_q_b"), scale=lnq16).then_inc(S["qa"], 1)
            if exp is not None:
                act.wait_ge(S["tok"], past(n - 1))
            A(base[:, (s % 2) * TOK:(s % 2 + 1) * TOK], pooled[:, (s % 2) * TOK:(s % 2 + 1) * TOK], ACT.Identity,
              bias=pbz, scale=1.0 / PX).then_inc(S["base"], 1)
            act.wait_ge(S["qq"], n + 1)
            if exp is not None:
                act.wait_ge(S["kq"], past((n - 1) * NCH))
            A(qs[:, (s % 2) * TOK:(s % 2 + 1) * TOK], ps[:, 0, 0:TOK], ACT.Copy, scale=float(C) ** -0.5).then_inc(S["qs"], 1)

        def exp_pair(n):
            act.wait_ge(S["shifted"], n + 1)
            act.wait_ge(S["er"], n)
            act.wait_ge(S["den"], n)
            A(expd[:, :], shifted[:, :], ACT.Exp).then_inc(S["exp"], 1)

        act.wait_ge(S["prep_dve"], 3)
        stage_a(0, 0)

        def step(i, s, last):
            n = i * NX + s
            if last and s == NX - 1:
                exp_pair(n)
            else:
                stage_a(n + 1, (s + 1) % NX, lambda: exp_pair(n))
            for c in range(NCH):
                act.wait_ge(S["wide_mm"], n * NCH + c + 1)
                act.wait_ge(S["zmul"], n * NCH + max(c - 3, 0))
                A(wide[:, (c % 4) * CH:(c % 4 + 1) * CH], ps[:, 6 + c % 2, :], ACT.Copy).then_inc(S["wide"], 1)

        for s in range(NX):
            step(0, s, False)
        with act.Fori(1, NP // NX - 1) as i:
            for s in range(NX):
                step(i, s, False)
        for s in range(NX):
            step(NP // NX - 1, s, True)

    @block.vector
    def _(dve):
        V = nc.vector
        V.tensor_scalar(wks[:, :], W("tok_wk"), W("L0_tok_ln_kv_w"), None, ALU.mult).then_inc(S["prep_dve"], 1)
        V.tensor_scalar(wvs[:, :], W("tok_wv"), W("L0_tok_ln_kv_w"), None, ALU.mult).then_inc(S["prep_dve"], 1)
        V.tensor_scalar(lnq16, W("L0_tok_ln_q_w"), 1.0 / PX, None, ALU.mult).then_inc(S["prep_dve"], 1)

        def query_norm(n):
            dve.wait_ge(S["qr"], n + 1)
            dve.wait_ge(S["qa"], n)
            V.tensor_tensor(qn[:, :], ps[:, 0, 0:TOK], qr[:, :], ALU.mult).then_inc(S["qn"], 1)

        query_norm(0)

        def step(i, s, last):
            n = i * NX + s
            q = qs[:, (s % 2) * TOK:(s % 2 + 1) * TOK]
            dve.wait_ge(S["qs"], n + 1)
            dve.wait_ge(S["scored"], n)
            for c in range(NCH):
                dve.wait_ge(S["kx"], n * NCH + c + 1)
                V.tensor_tensor(patches(kq[:, c * CH:(c + 1) * CH]), patches(ps[:, 2 + c % 2, :]),
                                over_pixels(q[:, c * CP:(c + 1) * CP], CP), ALU.mult).then_inc(S["kq"], 1)
            dve.wait_ge(S["scored"], n + 1)
            dve.wait_ge(S["rstd"], n + 1)
            dve.wait_ge(S["shifted"], n)
            V.tensor_tensor(score[:, :], ps[:, SCORE, :], rstd[:, (s % 2) * CH:(s % 2 + 1) * CH], ALU.mult).then_inc(S["s1"], 1)
            dve.wait_ge(S["s1"], n + 1)
            V.tensor_reduce(top[:, :], patches(score[:, :]), AX.X, ALU.max).then_inc(S["top"], 1)
            dve.wait_ge(S["top"], n + 1)
            dve.wait_ge(S["exp"], n)
            V.tensor_tensor(patches(shifted[:, :]), patches(score[:, :]), over_pixels(top[:, :], CP), ALU.subtract).then_inc(S["shifted"], 1)
            dve.wait_ge(S["exp"], n + 1)
            dve.wait_ge(S["rden"], n)
            V.tensor_reduce(den[:, :], patches(expd[:, :]), AX.X, ALU.add).then_inc(S["den"], 1)
            dve.wait_ge(S["den"], n + 1)
            dve.wait_ge(S["attn"], n)
            V.reciprocal(rden[:, :], den[:, :]).then_inc(S["rden"], 1)
            if not (last and s == NX - 1):
                query_norm(n + 1)

            def reduce(c):
                dve.wait_ge(S["zmul"], n * NCH + c + 1)
                if c == 0:
                    dve.wait_ge(S["pj"], n)
                V.tensor_reduce(z[:, c * CP:(c + 1) * CP], patches(zp[:, (c % 2) * CH:(c % 2 + 1) * CH]), AX.X, ALU.add).then_inc(S["zred"], 1)

            for c in range(NCH):
                dve.wait_ge(S["vx"], n * NCH + c + 1)
                dve.wait_ge(S["wide"], n * NCH + c + 1)
                dve.wait_ge(S["zred"], n * NCH + max(c - 1, 0))
                V.tensor_tensor(zp[:, (c % 2) * CH:(c % 2 + 1) * CH], ps[:, 2 + c % 2, :],
                                wide[:, (c % 4) * CH:(c % 4 + 1) * CH], ALU.mult).then_inc(S["zmul"], 1)
                if c:
                    reduce(c - 1)
            reduce(NCH - 1)
            dve.wait_ge(S["pj"], n + 1)
            dve.wait_ge(S["base"], n + 1)
            o = H[:, bass.ds(i * (NX * TOK) + s * TOK, TOK)]
            V.tensor_tensor(o, ps[:, 1, 0:TOK], base[:, (s % 2) * TOK:(s % 2 + 1) * TOK], ALU.add).then_inc(S["tok"], 1)

        for s in range(NX):
            step(0, s, False)
        with dve.Fori(1, NP // NX - 1) as i:
            for s in range(NX):
                step(i, s, False)
        for s in range(NX):
            step(NP // NX - 1, s, True)


U = 2
UT = U * TOK
NU = NP // U
QT = UT // P
NT = 2 * QT


def rounds(eng, body):
    body(0)
    with eng.Fori(1, NU // 2) as i:
        body(i)


class Norm:
    PARTS = "c sq v r x"

    def __init__(self, nc, S, K, name, ps, mean_bank, var_bank, sq, r):
        self.nc, self.S, self.K, self.name, self.ps = nc, S, K, name, ps
        self.mb, self.vb, self.sq, self.r = mean_bank, var_bank, sq, r

    @staticmethod
    def names(*norms):
        return " ".join(f"{n}_{p}" for n in norms for p in Norm.PARTS.split())

    def centre(self, src, s):
        self.nc.tensor.matmul(self.ps[:, 4 * s + self.mb, :], self.K("centre"), src, start=True, stop=True)\
            .then_inc(self.S[self.name + "_c"], 1)

    def square(self, act, n, s):
        act.wait_ge(self.S[self.name + "_c"], n + 1)
        self.nc.scalar.activation(self.sq[s], self.ps[:, 4 * s + self.mb, :], ACT.Square).then_inc(self.S[self.name + "_sq"], 1)

    def variance(self, pe, n, s):
        pe.wait_ge(self.S[self.name + "_sq"], n + 1)
        self.nc.tensor.matmul(self.ps[:, 4 * s + self.vb, :], self.K("mean"), self.sq[s], start=True, stop=True)\
            .then_inc(self.S[self.name + "_v"], 1)

    def rstd(self, act, n, s):
        act.wait_ge(self.S[self.name + "_v"], n + 1)
        self.nc.scalar.activation(self.r[s], self.ps[:, 4 * s + self.vb, :], ACT.Abs_reciprocal_sqrt, bias=self.K("eps"))\
            .then_inc(self.S[self.name + "_r"], 1)

    def scale(self, dve, n, s, out):
        dve.wait_ge(self.S[self.name + "_r"], n + 1)
        self.nc.vector.tensor_tensor(out, self.ps[:, 4 * s + self.mb, :], self.r[s], ALU.mult).then_inc(self.S[self.name + "_x"], 1)


def attention(nc, ctx, K, W, H, psum):
    NB = TOK // 128
    BK = 64
    S = Sems(nc, ctx, "at", "sp0 sp1 sp2 sp3 sp4 sp5 sp6 "
             + Norm.names("n1", "n2", "n3") +
             " tn q kv qsq qv qm qr qn ksq kss ksm kr kn v kpvp kpt vp sc mx sh ex den rden w wt wts ao aos wo o1 o2 o3")

    def sb(name, cols):
        t = ctx.enter_context(nc.sbuf_tensor("at_" + name, [P, 2, cols], F32))
        return [t[:, s, :] for s in range(2)]

    sq, r, xn, tn = sb("sq", UT), sb("r", UT), sb("xn", UT), sb("tn", UT)
    qm, qr, qn = sb("qm", UT), sb("qr", UT), sb("qn", UT)
    ksq, kn, v = sb("ksq", UT), sb("kn", UT), sb("v", UT)
    kss, ksm, kr = sb("kss", NT), sb("ksm", NT), sb("kr", NT)
    kpt, vp = sb("kpt", U * P), sb("vp", U * P)
    sh, ex, wts = sb("sh", NT * P), sb("ex", NT * P), sb("wts", NT * P)
    mx, den, rden = sb("mx", NT), sb("den", NT), sb("rden", NT)
    ao, o1, o2, o3 = sb("ao", UT), sb("o1", UT), sb("o2", UT), sb("o3", UT)
    sp_ = ctx.enter_context(nc.sbuf_tensor("at_softplus", [P, 8], F32))
    neg, low, el, onep, ln1, pos, sc = (sp_[:, k:k + 1] for k in range(7))
    ps = psum
    n1 = Norm(nc, S, K, "n1", ps, 0, 1, sq, r)
    n2 = Norm(nc, S, K, "n2", ps, 0, 1, sq, r)
    n3 = Norm(nc, S, K, "n3", ps, 2, 3, sq, r)

    def h(i, s):
        return H[:, bass.ds(i * (2 * UT) + s * UT, UT)]

    def bank(s, b, n=1):
        return ps[:, 4 * s + b:4 * s + b + n, :].rearrange("p a b -> p (a b)")

    def kv(s):
        return bank(s, 2, 2).rearrange("p (t m c) -> p t m c", t=QT, m=2)

    def tiles(v, n=NT):
        return v.rearrange("p (t k) -> p t k", t=n)

    def over(v, k):
        return v.unsqueeze(2).broadcast_to([P, v.shape[1], k])

    block = ctx.enter_context(nc.Block())

    @block.tensor
    def _(pe):
        mm = nc.tensor.matmul

        def body(i):
            for s in (0, 1):
                pe.wait_ge(S["n3_x"], past(2 * i + s - 1))
                n1.centre(h(i, s), s)
            for s in (0, 1):
                n1.variance(pe, 2 * i + s, s)
            for s in (0, 1):
                pe.wait_ge(S["tn"], 2 * i + s + 1)
                mm(ps[:, 4 * s, :], W("at_wq"), tn[s], start=True, stop=True).then_inc(S["q"], 1)
                for t in range(QT):
                    m = mm(bank(s, 2, 2)[:, 256 * t:256 * t + 256], tn[s][:, P * t:P * t + P], W("at_wkv"), start=True, stop=True)
                m.then_inc(S["kv"], 1)
            for s in (0, 1):
                pe.wait_ge(S["qsq"], 2 * i + s + 1)
                mm(ps[:, 4 * s + 1, :], K("mean"), sq[s], start=True, stop=True).then_inc(S["qv"], 1)
            for s in (0, 1):
                pe.wait_ge(S["kn"], 2 * i + s + 1)
                pe.wait_ge(S["v"], 2 * i + s + 1)
                pe.wait_ge(S["qn"], 2 * i + s + 1)
                for j in range(U):
                    for t in range(NB):
                        c = P * (NB * j + t)
                        mm(bank(s, 0)[:, P * j + BK * t:P * j + BK * t + BK], kn[s][:, c:c + P], W("at_e"), start=True, stop=True)
                        m = mm(ps[BK * t:BK * t + BK, 4 * s, 256 + P * j:256 + P * j + P], W("at_f"), v[s][:, c:c + P], start=True, stop=True)
                m.then_inc(S["kpvp"], 1)
            for s in (0, 1):
                pe.wait_ge(S["kpt"], 2 * i + s + 1)
                for j in range(U):
                    for img in range(2):
                        lo = 64 * img
                        for t in range(NB):
                            k = (img * U + j) * NB + t
                            m = mm(bank(s, 2, 2)[:, P * k:P * k + P], qn[s][lo:lo + 64, P * (NB * j + t):P * (NB * j + t) + P],
                                   kpt[s][lo:lo + 64, P * j:P * j + P], start=True, stop=True)
                m.then_inc(S["sc"], 1)
            for s in (0, 1):
                pe.wait_ge(S["w"], 2 * i + s + 1)
                pe.wait_ge(S["vp"], 2 * i + s + 1)
                for k in range(NT):
                    m = nc.tensor.transpose(bank(s, 0, 2)[:, P * k:P * k + P], ex[s][:, P * k:P * k + P], K("ident"))
                m.then_inc(S["wt"], 1)
            for s in (0, 1):
                pe.wait_ge(S["wts"], 2 * i + s + 1)
                for j in range(U):
                    for img in range(2):
                        k = (img * U + j) * TOK
                        m = mm(ps[64 * img:64 * img + 64, 4 * s + 2, TOK * j:TOK * j + TOK], vp[s][:, P * j + 64 * img:P * j + 64 * img + 64],
                               wts[s][:, k:k + TOK], start=True, stop=True)
                m.then_inc(S["ao"], 1)
            for s in (0, 1):
                pe.wait_ge(S["aos"], 2 * i + s + 1)
                mm(ps[:, 4 * s + 3, :], W("at_wo"), ao[s], start=True, stop=True).then_inc(S["wo"], 1)
            for s in (0, 1):
                pe.wait_ge(S["o1"], 2 * i + s + 1)
                n2.centre(o1[s], s)
            for s in (0, 1):
                n2.variance(pe, 2 * i + s, s)
            for s in (0, 1):
                pe.wait_ge(S["o3"], 2 * i + s + 1)
                n3.centre(o3[s], s)
            for s in (0, 1):
                n3.variance(pe, 2 * i + s, s)

        rounds(pe, body)

    @block.scalar
    def _(act):
        A = nc.scalar.activation
        act.wait_ge(S["sp1"], 1)
        A(el, low, ACT.Exp).then_inc(S["sp2"], 1)
        act.wait_ge(S["sp3"], 1)
        A(ln1, onep, ACT.Ln).then_inc(S["sp4"], 1)
        act.wait_ge(S["sp6"], 1)

        def body(i):
            for s in (0, 1):
                n1.square(act, 2 * i + s, s)
            for s in (0, 1):
                n1.rstd(act, 2 * i + s, s)
            for s in (0, 1):
                act.wait_ge(S["n1_x"], 2 * i + s + 1)
                A(tn[s], xn[s], ACT.Identity, bias=W("L0_attn_b1"), scale=W("L0_attn_g1")).then_inc(S["tn"], 1)
            for s in (0, 1):
                act.wait_ge(S["q"], 2 * i + s + 1)
                A(sq[s], ps[:, 4 * s, :], ACT.Square).then_inc(S["qsq"], 1)
                act.wait_ge(S["kv"], 2 * i + s + 1)
                A(tiles(ksq[s], QT), kv(s)[:, :, 0, :], ACT.Square).then_inc(S["ksq"], 1)
                A(tiles(v[s], QT), kv(s)[:, :, 1, :], ACT.Copy).then_inc(S["v"], 1)
            for s in (0, 1):
                act.wait_ge(S["qm"], 2 * i + s + 1)
                A(qr[s], qm[s], ACT.Abs_reciprocal_sqrt).then_inc(S["qr"], 1)
                act.wait_ge(S["ksm"], 2 * i + s + 1)
                A(kr[s], ksm[s], ACT.Abs_reciprocal_sqrt).then_inc(S["kr"], 1)
            for s in (0, 1):
                act.wait_ge(S["kpvp"], 2 * i + s + 1)
                A(kpt[s], bank(s, 0)[:, 0:U * P], ACT.Copy).then_inc(S["kpt"], 1)
                A(vp[s], bank(s, 0)[:, U * P:2 * U * P], ACT.Copy).then_inc(S["vp"], 1)
            for s in (0, 1):
                act.wait_ge(S["sh"], 2 * i + s + 1)
                A(sh[s], sh[s], ACT.Exp, scale=sc).then_inc(S["ex"], 1)
            for s in (0, 1):
                act.wait_ge(S["wt"], 2 * i + s + 1)
                A(wts[s], bank(s, 0, 2), ACT.Copy).then_inc(S["wts"], 1)
            for s in (0, 1):
                act.wait_ge(S["ao"], 2 * i + s + 1)
                A(ao[s], ps[:, 4 * s + 2, :], ACT.Copy).then_inc(S["aos"], 1)
            for s in (0, 1):
                n2.square(act, 2 * i + s, s)
            for s in (0, 1):
                n2.rstd(act, 2 * i + s, s)
            for s in (0, 1):
                act.wait_ge(S["n2_x"], 2 * i + s + 1)
                A(o2[s], xn[s], ACT.Identity, bias=W("L0_attn_b2"), scale=W("L0_attn_g2")).then_inc(S["o2"], 1)
            for s in (0, 1):
                n3.square(act, 2 * i + s, s)
            for s in (0, 1):
                n3.rstd(act, 2 * i + s, s)

        rounds(act, body)

    @block.vector
    def _(dve):
        V = nc.vector
        x = W("L0_attn_scale")
        V.tensor_scalar(neg, x, -1.0, None, ALU.mult).then_inc(S["sp0"], 1)
        dve.wait_ge(S["sp0"], 1)
        V.tensor_tensor(low, x, neg, ALU.min).then_inc(S["sp1"], 1)
        dve.wait_ge(S["sp2"], 1)
        V.tensor_scalar(onep, el, 1.0, None, ALU.add).then_inc(S["sp3"], 1)
        dve.wait_ge(S["sp4"], 1)
        V.scalar_tensor_tensor(pos, x, 0.0, ln1, ALU.max, ALU.add).then_inc(S["sp5"], 1)
        dve.wait_ge(S["sp5"], 1)
        V.tensor_scalar(sc, pos, float(C) ** -0.5, None, ALU.mult).then_inc(S["sp6"], 1)

        def body(i):
            for s in (0, 1):
                n1.scale(dve, 2 * i + s, s, xn[s])
            for s in (0, 1):
                dve.wait_ge(S["ksq"], 2 * i + s + 1)
                V.tensor_reduce(kss[s], tiles(ksq[s]), AX.X, ALU.add).then_inc(S["kss"], 1)
                dve.wait_ge(S["qv"], 2 * i + s + 1)
                V.tensor_scalar(qm[s], ps[:, 4 * s + 1, :], float(C), 1e-24, ALU.mult, ALU.max).then_inc(S["qm"], 1)
                dve.wait_ge(S["kss"], 2 * i + s + 1)
                V.tensor_scalar(ksm[s], kss[s], 1e-24, None, ALU.max).then_inc(S["ksm"], 1)
            for s in (0, 1):
                dve.wait_ge(S["qr"], 2 * i + s + 1)
                V.tensor_tensor(qn[s], ps[:, 4 * s, :], qr[s], ALU.mult).then_inc(S["qn"], 1)
                dve.wait_ge(S["kr"], 2 * i + s + 1)
                for m in range(2):
                    o = kn[s].rearrange("p (t m c) -> p t m c", t=QT, m=2)[:, :, m, :]
                    k = kr[s].rearrange("p (t m) -> p t m", m=2)[:, :, m]
                    last = V.tensor_tensor(o, kv(s)[:, :, 0, 64 * m:64 * m + 64], over(k, 64), ALU.mult)
                last.then_inc(S["kn"], 1)
            for s in (0, 1):
                dve.wait_ge(S["sc"], 2 * i + s + 1)
                V.tensor_reduce(mx[s], tiles(bank(s, 2, 2)), AX.X, ALU.max).then_inc(S["mx"], 1)
                dve.wait_ge(S["mx"], 2 * i + s + 1)
                V.tensor_tensor(tiles(sh[s]), tiles(bank(s, 2, 2)), over(mx[s], P), ALU.subtract).then_inc(S["sh"], 1)
            for s in (0, 1):
                dve.wait_ge(S["ex"], 2 * i + s + 1)
                V.tensor_reduce(den[s], tiles(sh[s]), AX.X, ALU.add).then_inc(S["den"], 1)
                dve.wait_ge(S["den"], 2 * i + s + 1)
                V.reciprocal(rden[s], den[s]).then_inc(S["rden"], 1)
                dve.wait_ge(S["rden"], 2 * i + s + 1)
                V.tensor_tensor(tiles(ex[s]), tiles(sh[s]), over(rden[s], P), ALU.mult).then_inc(S["w"], 1)
            for s in (0, 1):
                dve.wait_ge(S["wo"], 2 * i + s + 1)
                V.scalar_tensor_tensor(o1[s], ps[:, 4 * s + 3, :], 0.1, h(i, s), ALU.mult, ALU.add).then_inc(S["o1"], 1)
            for s in (0, 1):
                n2.scale(dve, 2 * i + s, s, xn[s])
            for s in (0, 1):
                dve.wait_ge(S["o2"], 2 * i + s + 1)
                V.tensor_tensor(o3[s], o2[s], h(i, s), ALU.add).then_inc(S["o3"], 1)
            for s in (0, 1):
                n3.scale(dve, 2 * i + s, s, h(i, s))

        rounds(dve, body)


def routed_ffn(nc, ctx, K, W, H, psum):
    KEPT = max(1, TOK // 2) - 1
    MH = 2
    S = Sems(nc, ctx, "ff", Norm.names("n1") + " hs wb wbs dg wc gt eq cnt f fr ft fts hid g0 g1 y yf o")

    def sb(name, cols):
        t = ctx.enter_context(nc.sbuf_tensor("ff_" + name, [P, 2, cols], F32))
        return [t[:, s, :] for s in range(2)]

    sq, r, hs, wbs, dg = sb("sq", UT), sb("r", UT), sb("hs", UT), sb("wbs", 2 * UT), sb("dg", 2 * UT)
    wc, gt, eq, cnt, f = (sb(n, NT) for n in ("wc", "gt", "eq", "cnt", "f"))
    fr, fts, yf, o = sb("fr", UT), sb("fts", UT), sb("yf", UT), sb("o", UT)
    g = sb("g", 2 * MH * UT)
    junk = ctx.enter_context(nc.sbuf_tensor("ff_junk", [P, NT, TOK], BF16))
    junk2 = ctx.enter_context(nc.sbuf_tensor("ff_junk2", [P, NT, TOK], BF16))
    ps = psum
    n1 = Norm(nc, S, K, "n1", ps, 2, 3, sq, r)

    def h(i, s):
        return H[:, bass.ds(i * (2 * UT) + s * UT, UT)]

    def bank(s, b, n=1):
        return ps[:, 4 * s + b:4 * s + b + n, :].rearrange("p a b -> p (a b)")

    def tiles(v, n=NT):
        return v.rearrange("p (t k) -> p t k", t=n)

    block = ctx.enter_context(nc.Block())

    @block.tensor
    def _(pe):
        mm = nc.tensor.matmul

        def body(i):
            for s in (0, 1):
                pe.wait_ge(S["hs"], 2 * i + s + 1)
                pe.wait_ge(S[f"g{s}"], i * (2 * MH))
                for img in range(2):
                    m = mm(ps[:, 4 * s + img, :], W("ff_wr")[64 * img:64 * img + 64, :], hs[s][64 * img:64 * img + 64, :], start=True, stop=True)
                m.then_inc(S["wb"], 1)
            for k in range(2 * MH):
                img, half = k % 2, k // 2
                lo = 64 * img
                for s in (0, 1):
                    n = 2 * i + s
                    pe.wait_ge(S["wbs"], n + 1)
                    if k >= 2:
                        pe.wait_ge(S[f"g{s}"], i * (2 * MH) + k - 1)
                    mm(ps[:, 4 * s + img, :], W("ff_w1")[lo:lo + 64, P * half:P * half + P], hs[s][lo:lo + 64, :],
                       start=True, stop=True).then_inc(S["hid"], 1)
            for s in (0, 1):
                pe.wait_ge(S["fr"], 2 * i + s + 1)
                pe.wait_ge(S["n1_x"], past(2 * i + s - 1))
                for t in range(QT):
                    m = mm(ps[:, 4 * s + 2, P * t:P * t + P], fr[s][:, P * t:P * t + P], K("ident"), start=True, stop=True)
                m.then_inc(S["ft"], 1)
            for s in (0, 1):
                pe.wait_ge(S[f"g{s}"], i * (2 * MH) + 2 * MH)
                for half in range(MH):
                    for img in range(2):
                        k = 2 * half + img
                        m = mm(ps[64 * img:64 * img + 64, 4 * s + 3, :], W("ff_w2")[:, 64 * half:64 * half + 64], g[s][:, UT * k:UT * k + UT],
                               start=(half == 0), stop=(half == MH - 1))
                m.then_inc(S["y"], 1)
            for s in (0, 1):
                pe.wait_ge(S["o"], 2 * i + s + 1)
                n1.centre(o[s], s)
            for s in (0, 1):
                n1.variance(pe, 2 * i + s, s)

        rounds(pe, body)

    @block.scalar
    def _(act):
        A = nc.scalar.activation

        def body(i):
            for s in (0, 1):
                n = 2 * i + s
                act.wait_ge(S["n1_c"], past(n - 1))
                act.wait_ge(S["o"], past(n - 1))
                A(hs[s], h(i, s), ACT.Copy).then_inc(S["hs"], 1)
            for s in (0, 1):
                act.wait_ge(S["wb"], 2 * i + s + 1)
                A(wbs[s], bank(s, 0, 2), ACT.Identity, bias=W("L0_ffn_br")).then_inc(S["wbs"], 1)
            for k in range(2 * MH):
                for s in (0, 1):
                    n = 2 * i + s
                    act.wait_ge(S["hid"], i * (4 * MH) + 2 * k + s + 1)
                    A(g[s][:, UT * k:UT * k + UT], ps[:, 4 * s + k % 2, :], ACT.Gelu_apprx_tanh, bias=W("ff_b1")[:, k // 2:k // 2 + 1]).then_inc(S[f"g{s}"], 1)
            for s in (0, 1):
                act.wait_ge(S["ft"], 2 * i + s + 1)
                A(fts[s], ps[:, 4 * s + 2, :], ACT.Copy).then_inc(S["fts"], 1)
            for s in (0, 1):
                n1.square(act, 2 * i + s, s)
            for s in (0, 1):
                n1.rstd(act, 2 * i + s, s)

        rounds(act, body)

    @block.vector
    def _(dve):
        V = nc.vector

        def body(i):
            for s in (0, 1):
                n = 2 * i + s
                dve.wait_ge(S["wbs"], n + 1)
                dve.wait_ge(S["wc"], past(n - 1))
                V.tensor_tensor(tiles(dg[s]), tiles(wbs[s]), K("ident").unsqueeze(1).broadcast_to([P, NT, P]), ALU.mult).then_inc(S["dg"], 1)
            for s in (0, 1):
                n = 2 * i + s
                dve.wait_ge(S["dg"], n + 1)
                V.tensor_reduce(wc[s], tiles(dg[s]), AX.X, ALU.add).then_inc(S["wc"], 1)
            for s in (0, 1):
                n = 2 * i + s
                dve.wait_ge(S["wc"], n + 1)
                dve.wait_ge(S["cnt"], n)
                for k in range(NT):
                    row = wbs[s][:, TOK * (k // 2):TOK * (k // 2) + TOK]
                    a = V.tensor_scalar(junk[:, k, :], row, wc[s][:, k:k + 1], None, ALU.is_gt, ALU.add, accum_out=gt[s][:, k:k + 1])
                    b = V.scalar_tensor_tensor(junk2[:, k, :], row, wc[s][:, k:k + 1], K("earlier")[:, TOK * (k % 2):TOK * (k % 2) + TOK],
                                               ALU.is_equal, ALU.mult, accum_out=eq[s][:, k:k + 1])
                a.then_inc(S["gt"], 1)
                b.then_inc(S["eq"], 1)
                dve.wait_ge(S["gt"], n + 1)
                dve.wait_ge(S["eq"], n + 1)
                V.tensor_tensor(cnt[s], gt[s], eq[s], ALU.add).then_inc(S["cnt"], 1)
                dve.wait_ge(S["cnt"], n + 1)
                V.scalar_tensor_tensor(f[s], cnt[s], KEPT - 0.5, wc[s], ALU.is_lt, ALU.mult).then_inc(S["f"], 1)
                dve.wait_ge(S["f"], n + 1)
                for img in range(2):
                    d = fr[s].rearrange("p (t m c) -> p t m c", t=QT, m=2)[:, :, img, :]
                    last = V.tensor_copy(d, f[s][:, QT * img:QT * img + QT].unsqueeze(2).broadcast_to([P, QT, 64]))
                last.then_inc(S["fr"], 1)
            for s in (0, 1):
                n = 2 * i + s
                dve.wait_ge(S["y"], n + 1)
                dve.wait_ge(S["fts"], n + 1)
                V.scalar_tensor_tensor(yf[s], ps[:, 4 * s + 3, :], W("ff_b2"), fts[s], ALU.add, ALU.mult).then_inc(S["yf"], 1)
                dve.wait_ge(S["yf"], n + 1)
                V.scalar_tensor_tensor(o[s], hs[s], 2.0, yf[s], ALU.mult, ALU.add).then_inc(S["o"], 1)
            for s in (0, 1):
                n1.scale(dve, 2 * i + s, s, h(i, s))

        rounds(dve, body)


PI = 3.1415925


def holographic(nc, ctx, K, W, H, psum):
    S = Sems(nc, ctx, "ho", Norm.names("n1", "n2") +
             " pr0 pr1 pr2 pr3 pr4 pr5 pr6 pr7 pr8 sn0 sn1 wg gb hs t1 a1 t2 a2 vp vps g1 g1s vt vts k2 tk uk kf q2 tq uq qf sa sb sas sbs"
             " ct cts gd gt gg mr mi mrs mis rr ri pos df dg cb nb wo wos o")

    def sb(name, cols, n=2):
        t = ctx.enter_context(nc.sbuf_tensor("ho_" + name, [P, n, cols], F32))
        return [t[:, s, :] for s in range(n)]

    sq, r, hs = sb("sq", UT), sb("r", UT), sb("hs", UT)
    a1, a2, vps, vts = sb("a1", UT), sb("a2", UT), sb("vps", UT), sb("vts", UT)
    g1s = sb("g1s", UT)
    tk, uk, kf, tq, uq, qf = (sb(n, UT) for n in ("tk", "uk", "kf", "tq", "uq", "qf"))
    sa, sc_ = sb("sa", 2 * UT), sb("sc", UT)
    cts, gt, gg = sb("cts", UT), sb("gt", UT), sb("gg", UT)
    mr, mi, mrs, mis = (sb(n, UT) for n in ("mr", "mi", "mrs", "mis"))
    pos, df, cb, nb, wos, o = (sb(n, UT) for n in ("pos", "df", "cb", "nb", "wos", "o"))
    rr, ri = mr, mi
    tab = ctx.enter_context(nc.sbuf_tensor("ho_tab", [P, 14, TOK], F32))
    turns, whole, red1, red2, red3, red, mag, low, sinp, cosp, sinn, cosn = (tab[:, k, :] for k in range(12))
    wgd = ctx.enter_context(nc.sbuf_tensor("ho_wgd", [32, P], F32))
    gb = ctx.enter_context(nc.sbuf_tensor("ho_gb", [P, 2], F32))
    ps = psum
    n1 = Norm(nc, S, K, "n1", ps, 1, 2, sq, r)
    n2 = Norm(nc, S, K, "n2", ps, 1, 2, sq, r)

    def h(i, s):
        return H[:, bass.ds(i * (2 * UT) + s * UT, UT)]

    def bank(s, b, n=1):
        return ps[:, 4 * s + b:4 * s + b + n, :].rearrange("p a b -> p (a b)")

    def tiles(v, n):
        return v.rearrange("p (t k) -> p t k", t=n)

    def each(v, n):
        return v.unsqueeze(1).broadcast_to([P, n, v.shape[1]])

    block = ctx.enter_context(nc.Block())

    @block.tensor
    def _(pe):
        mm = nc.tensor.matmul
        pe.wait_ge(S["wg"], 1)

        def body(i):
            for s in (0, 1):
                n = 2 * i + s
                pe.wait_ge(S["hs"], n + 1)
                pe.wait_ge(S["n2_x"], past(n - 1))
                mm(ps[:, 4 * s, :], W("ho_wk1"), hs[s], start=True, stop=True).then_inc(S["t1"], 1)
                mm(ps[:, 4 * s + 1, :], W("ho_wq1"), hs[s], start=True, stop=True).then_inc(S["t2"], 1)
                mm(ps[:, 4 * s + 2, :], W("ho_wvp"), hs[s], start=True, stop=True).then_inc(S["vp"], 1)
                for t in range(QT):
                    m = mm(ps[:, 4 * s + 3, P * t:P * t + P], hs[s][:, P * t:P * t + P], W("ho_wvc"), start=True, stop=True)
                m.then_inc(S["vt"], 1)
            for s in (0, 1):
                n = 2 * i + s
                pe.wait_ge(S["a1"], n + 1)
                mm(ps[:, 4 * s, :], W("ho_wk2"), a1[s], start=True, stop=True).then_inc(S["k2"], 1)
                pe.wait_ge(S["a2"], n + 1)
                mm(ps[:, 4 * s + 1, :], W("ho_wq2"), a2[s], start=True, stop=True).then_inc(S["q2"], 1)
                pe.wait_ge(S["vps"], n + 1)
                mm(ps[0:32, 4 * s + 2, :], W("ho_wg1"), hs[s], start=True, stop=True).then_inc(S["g1"], 1)
                pe.wait_ge(S["vts"], n + 1)
                pe.wait_ge(S["g1s"], n + 1)
                mm(ps[:, 4 * s + 3, :], wgd[:, :], g1s[s][0:32, :], start=True, stop=True).then_inc(S["gd"], 1)
            for s in (0, 1):
                n = 2 * i + s
                pe.wait_ge(S["kf"], n + 1)
                pe.wait_ge(S["qf"], n + 1)
                for img in range(2):
                    lo = 64 * img
                    for j in range(U):
                        c = TOK * j
                        m = mm(ps[:, 4 * s + img, TOK * j:TOK * j + TOK], kf[s][lo:lo + 64, c:c + P], qf[s][lo:lo + 64, c:c + TOK], start=True, stop=True)
                m.then_inc(S["sa"], 1)
                pe.wait_ge(S["gt"], n + 1)
                for img in range(2):
                    lo = 64 * img
                    for j in range(U):
                        c = TOK * j + P
                        k = img * U + j
                        m = mm(ps[:, 4 * s + 2 + img, P * j:P * j + P], kf[s][lo:lo + 64, c:c + P], qf[s][lo:lo + 64, c:c + P], start=True, stop=True)
                m.then_inc(S["sb"], 1)
            for s in (0, 1):
                n = 2 * i + s
                pe.wait_ge(S["sas"], n + 1)
                pe.wait_ge(S["sbs"], n + 1)
                for j in range(U):
                    for img in range(2):
                        k = img * U + j
                        o_ = ps[64 * img:64 * img + 64, 4 * s, TOK * j:TOK * j + TOK]
                        v0 = vts[s][:, 2 * P * j + 64 * img:2 * P * j + 64 * img + 64]
                        v1 = vts[s][:, 2 * P * j + P + 64 * img:2 * P * j + P + 64 * img + 64]
                        mm(o_, v0, sa[s][:, TOK * k:TOK * k + TOK], start=True, stop=False, skip_group_check=True)
                        m = mm(o_[:, P:], v1, sc_[s][:, P * k:P * k + P], start=False, stop=True, skip_group_check=True)
                m.then_inc(S["ct"], 1)
            for s in (0, 1):
                pe.wait_ge(S["cb"], 2 * i + s + 1)
                n1.centre(cb[s], s)
            for s in (0, 1):
                n1.variance(pe, 2 * i + s, s)
            for s in (0, 1):
                pe.wait_ge(S["nb"], 2 * i + s + 1)
                mm(ps[:, 4 * s + 3, :], W("ho_wo"), nb[s], start=True, stop=True).then_inc(S["wo"], 1)
            for s in (0, 1):
                pe.wait_ge(S["o"], 2 * i + s + 1)
                n2.centre(o[s], s)
            for s in (0, 1):
                n2.variance(pe, 2 * i + s, s)

        rounds(pe, body)

    @block.scalar
    def _(act):
        A = nc.scalar.activation
        act.wait_ge(S["pr6"], 1)
        A(sinp, red, ACT.Sin).then_inc(S["sn0"], 1)
        act.wait_ge(S["pr8"], 1)
        A(cosp, low, ACT.Sin).then_inc(S["sn1"], 1)
        act.wait_ge(S["gb"], 1)

        def body(i):
            for s in (0, 1):
                act.wait_ge(S["o"], past(2 * i + s - 1))
                A(hs[s], h(i, s), ACT.Copy).then_inc(S["hs"], 1)
            for s in (0, 1):
                n = 2 * i + s
                act.wait_ge(S["t1"], n + 1)
                A(a1[s], ps[:, 4 * s, :], ACT.Tanh, bias=W("L1_attn_bk1")).then_inc(S["a1"], 1)
                act.wait_ge(S["t2"], n + 1)
                A(a2[s], ps[:, 4 * s + 1, :], ACT.Tanh, bias=W("L1_attn_bq1")).then_inc(S["a2"], 1)
                act.wait_ge(S["vp"], n + 1)
                A(vps[s], ps[:, 4 * s + 2, :], ACT.Identity, bias=W("L1_attn_bvp")).then_inc(S["vps"], 1)
            for s in (0, 1):
                n = 2 * i + s
                act.wait_ge(S["g1"], n + 1)
                A(g1s[s][0:32, :], ps[0:32, 4 * s + 2, :], ACT.Relu, bias=W("ho_bg1")).then_inc(S["g1s"], 1)
                act.wait_ge(S["k2"], n + 1)
                A(tk[s], ps[:, 4 * s, :], ACT.Tanh, bias=W("ho_bk2")).then_inc(S["tk"], 1)
                act.wait_ge(S["q2"], n + 1)
                A(tq[s], ps[:, 4 * s + 1, :], ACT.Tanh, bias=W("ho_bq2")).then_inc(S["tq"], 1)
                act.wait_ge(S["gd"], n + 1)
                A(gt[s], ps[:, 4 * s + 3, :], ACT.Tanh, bias=gb[:, 1:2], scale=0.5).then_inc(S["gt"], 1)
            for s in (0, 1):
                n = 2 * i + s
                act.wait_ge(S["uk"], n + 1)
                A(kf[s], uk[s], ACT.Sin, bias=K("turn_bias"), scale=K("turn_scale")).then_inc(S["kf"], 1)
                act.wait_ge(S["uq"], n + 1)
                A(qf[s], uq[s], ACT.Sin, bias=K("turn_bias"), scale=K("turn_scale")).then_inc(S["qf"], 1)
            for s in (0, 1):
                n1.square(act, 2 * i + s, s)
            for s in (0, 1):
                n1.rstd(act, 2 * i + s, s)
            for s in (0, 1):
                act.wait_ge(S["n1_x"], 2 * i + s + 1)
                A(nb[s], df[s], ACT.Identity, bias=W("L1_attn_ln_b"), scale=W("L1_attn_ln_g")).then_inc(S["nb"], 1)
            for s in (0, 1):
                act.wait_ge(S["wo"], 2 * i + s + 1)
                A(wos[s], ps[:, 4 * s + 3, :], ACT.Identity, bias=W("L1_attn_bo")).then_inc(S["wos"], 1)
            for s in (0, 1):
                n2.square(act, 2 * i + s, s)
            for s in (0, 1):
                n2.rstd(act, 2 * i + s, s)

        rounds(act, body)

    @block.gpsimd
    def _(pool):
        G = nc.gpsimd
        pool.wait_ge(S["sn1"], 1)

        def body(i):
            for s in (0, 1):
                n = 2 * i + s
                pool.wait_ge(S["vps"], n + 1)
                pool.wait_ge(S["pos"], past(n - 1))
                G.tensor_tensor(tiles(mr[s], U), tiles(vps[s], U), each(cosp, U), ALU.mult).then_inc(S["mr"], 1)
                G.tensor_tensor(tiles(mi[s], U), tiles(vps[s], U), each(sinp, U), ALU.mult).then_inc(S["mi"], 1)

        rounds(pool, body)

    @block.vector
    def _(dve):
        V = nc.vector
        V.tensor_tensor(wgd[:, :], W("ho_wg2a"), W("ho_wg2b"), ALU.subtract).then_inc(S["wg"], 1)
        V.tensor_tensor(gb[:, 0:1], W("ho_bg2a"), W("ho_bg2b"), ALU.subtract).then_inc(S["pr0"], 1)
        dve.wait_ge(S["pr0"], 1)
        V.tensor_scalar(gb[:, 1:2], gb[:, 0:1], 0.5, None, ALU.mult).then_inc(S["gb"], 1)
        C1, C2 = 6.28125, 0.0019350051879882812
        C3 = 2 * np.pi - C1 - C2
        MAGIC = 1.5 * 2.0 ** 23
        ph = W("ho_phases")
        V.tensor_scalar(turns, ph, 1 / (2 * np.pi), MAGIC, ALU.mult, ALU.add).then_inc(S["pr1"], 1)
        dve.wait_ge(S["pr1"], 1)
        V.tensor_scalar(whole, turns, -MAGIC, None, ALU.add).then_inc(S["pr2"], 1)
        dve.wait_ge(S["pr2"], 1)
        V.scalar_tensor_tensor(red1, whole, -C1, ph, ALU.mult, ALU.add).then_inc(S["pr3"], 1)
        dve.wait_ge(S["pr3"], 1)
        V.scalar_tensor_tensor(red2, whole, -C2, red1, ALU.mult, ALU.add).then_inc(S["pr4"], 1)
        dve.wait_ge(S["pr4"], 1)
        V.scalar_tensor_tensor(red3, whole, -float(C3), red2, ALU.mult, ALU.add).then_inc(S["pr5"], 1)
        dve.wait_ge(S["pr5"], 1)
        V.tensor_scalar(red, red3, PI, -PI, ALU.min, ALU.max).then_inc(S["pr6"], 1)
        dve.wait_ge(S["pr6"], 1)
        V.scalar_tensor_tensor(mag, red, -1.0, red, ALU.mult, ALU.max).then_inc(S["pr7"], 1)
        dve.wait_ge(S["pr7"], 1)
        V.tensor_scalar(low, mag, -1.0, PI / 2, ALU.mult, ALU.add).then_inc(S["pr8"], 1)
        dve.wait_ge(S["sn1"], 1)
        dve.wait_ge(S["sn0"], 1)
        V.tensor_tensor(cosn, cosp, K("root"), ALU.mult)
        V.tensor_tensor(sinn, sinp, K("root"), ALU.mult).then_inc(S["pr0"], 1)
        dve.wait_ge(S["pr0"], 2)

        def body(i):
            for s in (0, 1):
                n = 2 * i + s
                dve.wait_ge(S["vt"], n + 1)
                V.tensor_tensor(tiles(vts[s], QT), tiles(ps[:, 4 * s + 3, :], QT), each(W("ho_bvc"), QT), ALU.add).then_inc(S["vts"], 1)
            for s in (0, 1):
                n = 2 * i + s
                dve.wait_ge(S["tk"], n + 1)
                V.scalar_tensor_tensor(uk[s], tk[s], K("turn_sign"), tk[s], ALU.mult, ALU.max).then_inc(S["uk"], 1)
                dve.wait_ge(S["tq"], n + 1)
                V.scalar_tensor_tensor(uq[s], tq[s], K("turn_sign"), tq[s], ALU.mult, ALU.max).then_inc(S["uq"], 1)
            for s in (0, 1):
                n = 2 * i + s
                dve.wait_ge(S["mr"], n + 1)
                for j in range(U):
                    m = V.tensor_tensor_scan(mrs[s][:, TOK * j:TOK * j + TOK], K("ones"), mr[s][:, TOK * j:TOK * j + TOK], 0.0, ALU.mult, ALU.add)
                m.then_inc(S["mrs"], 1)
                dve.wait_ge(S["mi"], n + 1)
                for j in range(U):
                    m = V.tensor_tensor_scan(mis[s][:, TOK * j:TOK * j + TOK], K("ones"), mi[s][:, TOK * j:TOK * j + TOK], 0.0, ALU.mult, ALU.add)
                m.then_inc(S["mis"], 1)
            for s in (0, 1):
                n = 2 * i + s
                dve.wait_ge(S["sa"], n + 1)
                V.tensor_tensor(tiles(sa[s], 2 * U), tiles(bank(s, 0, 2), 2 * U), each(K("causal"), 2 * U), ALU.mult).then_inc(S["sas"], 1)
                dve.wait_ge(S["sb"], n + 1)
                for img in range(2):
                    m = V.tensor_tensor(tiles(sc_[s][:, P * U * img:P * U * (img + 1)], U), tiles(ps[:, 4 * s + 2 + img, 0:U * P], U),
                                        each(K("causal")[:, 0:P], U), ALU.mult)
                m.then_inc(S["sbs"], 1)
            for s in (0, 1):
                n = 2 * i + s
                dve.wait_ge(S["mrs"], n + 1)
                V.tensor_tensor(tiles(rr[s], U), tiles(mrs[s], U), each(cosn, U), ALU.mult).then_inc(S["rr"], 1)
                dve.wait_ge(S["mis"], n + 1)
                V.tensor_tensor(tiles(ri[s], U), tiles(mis[s], U), each(sinn, U), ALU.mult).then_inc(S["ri"], 1)
                dve.wait_ge(S["gt"], n + 1)
                V.tensor_scalar(gg[s], gt[s], 0.5, 0.5, ALU.mult, ALU.add).then_inc(S["gg"], 1)
                dve.wait_ge(S["rr"], n + 1)
                dve.wait_ge(S["ri"], n + 1)
                V.tensor_tensor(pos[s], rr[s], ri[s], ALU.add).then_inc(S["pos"], 1)
            for s in (0, 1):
                n = 2 * i + s
                dve.wait_ge(S["ct"], n + 1)
                V.tensor_tensor(tiles(cts[s], U), tiles(ps[:, 4 * s, :], U), each(K("root32"), U), ALU.mult).then_inc(S["cts"], 1)
                dve.wait_ge(S["cts"], n + 1)
                dve.wait_ge(S["pos"], n + 1)
                V.tensor_tensor(df[s], pos[s], cts[s], ALU.subtract).then_inc(S["df"], 1)
                dve.wait_ge(S["df"], n + 1)
                dve.wait_ge(S["gg"], n + 1)
                V.tensor_tensor(gg[s], df[s], gg[s], ALU.mult).then_inc(S["dg"], 1)
                dve.wait_ge(S["dg"], n + 1)
                V.tensor_tensor(cb[s], gg[s], cts[s], ALU.add).then_inc(S["cb"], 1)
            for s in (0, 1):
                n1.scale(dve, 2 * i + s, s, df[s])
            for s in (0, 1):
                n = 2 * i + s
                dve.wait_ge(S["wos"], n + 1)
                V.scalar_tensor_tensor(o[s], hs[s], 2.0, wos[s], ALU.mult, ALU.add).then_inc(S["o"], 1)
            for s in (0, 1):
                n2.scale(dve, 2 * i + s, s, h(i, s))

        rounds(dve, body)


NE, FF = 16, 128
FAR = 3.0e38
PARTS = 3


def experts(nc, ctx, K, W, H, psum, w1_dram, w2_dram, sel_dram, out):
    GR = 2 * NE
    HID, Y, GB, M1, M2 = 0, 2, 4, 6, 7
    S = Sems(nc, ctx, "mo", "id16 w1in w2in selin wh wl sel b2h b2r b2m b2l"
             " hs xhi xlo lgp lg m1 e1 p1 q1 b1 l2 m2 e2 p2 q2 b2 dd ex s1 w1 w2 g1 g2 g gh gr gm_ gl gtp gts bb acc"
             " hid rel gb gbs y mul add fat fht sa ma xa sqa va ra na ga ba ha sz mz xz sqz vz rz o st0 st1")

    def sb(name, cols, dt=F32):
        t = ctx.enter_context(nc.sbuf_tensor("mo_" + name, [P, 2, cols], dt))
        return [t[:, s, :] for s in range(2)]

    stage = ctx.enter_context(nc.sbuf_tensor("mo_stage", [P, NE * FF], F32))
    stage2 = ctx.enter_context(nc.sbuf_tensor("mo_stage2", [P, NE * P], F32))
    wh = ctx.enter_context(nc.sbuf_tensor("mo_wh", [P, NE * FF], BF16))
    wl = ctx.enter_context(nc.sbuf_tensor("mo_wl", [P, NE * FF], BF16))
    w2 = ctx.enter_context(nc.sbuf_tensor("mo_wdown", [FF, NE * C], F32))
    sel = ctx.enter_context(nc.sbuf_tensor("mo_sel", [PARTS * GR, NE * P], BF16))
    b2p = ctx.enter_context(nc.sbuf_tensor("mo_b2p", [PARTS * GR, 3, P], BF16))
    b2r = ctx.enter_context(nc.sbuf_tensor("mo_b2r", [PARTS * GR, P], F32))
    ident16 = ctx.enter_context(nc.sbuf_tensor("mo_ident16", [P, P], BF16))
    hs, acc = sb("hs", UT), sb("acc", UT)
    xa, xb = sb("xsa", UT, BF16), sb("xsb", UT, BF16)
    lg, e1, p1, b1, l2, e2, p2, b2, g1, g2, gate, gr = (sb(n, NT * NE) for n in "lg e1 p1 b1 l2 e2 p2 b2 g1 g2 gate gr".split())
    m1, q1, m2, q2, dd, ex, s1, v1, v2 = (sb(n, NT) for n in "m1 q1 m2 q2 dd ex s1 v1 v2".split())
    g3 = sb("g3", QT * PARTS * GR, BF16)
    gts = sb("gts", UT, BF16)
    hid = sb("hid", 2 * UT)
    gbs, tmp = sb("gbs", UT), sb("tmp", UT)
    xc, sq, ya, yb = sb("xc", UT), sb("sq", UT), sb("ya", UT), sb("yb", UT)
    sm, mn, vs, rs = (sb(n, NT) for n in "sm mn vs rs".split())
    ps = psum

    def h(i, s):
        return H[:, bass.ds(i * (2 * UT) + s * UT, UT)]

    def tiles(v, n=NT):
        return v.rearrange("p (t k) -> p t k", t=n)

    def over(v, k):
        return v.unsqueeze(2).broadcast_to([P, v.shape[1], k])

    def each(v, n=NT):
        return v.unsqueeze(1).broadcast_to([P, n, v.shape[1]])

    def parts(v):
        return v.rearrange("p (t q r) -> p t q r", t=QT, q=PARTS)

    def turned(b):
        return ps[:, b, :].bitcast(BF16)

    out_v = out.rearrange("(u j m) (t p) c -> u p j t m c", j=U, m=2, p=P)
    block = ctx.enter_context(nc.Block())

    def sweep(eng, body):
        for s in (0, 1):
            body(0, s, first=(s == 0))
        with eng.Fori(1, NU // 2 - 1) as i:
            for s in (0, 1):
                body(i, s)
        for s in (0, 1):
            body(NU // 2 - 1, s, last=(s == 1))

    @block.sync
    def _(sp):
        sp.dma_start(stage[0:64, :].rearrange("h (e f) -> h e f", e=NE), w1_dram.rearrange("e h f -> h e f")).then_inc(S["w1in"], 16)
        sp.dma_start(stage[64:128, :].rearrange("h (e f) -> h e f", e=NE), w1_dram.rearrange("e h f -> h e f")).then_inc(S["w1in"], 16)
        sp.dma_start(stage2[0:PARTS * GR, :], sel_dram).then_inc(S["selin"], 16)
        sp.dma_start(w2[:, :].rearrange("f (e h) -> f e h", e=NE), w2_dram.rearrange("e f h -> f e h")).then_inc(S["w2in"], 16)

        def store(i, s):
            src = yb[s].rearrange("p (j t m c) -> p j t m c", j=U, t=2, m=2)
            sp.wait_ge(S["o"], 2 * i + s + 1)
            for j in range(U):
                for m in range(2):
                    sp.dma_start(out_v[bass.ds(2 * i + s, 1), :, j, :, m, :].rearrange("a p t c -> (a p) t c"), src[:, j, :, m, :])\
                      .then_inc(S[f"st{s}"], 16)

        for s in (0, 1):
            store(0, s)
        with sp.Fori(1, NU // 2) as i:
            for s in (0, 1):
                store(i, s)
        sp.wait_ge(S["st0"], 16 * 2 * U * (NU // 2))
        sp.wait_ge(S["st1"], 16 * 2 * U * (NU // 2))

    @block.tensor
    def _(pe):
        mm = nc.tensor.matmul

        def logits(g, s):
            pe.wait_ge(S["hs"], g + 1)
            pe.wait_ge(S["xa"], past(g - 1))
            for t in range(QT):
                m = mm(ps[:, M1, GR * t:GR * t + GR], hs[s][:, P * t:P * t + P], W("mo_gate"), start=True, stop=True)
            m.then_inc(S["lgp"], 1)

        def turn_gates(g, s):
            pe.wait_ge(S["gl"], g + 1)
            pe.wait_ge(S["ha"], past(g - 1))
            for t in range(QT):
                m = nc.tensor.transpose(turned(M2)[0:PARTS * GR, P * t:P * t + P], g3[s][:, PARTS * GR * t:PARTS * GR * (t + 1)], ident16[:, :])
            m.then_inc(S["gtp"], 1)

        def output_biases(g, s):
            pe.wait_ge(S["gts"], g + 1)
            for k in range(3):
                m = mm(ps[:, M2, :], b2p[:, k, :], gts[s][0:PARTS * GR, :], start=(k == 0), stop=(k == 2))
            m.then_inc(S["bb"], 1)

        def up(n, s, e):
            if e == 0:
                pe.wait_ge(S["xlo"], n + 1)
            for img, x in ((0, xa[s]), (1, xb[s])):
                pe.wait_ge(S["rel"], n * (2 * NE) + max(2 * e + img - 1, 0))
                mm(ps[:, HID + img, :], wh[:, FF * e:FF * e + FF], x, start=True, stop=False)
                mm(ps[:, HID + img, :], wl[:, FF * e:FF * e + FF], x, start=False, stop=True).then_inc(S["hid"], 1)

        def spread_gate(n, s, e):
            pe.wait_ge(S["gbs"], n * NE + max(e - 1, 0))
            mm(ps[:, GB + e % 2, :], sel[:, P * e:P * e + P], gts[s][0:PARTS * GR, :], start=True, stop=True).then_inc(S["gb"], 1)

        def down(n, s, e):
            pe.wait_ge(S["rel"], n * (2 * NE) + 2 * e + 2)
            pe.wait_ge(S["mul"], n * NE + max(e - 1, 0))
            for img in range(2):
                m = mm(ps[64 * img:64 * img + 64, Y + e % 2, :], w2[:, C * e:C * e + C], hid[e % 2][:, UT * img:UT * img + UT], start=True, stop=True)
            m.then_inc(S["y"], 1)

        def turn_tokens(f, s):
            pe.wait_ge(S["add"], NE * (f + 1))
            pe.wait_ge(S["lg"], f + 2)
            for t in range(QT):
                m = nc.tensor.transpose(ps[:, M1, P * t:P * t + P], acc[s][:, P * t:P * t + P], K("ident"))
            m.then_inc(S["fat"], 1)
            pe.wait_ge(S["acc"], f + 2)
            for t in range(QT):
                m = nc.tensor.transpose(ps[:, M2, P * t:P * t + P], hs[s][:, P * t:P * t + P], K("ident"))
            m.then_inc(S["fht"], 1)

        pe.wait_ge(S["w2in"], 16)
        pe.wait_ge(S["sel"], 1)
        pe.wait_ge(S["wl"], 1)
        pe.wait_ge(S["b2l"], 1)
        pe.wait_ge(S["id16"], 1)
        logits(0, 0)
        turn_gates(0, 0)
        output_biases(0, 0)

        def body(i, s, first=False, last=False):
            n = 2 * i + s
            up(n, s, 0)
            for e in range(NE):
                if e + 1 < NE:
                    up(n, s, e + 1)
                spread_gate(n, s, e)
                down(n, s, e)
                if e == 1 and not first:
                    turn_tokens(n - 1, 1 - s)
                if e == 4 and not last:
                    logits(n + 1, 1 - s)
                if e == 14 and not last:
                    turn_gates(n + 1, 1 - s)
                if e == 15 and not last:
                    output_biases(n + 1, 1 - s)

        sweep(pe, body)
        pe.wait_ge(S["add"], NE * NU)
        for t in range(QT):
            m = nc.tensor.transpose(ps[:, M1, P * t:P * t + P], acc[1][:, P * t:P * t + P], K("ident"))
        m.then_inc(S["fat"], 1)
        for t in range(QT):
            m = nc.tensor.transpose(ps[:, M2, P * t:P * t + P], hs[1][:, P * t:P * t + P], K("ident"))
        m.then_inc(S["fht"], 1)

    @block.scalar
    def _(act):
        A = nc.scalar.activation

        def tokens(i, s, g):
            act.wait_ge(S["fht"], past(g - 1))
            act.wait_ge(S["add"], past((g - 1) * NE))
            A(hs[s], h(i, s), ACT.Copy).then_inc(S["hs"], 1)
            act.wait_ge(S["hs"], g + 1)
            A(xa[s][0:64, :], hs[s][0:64, :], ACT.Copy).then_inc(S["xhi"], 1)
            A(xb[s][64:128, :], hs[s][64:128, :], ACT.Copy).then_inc(S["xhi"], 1)

        def exp(g, s):
            act.wait_ge(S["dd"], g + 1)
            A(ex[s], dd[s], ACT.Exp).then_inc(S["ex"], 1)

        def gates(g, s):
            act.wait_ge(S["gtp"], g + 1)
            A(gts[s][0:PARTS * GR, :], turned(M2)[0:PARTS * GR, 0:UT], ACT.Copy).then_inc(S["gts"], 1)

        def hidden(n, s, e):
            for img in range(2):
                act.wait_ge(S["hid"], n * (2 * NE) + 2 * e + img + 1)
                act.wait_ge(S["y"], n * NE + max(e - 1, 0))
                A(hid[e % 2][:, UT * img:UT * img + UT], ps[:, HID + img, :], ACT.Relu, bias=W("mo_b1")[:, e:e + 1]).then_inc(S["rel"], 1)

        def spread(n, s, e):
            act.wait_ge(S["gb"], n * NE + e + 1)
            act.wait_ge(S["mul"], n * NE + max(e - 1, 0))
            A(gbs[e % 2], ps[:, GB + e % 2, :], ACT.Copy).then_inc(S["gbs"], 1)

        def square(f, s, ready, done):
            act.wait_ge(S[ready], f + 1)
            A(sq[s], xc[s], ACT.Square).then_inc(S[done], 1)

        def rstd(f, s, ready, done):
            act.wait_ge(S[ready], f + 1)
            A(rs[s], vs[s], ACT.Abs_reciprocal_sqrt, bias=K("eps"), scale=1.0 / C).then_inc(S[done], 1)

        tokens(0, 0, 0)
        exp(0, 0)
        gates(0, 0)

        def body(i, s, first=False, last=False):
            n = 2 * i + s
            for e in range(NE):
                hidden(n, s, e)
                spread(n, s, e)
                if not first:
                    if e == 3:
                        square(n - 1, 1 - s, "xa", "sqa")
                    if e == 5:
                        rstd(n - 1, 1 - s, "va", "ra")
                    if e == 10:
                        square(n - 1, 1 - s, "xz", "sqz")
                    if e == 12:
                        rstd(n - 1, 1 - s, "vz", "rz")
                if not last:
                    if e == 2:
                        tokens(i + s, 1 - s, n + 1)
                    if e == 11:
                        exp(n + 1, 1 - s)
                    if e == 15:
                        gates(n + 1, 1 - s)

        sweep(act, body)
        square(NU - 1, 1, "xa", "sqa")
        rstd(NU - 1, 1, "va", "ra")
        square(NU - 1, 1, "xz", "sqz")
        rstd(NU - 1, 1, "vz", "rz")

    @block.gpsimd
    def _(pool):
        G = nc.gpsimd

        def affine(f, s):
            pool.wait_ge(S["na"], f + 1)
            G.tensor_tensor(tiles(ya[s]), tiles(ya[s]), each(W("mo_gamma")), ALU.mult).then_inc(S["ga"], 1)
            pool.wait_ge(S["ga"], f + 1)
            G.tensor_tensor(tiles(ya[s]), tiles(ya[s]), each(W("mo_beta")), ALU.add).then_inc(S["ba"], 1)

        def body(i, s, first=False, last=False):
            n = 2 * i + s
            pool.wait_ge(S["acc"], n + 1)
            for e in range(NE):
                pool.wait_ge(S["mul"], n * NE + e + 1)
                pool.wait_ge(S["add"], n * NE + e)
                G.tensor_tensor(acc[s], acc[s], tmp[e % 2], ALU.add).then_inc(S["add"], 1)
                if e == 7 and not first:
                    affine(n - 1, 1 - s)

        sweep(pool, body)
        affine(NU - 1, 1)

    @block.vector
    def _(dve):
        V = nc.vector

        def low_parts(g, s):
            dve.wait_ge(S["xhi"], 2 * (g + 1))
            V.tensor_tensor(xa[s][64:128, :], hs[s][0:64, :], xa[s][0:64, :], ALU.subtract)
            V.tensor_tensor(xb[s][0:64, :], hs[s][64:128, :], xb[s][64:128, :], ALU.subtract).then_inc(S["xlo"], 1)

        def logits(g, s):
            dve.wait_ge(S["lgp"], g + 1)
            V.tensor_tensor(tiles(lg[s]), tiles(ps[:, M1, 0:P]), each(W("mo_gate_b")), ALU.add).then_inc(S["lg"], 1)

        def best_a(g, s, src, mx, eq, ready, k_m, k_e):
            dve.wait_ge(S[ready], g + 1)
            V.tensor_reduce(mx[s], tiles(src[s]), AX.X, ALU.max).then_inc(S[k_m], 1)
            dve.wait_ge(S[k_m], g + 1)
            V.tensor_tensor(tiles(eq[s]), tiles(src[s]), over(mx[s], NE), ALU.is_equal).then_inc(S[k_e], 1)

        def best_b(g, s, eq, pr, pm, oh, k_e, k_p, k_q, k_o):
            dve.wait_ge(S[k_e], g + 1)
            V.tensor_tensor(tiles(pr[s]), tiles(eq[s]), each(K("priority")), ALU.mult).then_inc(S[k_p], 1)
            dve.wait_ge(S[k_p], g + 1)
            V.tensor_reduce(pm[s], tiles(pr[s]), AX.X, ALU.max).then_inc(S[k_q], 1)
            dve.wait_ge(S[k_q], g + 1)
            V.tensor_tensor(tiles(oh[s]), tiles(pr[s]), over(pm[s], NE), ALU.is_equal).then_inc(S[k_o], 1)

        def without_best(g, s):
            dve.wait_ge(S["b1"], g + 1)
            V.scalar_tensor_tensor(l2[s], b1[s], -FAR, lg[s], ALU.mult, ALU.add).then_inc(S["l2"], 1)

        def distance(g, s):
            dve.wait_ge(S["m2"], g + 1)
            V.tensor_tensor(dd[s], m2[s], m1[s], ALU.subtract).then_inc(S["dd"], 1)

        def gates(g, s):
            dve.wait_ge(S["ex"], g + 1)
            V.tensor_scalar(s1[s], ex[s], 1.0, None, ALU.add).then_inc(S["s1"], 1)
            dve.wait_ge(S["s1"], g + 1)
            V.reciprocal(v1[s], s1[s]).then_inc(S["w1"], 1)
            dve.wait_ge(S["w1"], g + 1)
            V.tensor_tensor(v2[s], ex[s], v1[s], ALU.mult).then_inc(S["w2"], 1)
            V.tensor_tensor(tiles(g1[s]), tiles(b1[s]), over(v1[s], NE), ALU.mult).then_inc(S["g1"], 1)
            dve.wait_ge(S["w2"], g + 1)
            dve.wait_ge(S["b2"], g + 1)
            V.tensor_tensor(tiles(g2[s]), tiles(b2[s]), over(v2[s], NE), ALU.mult).then_inc(S["g2"], 1)
            dve.wait_ge(S["g1"], g + 1)
            dve.wait_ge(S["g2"], g + 1)
            V.tensor_tensor(gate[s], g1[s], g2[s], ALU.add).then_inc(S["g"], 1)

        def split_gates(g, s):
            dve.wait_ge(S["g"], g + 1)
            t = gate[s].rearrange("p (t r) -> p t r", t=QT)
            r = gr[s].rearrange("p (t r) -> p t r", t=QT)
            V.tensor_copy(parts(g3[s])[:, :, 0, :], t).then_inc(S["gh"], 1)
            dve.wait_ge(S["gh"], g + 1)
            V.tensor_tensor(r, t, parts(g3[s])[:, :, 0, :], ALU.subtract).then_inc(S["gr"], 1)
            dve.wait_ge(S["gr"], g + 1)
            V.tensor_copy(parts(g3[s])[:, :, 1, :], r).then_inc(S["gm_"], 1)
            dve.wait_ge(S["gm_"], g + 1)
            V.tensor_tensor(parts(g3[s])[:, :, 2, :], r, parts(g3[s])[:, :, 1, :], ALU.subtract).then_inc(S["gl"], 1)

        def start_sum(g, s):
            dve.wait_ge(S["bb"], g + 1)
            dve.wait_ge(S["fat"], past(g - 1))
            V.tensor_tensor(acc[s], ps[:, M2, :], hs[s], ALU.add).then_inc(S["acc"], 1)

        def gated(n, s, e):
            dve.wait_ge(S["y"], n * NE + e + 1)
            dve.wait_ge(S["gbs"], n * NE + e + 1)
            dve.wait_ge(S["add"], n * NE + max(e - 1, 0))
            V.tensor_tensor(tmp[e % 2], ps[:, Y + e % 2, :], gbs[e % 2], ALU.mult).then_inc(S["mul"], 1)

        def norm_a(f, s, src, ready, k_s, k_m, k_x):
            dve.wait_ge(S[ready], f + 1)
            V.tensor_reduce(sm[s], tiles(src), AX.X, ALU.add).then_inc(S[k_s], 1)
            dve.wait_ge(S[k_s], f + 1)
            V.tensor_scalar(mn[s], sm[s], 1.0 / C, None, ALU.mult).then_inc(S[k_m], 1)
            dve.wait_ge(S[k_m], f + 1)
            V.tensor_tensor(tiles(xc[s]), tiles(src), over(mn[s], C), ALU.subtract).then_inc(S[k_x], 1)

        def norm_b(f, s, k_sq, k_v):
            dve.wait_ge(S[k_sq], f + 1)
            V.tensor_reduce(vs[s], tiles(sq[s]), AX.X, ALU.add).then_inc(S[k_v], 1)

        def norm_c(f, s, dst, k_r, k_o):
            dve.wait_ge(S[k_r], f + 1)
            V.tensor_tensor(tiles(dst[s]), tiles(xc[s]), over(rs[s], C), ALU.mult).then_inc(S[k_o], 1)

        def add_tokens(f, s):
            dve.wait_ge(S["ba"], f + 1)
            dve.wait_ge(S["fht"], f + 1)
            V.tensor_tensor(ya[s], ps[:, M2, :], ya[s], ALU.add).then_inc(S["ha"], 1)

        dve.wait_ge(S["w1in"], 32)
        V.tensor_copy(wh[:, :], stage[:, :]).then_inc(S["wh"], 1)
        dve.wait_ge(S["selin"], 16)
        V.tensor_copy(sel[:, :], stage2[0:PARTS * GR, :]).then_inc(S["sel"], 1)
        dve.wait_ge(S["wh"], 1)
        V.tensor_tensor(wl[:, :], stage[:, :], wh[:, :], ALU.subtract).then_inc(S["wl"], 1)
        V.tensor_copy(ident16[:, :], K("ident")).then_inc(S["id16"], 1)
        b2f = W("mo_b2")
        V.tensor_copy(b2p[:, 0, :], b2f).then_inc(S["b2h"], 1)
        dve.wait_ge(S["b2h"], 1)
        V.tensor_tensor(b2r[:, :], b2f, b2p[:, 0, :], ALU.subtract).then_inc(S["b2r"], 1)
        dve.wait_ge(S["b2r"], 1)
        V.tensor_copy(b2p[:, 1, :], b2r[:, :]).then_inc(S["b2m"], 1)
        dve.wait_ge(S["b2m"], 1)
        V.tensor_tensor(b2p[:, 2, :], b2r[:, :], b2p[:, 1, :], ALU.subtract).then_inc(S["b2l"], 1)

        low_parts(0, 0)
        logits(0, 0)
        best_a(0, 0, lg, m1, e1, "lg", "m1", "e1")
        best_b(0, 0, e1, p1, q1, b1, "e1", "p1", "q1", "b1")
        without_best(0, 0)
        best_a(0, 0, l2, m2, e2, "l2", "m2", "e2")
        distance(0, 0)
        best_b(0, 0, e2, p2, q2, b2, "e2", "p2", "q2", "b2")
        gates(0, 0)
        split_gates(0, 0)
        start_sum(0, 0)

        def body(i, s, first=False, last=False):
            n = 2 * i + s
            o = 1 - s
            for e in range(NE):
                gated(n, s, e)
                if not first:
                    if e == 2:
                        norm_a(n - 1, o, ps[:, M1, :], "fat", "sa", "ma", "xa")
                    if e == 4:
                        norm_b(n - 1, o, "sqa", "va")
                    if e == 6:
                        norm_c(n - 1, o, ya, "ra", "na")
                    if e == 9:
                        add_tokens(n - 1, o)
                        norm_a(n - 1, o, ya[o], "ha", "sz", "mz", "xz")
                    if e == 11:
                        norm_b(n - 1, o, "sqz", "vz")
                    if e == 13:
                        dve.wait_ge(S[f"st{o}"], (i - 1 + s) * (16 * 2 * U))
                        norm_c(n - 1, o, yb, "rz", "o")
                if not last:
                    if e == 3:
                        low_parts(n + 1, o)
                    if e == 5:
                        logits(n + 1, o)
                        best_a(n + 1, o, lg, m1, e1, "lg", "m1", "e1")
                    if e == 7:
                        best_b(n + 1, o, e1, p1, q1, b1, "e1", "p1", "q1", "b1")
                    if e == 8:
                        without_best(n + 1, o)
                        best_a(n + 1, o, l2, m2, e2, "l2", "m2", "e2")
                        distance(n + 1, o)
                    if e == 10:
                        best_b(n + 1, o, e2, p2, q2, b2, "e2", "p2", "q2", "b2")
                    if e == 12:
                        gates(n + 1, o)
                    if e == 14:
                        split_gates(n + 1, o)
            if not last:
                start_sum(n + 1, o)

        sweep(dve, body)
        norm_a(NU - 1, 1, ps[:, M1, :], "fat", "sa", "ma", "xa")
        norm_b(NU - 1, 1, "sqa", "va")
        norm_c(NU - 1, 1, ya, "ra", "na")
        add_tokens(NU - 1, 1)
        norm_a(NU - 1, 1, ya[1], "ha", "sz", "mz", "xz")
        norm_b(NU - 1, 1, "sqz", "vz")
        dve.wait_ge(S["st1"], (NU // 2 - 1) * (16 * 2 * U))
        norm_c(NU - 1, 1, yb, "rz", "o")


class Phase(ExitStack):

    def __init__(self, nc):
        super().__init__()
        self.nc, self.held = nc, []

    def semaphore(self, name):
        self.held.append(self.nc.alloc_semaphore(name=name))
        return self.held[-1]

    def done(self):
        self.nc.clear_and_free_semaphores(self.held)
        self.nc.all_engine_barrier()


def program(nc, x, consts, wts, w1, w2, sel, out, kat, wat, debug=None, debug_from=None, hin=None):
    with ExitStack() as ctx:
        def phase(build, *args):
            with Phase(nc) as p:
                build(nc, p, *args)
            p.done()

        kb = ctx.enter_context(nc.sbuf_tensor("consts_sb", [P, consts.shape[1]], F32))
        wb = ctx.enter_context(nc.sbuf_tensor("weights_sb", [P, wts.shape[1]], F32))
        H = ctx.enter_context(nc.sbuf_tensor("tokens", [P, NP * TOK], F32))
        loaded = ctx.enter_context(nc.semaphore("loaded"))
        stored = ctx.enter_context(nc.semaphore("stored"))

        def K(name):
            at, n, rows = kat[name]
            return kb[0:rows, at:at + n]

        def W(name):
            at, n, rows = wat[name]
            return wb[0:rows, at:at + n]

        with nc.Block() as block:
            @block.sync
            def _(sp):
                sp.dma_start(kb[:, :], consts).then_inc(loaded, 16)
                sp.dma_start(wb[:, :], wts).then_inc(loaded, 16)
                sp.wait_ge(loaded, 32)

        psum = ctx.enter_context(nc.psum_tensor("psum", [P, 8, CH], F32))
        if debug in (None, "tok") or debug_from is None:
            phase(tokenizer, x.rearrange("(n two) c h w -> n (two c) (h w)", two=2), K, W, H, psum)
        if debug_from is not None:
            with nc.Block() as block:
                @block.sync
                def _(sp):
                    sp.dma_start(H[:, :], hin).then_inc(stored, 16)
                    sp.wait_ge(stored, 16)
        todo = {"attn": attention, "ffn": routed_ffn, "holo": holographic}
        for name, build in todo.items():
            if debug is None or (list(todo).index(name) <= (list(todo).index(debug) if debug in todo else -1)
                                 and (debug_from is None or name == debug)):
                phase(build, K, W, H, psum)
        if debug in (None, "moe"):
            phase(experts, K, W, H, psum, w1, w2, sel, out)
        elif debug:
            with nc.Block() as block:
                @block.sync
                def _(sp):
                    sp.dma_start(out.rearrange("b t c -> (b t c)").rearrange("(p n) -> p n", p=P), H[:, :]).then_inc(stored, 16)
                    sp.wait_ge(stored, 32 if debug_from is not None else 16)


def kernel(debug=None, hstart=None, **inputs):
    import concourse.bacc as bacc
    from concourse.bass_utils import run_bass_kernel_spmd as run

    nc = bacc.Bacc("TRN2", target_bir_lowering=False, num_devices=1)
    k, w = shape_constants(), weights(inputs)
    k.add("eps", np.full((P, 1), EPS))
    arrays = {"x": np.ascontiguousarray(inputs["x"]), "consts": k.array(), "weights_in": w.array(),
              "experts_up": np.ascontiguousarray(inputs["L1_ffn_w1"]), "experts_down": np.ascontiguousarray(inputs["L1_ffn_w2"]),
              "gate_rows": gate_rows()}
    aps = [nc.dram_tensor(n, a.shape, F32, kind="ExternalInput").ap() for n, a in arrays.items()]
    out = nc.dram_tensor("out", (B, TOK, C), F32, kind="ExternalOutput").ap()
    hin = None
    if hstart is not None:
        arrays["hin"] = hstart
        hin = nc.dram_tensor("hin", hstart.shape, F32, kind="ExternalInput").ap()
    program(nc, *aps, out, k.at, w.at, debug, None if hstart is None else 1, hin)
    r = run(nc, [arrays], core_ids=[0])
    return r.results[0]["out"]
```

```python
from contextlib import ExitStack

import numpy as np
import concourse.bass as bass
from concourse import mybir

F32 = mybir.dt.float32
BF16 = mybir.dt.bfloat16
ALU = mybir.AluOpType
ACT = mybir.ActivationFunctionType
AX = mybir.AxisListType

B, C, IMG = 64, 64, 64
STRIDE, HEADS = 4, 8
HD = C // HEADS
SIDE = IMG // STRIDE
TOK = SIDE * SIDE
PX = STRIDE * STRIDE
PIX = IMG * IMG
P = 128
NP = B // 2
CH = 512
NCH = PIX // CH
CP = CH // PX
EPS = 1e-5


class Pack:

    def __init__(self):
        self.parts, self.at, self.n = [], {}, 0

    def add(self, name, a):
        a = np.asarray(a, np.float32)
        full = np.zeros((P, a.shape[1]), np.float32)
        full[: a.shape[0]] = a
        self.at[name] = (self.n, a.shape[1], a.shape[0])
        self.parts.append(full)
        self.n += a.shape[1]

    def array(self):
        return np.ascontiguousarray(np.concatenate(self.parts, axis=1))


def twice(m):
    m = np.asarray(m, np.float32)
    out = np.zeros((2 * m.shape[0], 2 * m.shape[1]), np.float32)
    out[: m.shape[0], : m.shape[1]] = m
    out[m.shape[0]:, m.shape[1]:] = m
    return out


def column(v):
    v = np.asarray(v, np.float32).reshape(-1, 1)
    return np.concatenate([v, v], axis=0)


def shape_constants():
    k = Pack()
    eye = np.eye(P, dtype=np.float32)
    k.add("ident", eye)
    k.add("centre", twice(np.eye(C) - 1.0 / C))
    k.add("mean", twice(np.full((C, C), 1.0 / C)))
    var_sel = np.zeros((P, 2, 32), np.float32)
    head_sel = np.zeros((P, 2, 32), np.float32)
    spread = np.zeros((P, 2, P), np.float32)
    for a in range(2):
        for img in range(2):
            for h in range(HEADS):
                row = 16 * a + 8 * img + h
                lo = 64 * img + HD * h
                var_sel[64 * img:64 * img + 64, a, row] = 1.0 / C
                head_sel[lo:lo + HD, a, row] = 1.0
                for part in range(PARTS):
                    spread[32 * part + row, a, lo:lo + HD] = 1.0
    k.add("var_sel", var_sel.reshape(P, -1))
    k.add("head_sel", head_sel.reshape(P, -1))
    part, col = np.arange(P)[:, None], np.arange(TOK)[None]
    k.add("earlier", np.concatenate([col < part, col < part + P], axis=1))
    k.add("priority", np.broadcast_to(16.0 - np.arange(16)[None], (P, 16)))
    k.add("causal", part <= col)
    k.add("ones", np.ones((P, TOK)))
    k.add("root", np.broadcast_to(1 / np.sqrt(col + 1.0), (P, TOK)))
    k.add("root32", np.broadcast_to(1 / np.sqrt((col + 1.0) * 32), (P, TOK)))
    cosine = (np.arange(P)[:, None] // 32) % 2 == 0
    k.add("turn_sign", np.where(cosine, -1.0, 1.0))
    k.add("turn_scale", np.where(cosine, -PI, PI))
    k.add("turn_bias", np.where(cosine, PI / 2, 0.0))
    k.add("spread", spread.reshape(P, -1))
    k.add("eps", np.full((P, 1), EPS))
    return k


def gate_rows():
    sel = np.zeros((PARTS, 2, NE, NE, 2, C), np.float32)
    for e in range(NE):
        for img in range(2):
            sel[:, img, e, e, img] = 1.0
    return sel.reshape(PARTS * 2 * NE, NE * P)


def weights(x):
    w = Pack()
    wkv = np.asarray(x["L0_tok_Wkv"])
    w.add("tok_wq", twice(np.asarray(x["L0_tok_Wq"]).T))
    w.add("tok_wk", twice(wkv[:C].T))
    w.add("tok_wv", twice(wkv[C:].T))
    w.add("tok_wp", twice(np.asarray(x["L0_tok_proj_w"]).T))
    w.add("at_wq", twice(np.asarray(x["L0_attn_W_q"]).T))
    kv = [twice(np.asarray(x[n]).T) for n in ("L0_attn_W_k", "L0_attn_W_v")]
    w.add("at_wkv", np.concatenate(kv, axis=1))
    w.add("at_wo", twice(np.asarray(x["L0_attn_W_o"]).T))
    w.add("at_e", np.asarray(x["L0_attn_E_block"]).T)
    w.add("at_f", np.asarray(x["L0_attn_F_block"]).T)
    for name in ("L0_attn_g1", "L0_attn_b1", "L0_attn_g2", "L0_attn_b2"):
        w.add(name, column(x[name]))
    w.add("ff_wr", np.tile(np.broadcast_to(np.asarray(x["L0_ffn_wr"]), (C, P)), (2, 1)))
    w.add("L0_ffn_br", np.broadcast_to(np.asarray(x["L0_ffn_br"]).reshape(1, 1), (P, 1)))
    w.add("ff_w1", np.tile(np.asarray(x["L0_ffn_w1"]), (2, 1)))
    w.add("ff_b1", np.asarray(x["L0_ffn_b1"]).reshape(2, P).T)
    w.add("ff_w2", np.concatenate(np.split(np.asarray(x["L0_ffn_w2"]), 2), axis=1))
    w.add("ff_b2", column(x["L0_ffn_b2"]))

    def features(m):
        m = np.asarray(m)
        return np.concatenate([m, m], axis=1)

    for n in ("k", "q"):
        w.add(f"ho_w{n}1", twice(x[f"L1_attn_W{n}1"]))
        w.add(f"ho_w{n}2", twice(features(x[f"L1_attn_W{n}2"])))
        w.add(f"ho_b{n}2", column(features(np.asarray(x[f"L1_attn_b{n}2"])[None])))
        w.add(f"L1_attn_b{n}1", column(x[f"L1_attn_b{n}1"]))
    w.add("ho_wvp", twice(x["L1_attn_Wvp"]))
    w.add("ho_wvc", twice(x["L1_attn_Wvc"]))
    w.add("ho_bvc", np.broadcast_to(column(x["L1_attn_bvc"]).T, (P, P)))
    w.add("ho_wg1", twice(x["L1_attn_Wg1"]))
    w.add("ho_bg1", column(x["L1_attn_bg1"]))
    for k, n in enumerate("ab"):
        w.add(f"ho_wg2{n}", twice(np.broadcast_to(np.asarray(x["L1_attn_Wg2"])[:, k:k + 1], (C // 4, C))))
        w.add(f"ho_bg2{n}", np.broadcast_to(np.asarray(x["L1_attn_bg2"])[k:k + 1].reshape(1, 1), (P, 1)))
    w.add("ho_phases", np.tile(np.asarray(x["L1_attn_base_phases"])[:TOK].T, (2, 1)))
    w.add("mo_gate", twice(x["L1_ffn_gate_w"]))
    w.add("mo_gate_b", np.broadcast_to(np.asarray(x["L1_ffn_gate_b"])[None], (P, 16)))
    w.add("mo_b1", np.asarray(x["L1_ffn_b1"]).T)
    w.add("mo_b2", np.tile(twice(x["L1_ffn_b2"]), (3, 1)))
    w.add("mo_gamma", np.broadcast_to(np.asarray(x["L1_ffn_gamma"])[None], (P, C)))
    w.add("mo_beta", np.broadcast_to(np.asarray(x["L1_ffn_beta"])[None], (P, C)))
    w.add("ho_wo", twice(x["L1_attn_Wo"]))
    for name in ("L1_attn_bvp", "L1_attn_ln_g", "L1_attn_ln_b", "L1_attn_bo"):
        w.add(name, column(x[name]))
    w.add("L0_attn_scale", np.broadcast_to(np.asarray(x["L0_attn_scale"]).reshape(1, 1), (P, 1)))
    for name in ("L0_tok_ln_q_w", "L0_tok_ln_q_b", "L0_tok_ln_kv_w", "L0_tok_ln_kv_b", "L0_tok_proj_b"):
        w.add(name, column(x[name]))
    return w


class Sems:

    def __init__(self, nc, ctx, phase, names):
        self.s = {n: ctx.semaphore(f"{phase}_{n}") for n in names.split()}

    def __getitem__(self, n):
        return self.s[n]


def past(count):
    return max(count, 0) if isinstance(count, int) else count


PARTS = 3
LAG = 5


def tokenizer(nc, ctx, x, K, W, H, psum):
    NX = 4
    NG = 4

    def sb(name, cols, dt=F32):
        return ctx.enter_context(nc.sbuf_tensor(name, [P, cols], dt))

    def sem(name):
        return ctx.semaphore("tok_" + name)

    xt = sb("tok_x", NX * PIX)
    sq = sb("tok_sq", NCH * CH)
    kq = sb("tok_kq", NCH * CH)
    half = sb("tok_half", PIX // 2)
    quarter = sb("tok_quarter", PIX // 4)
    eighth = half[:, 0:PIX // 8]
    pooled = sb("tok_pooled", 2 * TOK)
    base = sb("tok_base", 2 * TOK)
    qsq, qr, qn, qa = (kq[:, CH + k * TOK:CH + (k + 1) * TOK] for k in range(4))
    qs = sb("tok_qs", 2 * TOK)
    mean2 = sb("tok_mean2", CH)
    rstd = sb("tok_rstd", 2 * CH)
    score = sb("tok_score", CH)
    attn = sb("tok_attn", CH)
    top = sb("tok_top", CP)
    den = sb("tok_den", CP)
    rden = sb("tok_rden", CP)
    part = [sb(f"tok_part{k}", CH, BF16) for k in range(PARTS)]
    stack = sb("tok_stack", 2 * NG * CH, BF16)
    spread = sb("tok_spread", 2 * P, BF16)
    wide = sb("tok_wide", 3 * CH)
    zp = sb("tok_zp", 3 * CH)
    z = sb("tok_z", TOK)
    wkc = sb("tok_wkc", P)
    wvc = sb("tok_wvc", P)
    wks, wvs = kq[:, 0:P], kq[:, P:2 * P]
    small = sb("tok_small", 4)
    lnq16, bv, pbz = small[:, 0:1], small[:, 1:2], small[:, 2:3]

    ps = psum
    KEY, VALUE, WIDE = (2, 3), (0, 1), (6, 7)
    VAR, SCORE = 4, 5
    QUERY, MEAN, PROJ = 3, 2, 0

    x_in = [sem(f"x_in{s}") for s in range(NX)]
    moved = [sem("moved_hi"), sem("moved_mid")]
    moved_lo = [sem(f"moved_lo{g}") for g in range(NG)]
    names = ("prep_dve prep_pe prep_act prep2_pe prep2_act half quarter eighth pooled sq mean mean2 varq low0 var rstd qc qsq qv qr qn qa qq qs base "
             "kx kq scored s1 top shifted exp den rden er attn hi rest mid lo wide_mm wide vx zmul zred pj tok")
    S = Sems(nc, ctx, "tok", names)

    def mm(out, lhsT, rhs, start=True, stop=True, **kw):
        return nc.tensor.matmul(out, lhsT, rhs, start=start, stop=stop, **kw)

    def pixel_mm(out, lhsT, slot, c):
        n = STRIDE * IMG
        for k in range(CH // n):
            at = slot * PIX + c * CH + k * n
            v = xt[:, at:at + n].rearrange("p (i w j) -> p w i j", i=STRIDE, w=SIDE, j=STRIDE)
            last = mm(out[:, k * n:(k + 1) * n], lhsT, v)
        return last

    def by_patch(v, k):
        n = STRIDE * IMG
        return v[:, k * n:(k + 1) * n].rearrange("p (i w j) -> p w i j", i=STRIDE, w=SIDE, j=STRIDE)

    def patches(v):
        return v.rearrange("p (a b) -> p a b", b=PX)

    def over_pixels(v, n):
        return v.unsqueeze(2).broadcast_to([P, n, PX])

    def steps(eng, step):
        for s in range(NX):
            step(0, s, NX)
        with eng.Fori(1, NP // NX - 1) as i:
            for s in range(NX):
                step(i, s, NX)
        for s in range(NX):
            step(NP // NX - 1, s, NX - 1 - s)

    block = ctx.enter_context(nc.Block())

    @block.sync
    def _(sp):
        for s in range(NX):
            sp.dma_start(xt[:, s * PIX:(s + 1) * PIX], x[s]).then_inc(x_in[s], 16)

        def stack_parts(i, s):
            n = i * NX + s
            for k, name in enumerate(("hi", "mid", "lo")):
                sp.wait_ge(S[name], n + 1)
                for g in range(NG):
                    at = ((s % 2) * NG + g) * CH
                    sp.dma_start(stack[32 * k:32 * k + 32, at:at + CH], part[k][32 * g:32 * g + 32, :])\
                      .then_inc(moved[k] if k < PARTS - 1 else moved_lo[g], 16)

        def reload(i, s):
            sp.wait_ge(S["vx"], i * (NX * NCH) + (NCH * s + NCH))
            sp.dma_start(xt[:, s * PIX:(s + 1) * PIX], x[i * NX + (NX + s)]).then_inc(x_in[s], 16)

        for s in range(NX):
            stack_parts(0, s)
            if s:
                reload(0, s - 1)
        with sp.Fori(1, NP // NX - 1) as i:
            for s in range(NX):
                stack_parts(i, s)
                if s:
                    reload(i, s - 1)
                else:
                    reload(i - 1, NX - 1)
        stack_parts(NP // NX - 1, 0)
        reload(NP // NX - 2, NX - 1)
        for s in range(1, NX):
            stack_parts(NP // NX - 1, s)

    @block.gpsimd
    def _(pool):
        def pool_pair(n, s, x_loads):
            pool.wait_ge(x_in[s], x_loads)
            pool.wait_ge(S["base"], past(n - 1))
            pool.wait_ge(S["qc"], past(n - 1))
            pool.wait_ge(S["pooled"], n)
            v = xt[:, s * PIX:(s + 1) * PIX].rearrange("p (h i w) -> p h i w", i=STRIDE, w=IMG)
            h = half[:, :].rearrange("p (h i w) -> p h i w", i=2, w=IMG)
            nc.gpsimd.tensor_tensor(h, v[:, :, 0:2], v[:, :, 2:4], ALU.add).then_inc(S["half"], 1)
            pool.wait_ge(S["half"], n + 1)
            q = quarter[:, :].rearrange("p (h w) -> p h w", w=IMG)
            nc.gpsimd.tensor_tensor(q, h[:, :, 0], h[:, :, 1], ALU.add).then_inc(S["quarter"], 1)
            pool.wait_ge(S["quarter"], n + 1)
            q = quarter[:, :].rearrange("p (t j) -> p t j", j=4)
            e = eighth[:, :].rearrange("p (t j) -> p t j", j=2)
            nc.gpsimd.tensor_tensor(e, q[:, :, 0:2], q[:, :, 2:4], ALU.add).then_inc(S["eighth"], 1)
            pool.wait_ge(S["eighth"], n + 1)
            o = pooled[:, (s % 2) * TOK:(s % 2 + 1) * TOK]
            nc.gpsimd.tensor_tensor(o, e[:, :, 0], e[:, :, 1], ALU.add).then_inc(S["pooled"], 1)

        def weights_of(n, s):
            pool.wait_ge(S["exp"], n + 1)
            pool.wait_ge(S["rstd"], n + 1)
            pool.wait_ge(S["lo"], n)
            nc.gpsimd.tensor_tensor(attn[:, :], score[:, :], rstd[:, (s % 2) * CH:(s % 2 + 1) * CH], ALU.mult).then_inc(S["er"], 1)
            pool.wait_ge(S["attn"], n + 1)
            nc.gpsimd.tensor_tensor(attn[:, :], attn[:, :], part[0][:, :], ALU.subtract).then_inc(S["rest"], 1)
            pool.wait_ge(S["mid"], n + 1)
            pool.wait_ge(S["rest"], n + 1)
            for g in range(NG):
                pool.wait_ge(moved_lo[g], n * 16)
            nc.gpsimd.tensor_tensor(part[2][:, :], attn[:, :], part[1][:, :], ALU.subtract).then_inc(S["lo"], 1)

        for s in range(2):
            pool_pair(s, s, 16)
        weights_of(0, 0)
        pool_pair(2, 2, 16)

        def step(i, s, ahead):
            n = i * NX + s
            if ahead > 0:
                weights_of(n + 1, (s + 1) % NX)
            if ahead > 2:
                pool_pair(n + 3, (s + 3) % NX, 16 * i + 16 * ((s + 3) // NX + 1))

        steps(pool, step)

    @block.tensor
    def _(pe):
        pe.wait_ge(S["prep_dve"], 4)
        mm(ps[:, 0, 0:P], K("centre"), wks[:, :])
        mm(ps[:, 0, P:2 * P], K("centre"), wvs[:, :])
        mm(ps[:, 1, 0:1], W("tok_wv"), W("L0_tok_ln_kv_b")).then_inc(S["prep_pe"], 1)
        pe.wait_ge(S["prep_act"], 3)
        mm(ps[:, 1, 1:2], W("tok_wp"), bv).then_inc(S["prep2_pe"], 1)
        pe.wait_ge(S["prep2_act"], 1)

        def mean_mm(m, s, c0):
            for c in range(c0, c0 + 4):
                g, at = c % 4, s * PIX + c * CH
                last = mm(ps[32 * g:32 * g + 32, MEAN, :], K("var_sel")[:, 32 * (c // 4):32 * (c // 4) + 32], xt[:, at:at + CH],
                          start=(c < 4), stop=(c >= 4))
            if c0:
                last.then_inc(S["mean"], 1)

        def var_mm(m, c0):
            pe.wait_ge(S["sq"], m * (NCH // 2) + (c0 + 4) // 2)
            if c0 == 0:
                pe.wait_ge(S["varq"], m)
            for c in range(c0, c0 + 4):
                g = c % 4
                last = mm(ps[32 * g:32 * g + 32, VAR, :], K("var_sel")[:, 32 * (c // 4):32 * (c // 4) + 32], sq[:, c * CH:(c + 1) * CH],
                          start=(c < 4), stop=(c >= 4))
            if c0:
                last.then_inc(S["var"], 1)

        def score_mm(m, c0):
            pe.wait_ge(S["kq"], m * NCH + c0 + 4)
            if c0 == 0:
                pe.wait_ge(S["s1"], m)
            for c in range(c0, c0 + 4):
                g = c % 4
                last = mm(ps[32 * g:32 * g + 32, SCORE, :], K("head_sel")[:, 32 * (c // 4):32 * (c // 4) + 32], kq[:, c * CH:(c + 1) * CH],
                          start=(c < 4), stop=(c >= 4))
            if c0:
                last.then_inc(S["scored"], 1)

        def project(n):
            pe.wait_ge(S["zred"], n * NCH + NCH)
            mm(ps[:, PROJ, 0:TOK], W("tok_wp"), z[:, :]).then_inc(S["pj"], 1)

        def key(m, s, c):
            if c == 0:
                pe.wait_ge(S["mean2"], m + 1)
            elif c == 1:
                pe.wait_ge(S["qs"], m + 1)
            else:
                pe.wait_ge(S["kq"], m * NCH + c - 1)
            pixel_mm(ps[:, KEY[c % 2], :], wkc[:, :], s, c).then_inc(S["kx"], 1)
            if c == 0:
                pe.wait_ge(S["qa"], m + 1)
                mm(ps[:, QUERY, TOK:2 * TOK], W("tok_wq"), qa[:, :]).then_inc(S["qq"], 1)
            if c == 5:
                score_mm(m, 0)

        def value(n, s, c):
            if c == 0:
                for k in range(PARTS - 1):
                    pe.wait_ge(moved[k], n * (16 * NG) + (16 * NG))
            if c < NG:
                pe.wait_ge(moved_lo[c], n * 16 + 16)
            if c < 2:
                pe.wait_ge(S["wide"], n * NCH)
            else:
                pe.wait_ge(S["wide"], n * NCH + c - 1)
            R = 32 * PARTS
            at = ((s % 2) * NG + c % NG) * CH
            mm(ps[:, WIDE[c % 2], :], spread[0:R, (c // NG) * P:(c // NG + 1) * P], stack[0:R, at:at + CH]).then_inc(S["wide_mm"], 1)
            if c == 0:
                pe.wait_ge(S["tok"], n)
            elif c == 1:
                pe.wait_ge(S["zmul"], n * NCH)
            else:
                pe.wait_ge(S["zmul"], n * NCH + c - 1)
            pixel_mm(ps[:, VALUE[c % 2], :], wvc[:, :], s, c).then_inc(S["vx"], 1)

        def ahead_of(a, s, x_loads, c):
            if c == 0:
                pe.wait_ge(x_in[s], x_loads)
                mean_mm(a, s, 0)
            elif c == 1:
                mean_mm(a, s, 4)
                pe.wait_ge(S["pooled"], a + 1)
                mm(ps[:, QUERY, 0:TOK], K("centre"), pooled[:, (s % 2) * TOK:(s % 2 + 1) * TOK]).then_inc(S["qc"], 1)
            elif c == 2:
                var_mm(a, 0)
                pe.wait_ge(S["qsq"], a + 1)
                mm(ps[:, QUERY, TOK:2 * TOK], K("mean"), qsq[:, :]).then_inc(S["qv"], 1)
            elif c == 3:
                var_mm(a, 4)

        for c in range(NCH):
            ahead_of(0, 0, 16, c)
        for c in range(NCH):
            key(0, 0, c)
        score_mm(0, 4)
        for c in range(NCH):
            ahead_of(1, 1, 16, c)

        def step(i, s, ahead):
            n = i * NX + s
            if ahead > 0:
                for c in range(NCH):
                    key(n + 1, (s + 1) % NX, c)
                    if c == 1 and not (isinstance(n, int) and n == 0):
                        project(n - 1)
                    if c >= LAG:
                        value(n, s, c - LAG)
                score_mm(n + 1, 4)
            else:
                project(n - 1)
                for c in range(NCH - LAG):
                    value(n, s, c)
            for c in range(LAG):
                value(n, s, NCH - LAG + c)
                if ahead > 1:
                    ahead_of(n + 2, (s + 2) % NX, i * 16 + 16 * ((s + 2) // NX + 1), c)

        steps(pe, step)
        project(NP - 1)

    @block.scalar
    def _(act):
        A = nc.scalar.activation
        act.wait_ge(S["prep_pe"], 1)
        A(wkc[:, :], ps[:, 0, 0:P], ACT.Copy).then_inc(S["prep_act"], 1)
        A(wvc[:, :], ps[:, 0, P:2 * P], ACT.Copy).then_inc(S["prep_act"], 1)
        A(bv, ps[:, 1, 0:1], ACT.Copy).then_inc(S["prep_act"], 1)
        act.wait_ge(S["prep2_pe"], 1)
        A(pbz, ps[:, 1, 1:2], ACT.Identity, bias=W("L0_tok_proj_b")).then_inc(S["prep2_act"], 1)
        act.wait_ge(S["prep2_act"], 1)
        act.wait_ge(S["prep_dve"], 4)

        def squares(a, s, x_loads):
            act.wait_ge(x_in[s], x_loads)
            act.wait_ge(S["var"], a)
            for c in range(0, NCH, 2):
                at = s * PIX + c * CH
                A(sq[:, c * CH:(c + 2) * CH], xt[:, at:at + 2 * CH], ACT.Square).then_inc(S["sq"], 1)

        def middle_part(m):
            act.wait_ge(S["rest"], m + 1)
            act.wait_ge(moved[1], m * (16 * NG))
            A(part[1][:, :], attn[:, :], ACT.Copy).then_inc(S["mid"], 1)

        def exp_pair(m):
            act.wait_ge(S["shifted"], m + 1)
            A(score[:, :], score[:, :], ACT.Exp).then_inc(S["exp"], 1)

        def rstd_of(m, s):
            r = rstd[:, (s % 2) * CH:(s % 2 + 1) * CH]
            act.wait_ge(S["varq"], m + 1)
            A(r, r, ACT.Relu).then_inc(S["low0"], 1)
            act.wait_ge(S["low0"], m + 1)
            A(r, r, ACT.Abs_reciprocal_sqrt, bias=K("eps")).then_inc(S["rstd"], 1)

        def base_of(m, s):
            act.wait_ge(S["pooled"], m + 1)
            act.wait_ge(S["tok"], past(m - 1))
            A(base[:, (s % 2) * TOK:(s % 2 + 1) * TOK], pooled[:, (s % 2) * TOK:(s % 2 + 1) * TOK], ACT.Identity,
              bias=pbz, scale=1.0 / PX).then_inc(S["base"], 1)

        def spread_weights(n, c):
            act.wait_ge(S["wide_mm"], n * NCH + c + 1)
            act.wait_ge(S["zmul"], past(n * NCH + c - 2))
            A(wide[:, (c % 3) * CH:(c % 3 + 1) * CH], ps[:, WIDE[c % 2], :], ACT.Copy).then_inc(S["wide"], 1)

        def ahead_of(a, s, c):
            if c == 1:
                act.wait_ge(S["qc"], a + 1)
                act.wait_ge(S["qv"], a)
                A(qsq[:, :], ps[:, QUERY, 0:TOK], ACT.Square, scale=1.0 / PX).then_inc(S["qsq"], 1)
            elif c == 3:
                act.wait_ge(S["qv"], a + 1)
                act.wait_ge(S["qn"], a)
                A(qr[:, :], ps[:, QUERY, TOK:2 * TOK], ACT.Abs_reciprocal_sqrt, bias=K("eps")).then_inc(S["qr"], 1)
                act.wait_ge(S["mean"], a + 1)
                act.wait_ge(S["varq"], a)
                A(mean2[:, :], ps[:, MEAN, :], ACT.Square).then_inc(S["mean2"], 1)
            elif c == 4:
                act.wait_ge(S["qn"], a + 1)
                act.wait_ge(S["qq"], a)
                A(qa[:, :], qn[:, :], ACT.Identity, bias=W("L0_tok_ln_q_b"), scale=lnq16).then_inc(S["qa"], 1)
                act.wait_ge(S["qq"], a + 1)
                act.wait_ge(S["kq"], past((a - 1) * NCH))
                A(qs[:, (s % 2) * TOK:(s % 2 + 1) * TOK], ps[:, QUERY, TOK:2 * TOK], ACT.Copy, scale=float(C) ** -0.5).then_inc(S["qs"], 1)

        squares(0, 0, 16)
        for c in range(NCH):
            ahead_of(0, 0, c)
        squares(1, 1, 16)
        rstd_of(0, 0)
        base_of(0, 0)
        exp_pair(0)
        for c in range(NCH):
            ahead_of(1, 1, c)
        middle_part(0)

        def step(i, s, ahead):
            n = i * NX + s
            if ahead > 1:
                squares(n + 2, (s + 2) % NX, i * 16 + 16 * ((s + 2) // NX + 1))
            if ahead > 0:
                rstd_of(n + 1, (s + 1) % NX)
            for c in range(NCH - LAG):
                spread_weights(n, c)
            for c in range(LAG):
                spread_weights(n, NCH - LAG + c)
                if c == 2 and ahead > 0:
                    exp_pair(n + 1)
                if ahead > 1:
                    ahead_of(n + 2, (s + 2) % NX, c)
            if ahead > 0:
                middle_part(n + 1)
                base_of(n + 1, (s + 1) % NX)

        steps(act, step)

    @block.vector
    def _(dve):
        V = nc.vector
        V.tensor_scalar(wks[:, :], W("tok_wk"), W("L0_tok_ln_kv_w"), None, ALU.mult).then_inc(S["prep_dve"], 1)
        V.tensor_scalar(wvs[:, :], W("tok_wv"), W("L0_tok_ln_kv_w"), None, ALU.mult).then_inc(S["prep_dve"], 1)
        V.tensor_scalar(lnq16, W("L0_tok_ln_q_w"), 1.0 / PX, None, ALU.mult).then_inc(S["prep_dve"], 1)
        V.tensor_copy(spread[:, :], K("spread")).then_inc(S["prep_dve"], 1)

        def query_norm(m):
            dve.wait_ge(S["qr"], m + 1)
            dve.wait_ge(S["qa"], m)
            V.tensor_tensor(qn[:, :], ps[:, QUERY, 0:TOK], qr[:, :], ALU.mult).then_inc(S["qn"], 1)

        def key(m, s, c):
            if c == 0:
                dve.wait_ge(S["qs"], m + 1)
                dve.wait_ge(S["scored"], m)
            dve.wait_ge(S["kx"], m * NCH + c + 1)
            at = (s % 2) * TOK + c * CP
            V.tensor_tensor(patches(kq[:, c * CH:(c + 1) * CH]), patches(ps[:, KEY[c % 2], :]),
                            over_pixels(qs[:, at:at + CP], CP), ALU.mult).then_inc(S["kq"], 1)

        def reduce(n, c):
            dve.wait_ge(S["zmul"], n * NCH + c + 1)
            if c == 0:
                dve.wait_ge(S["pj"], n)
            V.tensor_reduce(z[:, c * CP:(c + 1) * CP], patches(zp[:, (c % 3) * CH:(c % 3 + 1) * CH]), AX.X, ALU.add).then_inc(S["zred"], 1)

        def value(n, c):
            dve.wait_ge(S["vx"], n * NCH + c + 1)
            dve.wait_ge(S["wide"], n * NCH + c + 1)
            dve.wait_ge(S["zred"], past(n * NCH + c - 2))
            V.tensor_tensor(zp[:, (c % 3) * CH:(c % 3 + 1) * CH], ps[:, VALUE[c % 2], :],
                            wide[:, (c % 3) * CH:(c % 3 + 1) * CH], ALU.mult).then_inc(S["zmul"], 1)
            if c:
                reduce(n, c - 1)

        def token(n, i, s):
            dve.wait_ge(S["pj"], n + 1)
            dve.wait_ge(S["base"], n + 1)
            p = s % 2
            V.tensor_tensor(H[:, bass.ds(i * (NX * TOK) + s * TOK, TOK)], ps[:, PROJ, 0:TOK], base[:, p * TOK:(p + 1) * TOK], ALU.add)\
                .then_inc(S["tok"], 1)

        def softmax(m, s, c):
            if c == 0:
                dve.wait_ge(S["scored"], m + 1)
                dve.wait_ge(S["rstd"], m + 1)
                dve.wait_ge(S["er"], m)
                dve.wait_ge(S["den"], m)
                V.tensor_tensor(score[:, :], ps[:, SCORE, :], rstd[:, (s % 2) * CH:(s % 2 + 1) * CH], ALU.mult).then_inc(S["s1"], 1)
            elif c == 1:
                dve.wait_ge(S["s1"], m + 1)
                V.tensor_reduce(top[:, :], patches(score[:, :]), AX.X, ALU.max).then_inc(S["top"], 1)
            elif c == 2:
                dve.wait_ge(S["top"], m + 1)
                V.tensor_tensor(patches(score[:, :]), patches(score[:, :]), over_pixels(top[:, :], CP), ALU.subtract).then_inc(S["shifted"], 1)
            elif c == 3:
                dve.wait_ge(S["exp"], m + 1)
                V.tensor_reduce(den[:, :], patches(score[:, :]), AX.X, ALU.add).then_inc(S["den"], 1)
                dve.wait_ge(S["den"], m + 1)
                dve.wait_ge(S["attn"], m)
                V.reciprocal(rden[:, :], den[:, :]).then_inc(S["rden"], 1)
            elif c == 4:
                dve.wait_ge(S["er"], m + 1)
                dve.wait_ge(S["rden"], m + 1)
                dve.wait_ge(moved[0], m * (16 * NG))
                V.tensor_tensor(patches(part[0][:, :]), patches(attn[:, :]), over_pixels(rden[:, :], CP), ALU.mult).then_inc(S["hi"], 1)
                dve.wait_ge(S["hi"], m + 1)
                V.tensor_tensor(patches(attn[:, :]), patches(attn[:, :]), over_pixels(rden[:, :], CP), ALU.mult).then_inc(S["attn"], 1)

        def ahead_of(a, s, c):
            if c == 3:
                query_norm(a)

        def variance(a, s):
            dve.wait_ge(S["var"], a + 1)
            dve.wait_ge(S["mean2"], a + 1)
            dve.wait_ge(S["er"], past(a - 1))
            dve.wait_ge(S["s1"], past(a - 1))
            n = STRIDE * IMG
            for k in range(CH // n):
                at = (s % 2) * CH + k * n
                v = rstd[:, at:at + n].rearrange("p (w i j) -> p w i j", i=STRIDE, w=SIDE, j=STRIDE)
                last = V.tensor_tensor(v, by_patch(ps[:, VAR, :], k), by_patch(mean2[:, :], k), ALU.subtract)
            last.then_inc(S["varq"], 1)

        for c in range(NCH):
            ahead_of(0, 0, c)
        for c in range(NCH):
            key(0, 0, c)
            if c == 1:
                variance(0, 0)
        for c in range(NCH):
            softmax(0, 0, c)
            ahead_of(1, 1, c)

        def step(i, s, ahead):
            n = i * NX + s
            for c in range(NCH):
                if ahead > 0:
                    key(n + 1, (s + 1) % NX, c)
                    if c == 1:
                        variance(n + 1, (s + 1) % NX)
                if c == 3 and not (isinstance(n, int) and n == 0):
                    token(n - 1, i, s - 1)
                if c >= LAG:
                    value(n, c - LAG)
            for c in range(LAG):
                if ahead > 0:
                    softmax(n + 1, (s + 1) % NX, c)
                value(n, NCH - LAG + c)
                if ahead > 1:
                    ahead_of(n + 2, (s + 2) % NX, c)
            if ahead > 0:
                softmax(n + 1, (s + 1) % NX, LAG)
            reduce(n, NCH - 1)

        steps(dve, step)
        token(NP - 1, NP // NX - 1, NX - 1)


U = 1
UT = U * TOK
NU = NP // U
SLOTS = 4
QT = UT // P
NT = 2 * QT


def rounds(eng, steps, lag, stage):
    def turn(i):
        for k in range(steps):
            for s in range(SLOTS):
                behind = lag if s >= SLOTS // 2 else 0
                if k >= behind:
                    stage(k - behind, i, s)
                elif not (isinstance(i, int) and i == 0):
                    stage(k - behind + steps, i - 1, s)

    turn(0)
    turn(1)
    with eng.Fori(2, NU // SLOTS) as i:
        turn(i)
    for k in range(steps - lag, steps):
        for s in range(SLOTS // 2, SLOTS):
            stage(k, NU // SLOTS - 1, s)


def area(ps, s, b):
    return ps[:, 2 * s + b % 2, UT * (b // 2):UT * (b // 2) + UT]


def areas(ps, s, b):
    return ps[:, 2 * s:2 * s + 2, UT * (b // 2):UT * (b // 2) + UT]


class Norm:
    PARTS = "c sq v r x"

    def __init__(self, nc, S, K, name, ps, mean_bank, var_bank, sq, r):
        self.nc, self.S, self.K, self.name, self.ps = nc, S, K, name, ps
        self.mb, self.vb, self.sq, self.r = mean_bank, var_bank, sq, r

    @staticmethod
    def names(*norms):
        return " ".join(f"{n}_{p}" for n in norms for p in Norm.PARTS.split())

    def centre(self, src, s):
        self.nc.tensor.matmul(area(self.ps, s, self.mb), self.K("centre"), src, start=True, stop=True)\
            .then_inc(self.S[self.name + "_c"], 1)

    def square(self, act, n, s):
        act.wait_ge(self.S[self.name + "_c"], n + 1)
        self.nc.scalar.activation(self.sq[s], area(self.ps, s, self.mb), ACT.Square).then_inc(self.S[self.name + "_sq"], 1)

    def variance(self, pe, n, s):
        pe.wait_ge(self.S[self.name + "_sq"], n + 1)
        self.nc.tensor.matmul(area(self.ps, s, self.vb), self.K("mean"), self.sq[s], start=True, stop=True)\
            .then_inc(self.S[self.name + "_v"], 1)

    def rstd(self, act, n, s):
        act.wait_ge(self.S[self.name + "_v"], n + 1)
        self.nc.scalar.activation(self.r[s], area(self.ps, s, self.vb), ACT.Abs_reciprocal_sqrt, bias=self.K("eps"))\
            .then_inc(self.S[self.name + "_r"], 1)

    def scale(self, dve, n, s, out):
        dve.wait_ge(self.S[self.name + "_r"], n + 1)
        self.nc.vector.tensor_tensor(out, area(self.ps, s, self.mb), self.r[s], ALU.mult).then_inc(self.S[self.name + "_x"], 1)


def attention(nc, ctx, K, W, H, psum):
    NB = TOK // 128
    BK = 64
    STEPS, BEHIND = 21, 12
    S = Sems(nc, ctx, "at", "sp0 sp1 sp2 sp3 sp4 sp5 sp6 "
             + Norm.names("n1", "n2", "n3") +
             " tn kv qsq qv qm qr qn ksq kss ksm kr kn v kpvp kpt vp sc mx sh ex den rden w wt wts ao aos wo o1 hb o3")

    def sb(name, cols):
        t = ctx.enter_context(nc.sbuf_tensor("at_" + name, [P, SLOTS, cols], F32))
        return [t[:, s, :] for s in range(SLOTS)]

    sq, r, xn, tn = sb("sq", UT), sb("r", UT), sb("xn", UT), sb("tn", UT)
    qm, qr, qn = sb("qm", UT), sb("qr", UT), sb("qn", UT)
    ksq, kn, v = sb("ksq", UT), sb("kn", UT), sb("v", UT)
    kss, ksm, kr = sb("kss", NT), sb("ksm", NT), sb("kr", NT)
    kpt, vp = sb("kpt", U * P), sb("vp", U * P)
    sh, ex, wts = sb("sh", NT * P), sb("ex", NT * P), sb("wts", NT * P)
    mx, den, rden = sb("mx", NT), sb("den", NT), sb("rden", NT)
    ao, o1, hb, o3 = sb("ao", UT), sb("o1", UT), sb("hb", UT), sb("o3", UT)
    sp_ = ctx.enter_context(nc.sbuf_tensor("at_softplus", [P, 8], F32))
    neg, low, el, onep, ln1, pos, sc = (sp_[:, k:k + 1] for k in range(7))
    ps = psum
    n1 = Norm(nc, S, K, "n1", ps, 0, 1, sq, r)
    n2 = Norm(nc, S, K, "n2", ps, 0, 1, sq, r)
    n3 = Norm(nc, S, K, "n3", ps, 2, 3, sq, r)

    def h(i, s):
        return H[:, bass.ds(i * (SLOTS * UT) + s * UT, UT)]

    def kv(s):
        return areas(ps, s, 2).rearrange("p t (m c) -> p t m c", m=2)

    def tiles(v, n=NT):
        return v.rearrange("p (t k) -> p t k", t=n)

    def over(v, k):
        return v.unsqueeze(2).broadcast_to([P, v.shape[1], k])

    def halves(v):
        return v.rearrange("p (m k) -> p m k", m=2)

    def scores(s):
        return areas(ps, s, 2).rearrange("p m (t k) -> p m t k", k=P)

    block = ctx.enter_context(nc.Block())

    @block.tensor
    def _(pe):
        mm = nc.tensor.matmul

        def stage(step, i, s):
            if step == 0:
                pe.wait_ge(S["n3_x"], past(SLOTS * i + s - (SLOTS - 1)))
                n1.centre(h(i, s), s)
            if step == 1:
                n1.variance(pe, SLOTS * i + s, s)
            if step == 3:
                pe.wait_ge(S["tn"], SLOTS * i + s + 1)
                mm(area(ps, s, 0), W("at_wq"), tn[s], start=True, stop=True)
                for t in range(QT):
                    m = mm(area(ps, s, 2 + t), tn[s][:, P * t:P * t + P], W("at_wkv"), start=True, stop=True)
                m.then_inc(S["kv"], 1)
            if step == 4:
                pe.wait_ge(S["qsq"], SLOTS * i + s + 1)
                pe.wait_ge(S["v"], SLOTS * i + s + 1)
                mm(area(ps, s, 1), K("mean"), sq[s], start=True, stop=True).then_inc(S["qv"], 1)
            if step == 6:
                pe.wait_ge(S["kn"], SLOTS * i + s + 1)
                pe.wait_ge(S["v"], SLOTS * i + s + 1)
                pe.wait_ge(S["qn"], SLOTS * i + s + 1)
                for j in range(U):
                    for t in range(NB):
                        c = P * (NB * j + t)
                        mm(area(ps, s, 0)[:, P * j + BK * t:P * j + BK * t + BK], kn[s][:, c:c + P], W("at_e"), start=True, stop=True)
                        m = mm(area(ps, s, 0)[BK * t:BK * t + BK, P * (U + j):P * (U + j) + P], W("at_f"), v[s][:, c:c + P], start=True, stop=True)
                m.then_inc(S["kpvp"], 1)
            if step == 7:
                pe.wait_ge(S["kpt"], SLOTS * i + s + 1)
                pe.wait_ge(S["vp"], SLOTS * i + s + 1)
                for j in range(U):
                    for img in range(2):
                        lo = 64 * img
                        for t in range(NB):
                            k = j * NB + t
                            m = mm(area(ps, s, 2 + img)[:, P * k:P * k + P], qn[s][lo:lo + 64, P * (NB * j + t):P * (NB * j + t) + P],
                                   kpt[s][lo:lo + 64, P * j:P * j + P], start=True, stop=True)
                m.then_inc(S["sc"], 1)
            if step == 11:
                pe.wait_ge(S["w"], SLOTS * i + s + 1)
                pe.wait_ge(S["vp"], SLOTS * i + s + 1)
                for k in range(NT):
                    m = nc.tensor.transpose(area(ps, s, k // QT)[:, P * (k % QT):P * (k % QT) + P], ex[s][:, P * k:P * k + P], K("ident"))
                m.then_inc(S["wt"], 1)
            if step == 12:
                pe.wait_ge(S["wts"], SLOTS * i + s + 1)
                for j in range(U):
                    for img in range(2):
                        k = (img * U + j) * TOK
                        m = mm(area(ps, s, 2)[64 * img:64 * img + 64, TOK * j:TOK * j + TOK], vp[s][:, P * j + 64 * img:P * j + 64 * img + 64],
                               wts[s][:, k:k + TOK], start=True, stop=True)
                m.then_inc(S["ao"], 1)
            if step == 13:
                pe.wait_ge(S["aos"], SLOTS * i + s + 1)
                mm(area(ps, s, 3), W("at_wo"), ao[s], start=True, stop=True).then_inc(S["wo"], 1)
            if step == 14:
                pe.wait_ge(S["o1"], SLOTS * i + s + 1)
                n2.centre(o1[s], s)
            if step == 15:
                n2.variance(pe, SLOTS * i + s, s)
            if step == 17:
                pe.wait_ge(S["o3"], SLOTS * i + s + 1)
                n3.centre(o3[s], s)
            if step == 18:
                n3.variance(pe, SLOTS * i + s, s)

        rounds(pe, STEPS, BEHIND, stage)

    @block.scalar
    def _(act):
        A = nc.scalar.activation
        act.wait_ge(S["sp1"], 1)
        A(el, low, ACT.Exp).then_inc(S["sp2"], 1)
        act.wait_ge(S["sp3"], 1)
        A(ln1, onep, ACT.Ln).then_inc(S["sp4"], 1)
        act.wait_ge(S["sp6"], 1)

        def stage(step, i, s):
            if step == 0:
                n1.square(act, SLOTS * i + s, s)
            if step == 1:
                n1.rstd(act, SLOTS * i + s, s)
            if step == 2:
                act.wait_ge(S["n1_x"], SLOTS * i + s + 1)
                A(tn[s], xn[s], ACT.Identity, bias=W("L0_attn_b1"), scale=W("L0_attn_g1")).then_inc(S["tn"], 1)
            if step == 3:
                act.wait_ge(S["kv"], SLOTS * i + s + 1)
                A(sq[s], area(ps, s, 0), ACT.Square).then_inc(S["qsq"], 1)
                A(tiles(ksq[s], QT), kv(s)[:, :, 0, :], ACT.Square).then_inc(S["ksq"], 1)
                A(tiles(v[s], QT), kv(s)[:, :, 1, :], ACT.Copy).then_inc(S["v"], 1)
            if step == 4:
                act.wait_ge(S["qm"], SLOTS * i + s + 1)
                A(qr[s], qm[s], ACT.Abs_reciprocal_sqrt).then_inc(S["qr"], 1)
                act.wait_ge(S["ksm"], SLOTS * i + s + 1)
                A(kr[s], ksm[s], ACT.Abs_reciprocal_sqrt).then_inc(S["kr"], 1)
            if step == 6:
                act.wait_ge(S["kpvp"], SLOTS * i + s + 1)
                A(kpt[s], area(ps, s, 0)[:, 0:U * P], ACT.Copy).then_inc(S["kpt"], 1)
                A(vp[s], area(ps, s, 0)[:, U * P:2 * U * P], ACT.Copy).then_inc(S["vp"], 1)
            if step == 7:
                act.wait_ge(S["o3"], past(SLOTS * i + s - (SLOTS - 1)))
                A(hb[s], h(i, s), ACT.Identity, bias=W("L0_attn_b2")).then_inc(S["hb"], 1)
            if step == 8:
                act.wait_ge(S["sh"], SLOTS * i + s + 1)
                A(sh[s], sh[s], ACT.Exp, scale=sc).then_inc(S["ex"], 1)
            if step == 11:
                act.wait_ge(S["wt"], SLOTS * i + s + 1)
                A(halves(wts[s]), areas(ps, s, 0), ACT.Copy).then_inc(S["wts"], 1)
            if step == 12:
                act.wait_ge(S["ao"], SLOTS * i + s + 1)
                A(ao[s], area(ps, s, 2), ACT.Copy).then_inc(S["aos"], 1)
            if step == 14:
                n2.square(act, SLOTS * i + s, s)
            if step == 15:
                n2.rstd(act, SLOTS * i + s, s)
            if step == 17:
                n3.square(act, SLOTS * i + s, s)
            if step == 18:
                n3.rstd(act, SLOTS * i + s, s)

        rounds(act, STEPS, BEHIND, stage)

    @block.vector
    def _(dve):
        V = nc.vector
        x = W("L0_attn_scale")
        V.tensor_scalar(neg, x, -1.0, None, ALU.mult).then_inc(S["sp0"], 1)
        dve.wait_ge(S["sp0"], 1)
        V.tensor_tensor(low, x, neg, ALU.min).then_inc(S["sp1"], 1)
        dve.wait_ge(S["sp2"], 1)
        V.tensor_scalar(onep, el, 1.0, None, ALU.add).then_inc(S["sp3"], 1)
        dve.wait_ge(S["sp4"], 1)
        V.scalar_tensor_tensor(pos, x, 0.0, ln1, ALU.max, ALU.add).then_inc(S["sp5"], 1)
        dve.wait_ge(S["sp5"], 1)
        V.tensor_scalar(sc, pos, float(C) ** -0.5, None, ALU.mult).then_inc(S["sp6"], 1)

        def stage(step, i, s):
            if step == 2:
                n1.scale(dve, SLOTS * i + s, s, xn[s])
            if step == 4:
                dve.wait_ge(S["ksq"], SLOTS * i + s + 1)
                V.tensor_reduce(kss[s], tiles(ksq[s]), AX.X, ALU.add).then_inc(S["kss"], 1)
                dve.wait_ge(S["qv"], SLOTS * i + s + 1)
                V.tensor_scalar(qm[s], area(ps, s, 1), float(C), 1e-24, ALU.mult, ALU.max).then_inc(S["qm"], 1)
                dve.wait_ge(S["kss"], SLOTS * i + s + 1)
                V.tensor_scalar(ksm[s], kss[s], 1e-24, None, ALU.max).then_inc(S["ksm"], 1)
            if step == 5:
                dve.wait_ge(S["qr"], SLOTS * i + s + 1)
                V.tensor_tensor(qn[s], area(ps, s, 0), qr[s], ALU.mult).then_inc(S["qn"], 1)
                dve.wait_ge(S["kr"], SLOTS * i + s + 1)
                for m in range(2):
                    o = kn[s].rearrange("p (t m c) -> p t m c", t=QT, m=2)[:, :, m, :]
                    k = kr[s].rearrange("p (t m) -> p t m", m=2)[:, :, m]
                    last = V.tensor_tensor(o, kv(s)[:, :, 0, 64 * m:64 * m + 64], over(k, 64), ALU.mult)
                last.then_inc(S["kn"], 1)
            if step == 7:
                dve.wait_ge(S["sc"], SLOTS * i + s + 1)
                V.tensor_reduce(halves(mx[s]), scores(s), AX.X, ALU.max).then_inc(S["mx"], 1)
            if step == 7:
                dve.wait_ge(S["mx"], SLOTS * i + s + 1)
                V.tensor_tensor(halves(sh[s]).rearrange("p m (t k) -> p m t k", k=P), scores(s),
                                halves(mx[s]).unsqueeze(3).broadcast_to([P, 2, QT, P]), ALU.subtract).then_inc(S["sh"], 1)
            if step == 10:
                dve.wait_ge(S["ex"], SLOTS * i + s + 1)
                V.tensor_reduce(den[s], tiles(sh[s]), AX.X, ALU.add).then_inc(S["den"], 1)
            if step == 10:
                dve.wait_ge(S["den"], SLOTS * i + s + 1)
                V.reciprocal(rden[s], den[s]).then_inc(S["rden"], 1)
            if step == 10:
                dve.wait_ge(S["rden"], SLOTS * i + s + 1)
                V.tensor_tensor(tiles(ex[s]), tiles(sh[s]), over(rden[s], P), ALU.mult).then_inc(S["w"], 1)
            if step == 13:
                dve.wait_ge(S["wo"], SLOTS * i + s + 1)
                V.scalar_tensor_tensor(o1[s], area(ps, s, 3), 0.1, h(i, s), ALU.mult, ALU.add).then_inc(S["o1"], 1)
            if step == 15:
                n2.scale(dve, SLOTS * i + s, s, xn[s])
            if step == 16:
                dve.wait_ge(S["hb"], SLOTS * i + s + 1)
                dve.wait_ge(S["n2_x"], SLOTS * i + s + 1)
                V.scalar_tensor_tensor(o3[s], xn[s], W("L0_attn_g2"), hb[s], ALU.mult, ALU.add).then_inc(S["o3"], 1)
            if step == 19:
                n3.scale(dve, SLOTS * i + s, s, h(i, s))

        rounds(dve, STEPS, BEHIND, stage)


def routed_ffn(nc, ctx, K, W, H, psum):
    KEPT = max(1, TOK // 2) - 1
    MH = 2
    STEPS, BEHIND = 13, 6
    S = Sems(nc, ctx, "ff", Norm.names("n1") + " hs wb wbs dg wc gt eq cnt f fr ft fts " + " ".join(f"hid{s} g{s}" for s in range(SLOTS)) + " y yf o")

    def sb(name, cols):
        t = ctx.enter_context(nc.sbuf_tensor("ff_" + name, [P, SLOTS, cols], F32))
        return [t[:, s, :] for s in range(SLOTS)]

    sq, r, hs, wbs, dg = sb("sq", UT), sb("r", UT), sb("hs", UT), sb("wbs", 2 * UT), sb("dg", 2 * UT)
    wc, gt, eq, cnt, f = (sb(n, NT) for n in ("wc", "gt", "eq", "cnt", "f"))
    fr, fts, yf, o = sb("fr", UT), sb("fts", UT), sb("yf", UT), sb("o", UT)
    g = sb("g", 2 * MH * UT)
    junk = ctx.enter_context(nc.sbuf_tensor("ff_junk", [P, NT, TOK], BF16))
    junk2 = ctx.enter_context(nc.sbuf_tensor("ff_junk2", [P, NT, TOK], BF16))
    ps = psum
    n1 = Norm(nc, S, K, "n1", ps, 2, 3, sq, r)

    def h(i, s):
        return H[:, bass.ds(i * (SLOTS * UT) + s * UT, UT)]

    def tiles(v, n=NT):
        return v.rearrange("p (t k) -> p t k", t=n)

    block = ctx.enter_context(nc.Block())

    @block.tensor
    def _(pe):
        mm = nc.tensor.matmul

        def stage(step, i, s):
            if step == 1:
                pe.wait_ge(S["hs"], SLOTS * i + s + 1)
                pe.wait_ge(S[f"g{s}"], i * (2 * MH))
                pe.wait_ge(S["n1_x"], past(SLOTS * i + s - (SLOTS - 1)))
                for img in range(2):
                    m = mm(area(ps, s, img), W("ff_wr")[64 * img:64 * img + 64, :], hs[s][64 * img:64 * img + 64, :], start=True, stop=True)
                m.then_inc(S["wb"], 1)
            for k in range(2 * MH):
                img, half = k % 2, k // 2
                lo = 64 * img
                if step == 2 + k:
                    n = SLOTS * i + s
                    pe.wait_ge(S["wbs"], n + 1)
                    if k >= 2:
                        pe.wait_ge(S[f"g{s}"], i * (2 * MH) + k - 1)
                    mm(area(ps, s, img), W("ff_w1")[lo:lo + 64, P * half:P * half + P], hs[s][lo:lo + 64, :],
                       start=True, stop=True).then_inc(S[f"hid{s}"], 1)
            if step == 7:
                pe.wait_ge(S["fr"], SLOTS * i + s + 1)
                pe.wait_ge(S[f"g{s}"], i * (2 * MH) + 2 * MH)
                for t in range(QT):
                    m = mm(area(ps, s, 2)[:, P * t:P * t + P], fr[s][:, P * t:P * t + P], K("ident"), start=True, stop=True)
                m.then_inc(S["ft"], 1)
            if step == 6:
                pe.wait_ge(S[f"g{s}"], i * (2 * MH) + 2 * MH)
                for half in range(MH):
                    for img in range(2):
                        k = 2 * half + img
                        m = mm(area(ps, s, 3)[64 * img:64 * img + 64, :], W("ff_w2")[:, 64 * half:64 * half + 64], g[s][:, UT * k:UT * k + UT],
                               start=(half == 0), stop=(half == MH - 1))
                m.then_inc(S["y"], 1)
            if step == 9:
                pe.wait_ge(S["o"], SLOTS * i + s + 1)
                n1.centre(o[s], s)
            if step == 9:
                n1.variance(pe, SLOTS * i + s, s)

        rounds(pe, STEPS, BEHIND, stage)

    @block.scalar
    def _(act):
        A = nc.scalar.activation

        def stage(step, i, s):
            if step == 0:
                n = SLOTS * i + s
                act.wait_ge(S["n1_c"], past(n - (SLOTS - 1)))
                act.wait_ge(S["o"], past(n - (SLOTS - 1)))
                A(hs[s], h(i, s), ACT.Copy).then_inc(S["hs"], 1)
            if step == 1:
                act.wait_ge(S["wb"], SLOTS * i + s + 1)
                A(wbs[s].rearrange("p (m k) -> p m k", m=2), areas(ps, s, 0), ACT.Identity, bias=W("L0_ffn_br")).then_inc(S["wbs"], 1)
            for k in range(2 * MH):
                if step == 2 + k:
                    n = SLOTS * i + s
                    act.wait_ge(S[f"hid{s}"], i * (2 * MH) + k + 1)
                    A(g[s][:, UT * k:UT * k + UT], area(ps, s, k % 2), ACT.Gelu_apprx_tanh, bias=W("ff_b1")[:, k // 2:k // 2 + 1]).then_inc(S[f"g{s}"], 1)
            if step == 7:
                act.wait_ge(S["ft"], SLOTS * i + s + 1)
                A(fts[s], area(ps, s, 2), ACT.Copy).then_inc(S["fts"], 1)
            if step == 9:
                n1.square(act, SLOTS * i + s, s)
            if step == 9:
                n1.rstd(act, SLOTS * i + s, s)

        rounds(act, STEPS, BEHIND, stage)

    @block.vector
    def _(dve):
        V = nc.vector

        def stage(step, i, s):
            if step == 2:
                n = SLOTS * i + s
                dve.wait_ge(S["wbs"], n + 1)
                dve.wait_ge(S["wc"], past(n - (SLOTS - 1)))
                V.tensor_tensor(tiles(dg[s]), tiles(wbs[s]), K("ident").unsqueeze(1).broadcast_to([P, NT, P]), ALU.mult).then_inc(S["dg"], 1)
            if step == 3:
                n = SLOTS * i + s
                dve.wait_ge(S["dg"], n + 1)
                V.tensor_reduce(wc[s], tiles(dg[s]), AX.X, ALU.add).then_inc(S["wc"], 1)
            if step == 3:
                n = SLOTS * i + s
                dve.wait_ge(S["wc"], n + 1)
                dve.wait_ge(S["cnt"], n)
                for k in range(NT):
                    row = wbs[s][:, TOK * (k // 2):TOK * (k // 2) + TOK]
                    a = V.tensor_scalar(junk[:, k, :], row, wc[s][:, k:k + 1], None, ALU.is_gt, ALU.add, accum_out=gt[s][:, k:k + 1])
                    b = V.scalar_tensor_tensor(junk2[:, k, :], row, wc[s][:, k:k + 1], K("earlier")[:, TOK * (k % 2):TOK * (k % 2) + TOK],
                                               ALU.is_equal, ALU.mult, accum_out=eq[s][:, k:k + 1])
                a.then_inc(S["gt"], 1)
                b.then_inc(S["eq"], 1)
                dve.wait_ge(S["gt"], n + 1)
                dve.wait_ge(S["eq"], n + 1)
                V.tensor_tensor(cnt[s], gt[s], eq[s], ALU.add).then_inc(S["cnt"], 1)
                dve.wait_ge(S["cnt"], n + 1)
                V.scalar_tensor_tensor(f[s], cnt[s], KEPT - 0.5, wc[s], ALU.is_lt, ALU.mult).then_inc(S["f"], 1)
                dve.wait_ge(S["f"], n + 1)
                for img in range(2):
                    d = fr[s].rearrange("p (t m c) -> p t m c", t=QT, m=2)[:, :, img, :]
                    last = V.tensor_copy(d, f[s][:, QT * img:QT * img + QT].unsqueeze(2).broadcast_to([P, QT, 64]))
                last.then_inc(S["fr"], 1)
            if step == 8:
                n = SLOTS * i + s
                dve.wait_ge(S["y"], n + 1)
                dve.wait_ge(S["fts"], n + 1)
                V.scalar_tensor_tensor(yf[s], area(ps, s, 3), W("ff_b2"), fts[s], ALU.add, ALU.mult).then_inc(S["yf"], 1)
                dve.wait_ge(S["yf"], n + 1)
                V.scalar_tensor_tensor(o[s], hs[s], 2.0, yf[s], ALU.mult, ALU.add).then_inc(S["o"], 1)
            if step == 11:
                n1.scale(dve, SLOTS * i + s, s, h(i, s))

        rounds(dve, STEPS, BEHIND, stage)


PI = 3.1415925


def holographic(nc, ctx, K, W, H, psum, fetch):
    STEPS, BEHIND = 17, 14
    S = Sems(nc, ctx, "ho", Norm.names("n1", "n2") +
             " pr0 pr1 pr2 pr3 pr4 pr5 pr6 pr7 pr8 sn0 sn1 wg gb silu0 silu1 silu2 silu3 hs a1 a2 vps g1 g1s vt vts tk uk kf tq uq qf sa sb sas sbs"
             " ct cts gd gt gg mr mi mrs mis rr ri pos df dg cb nb wo hb o")

    def sb(name, cols, n=SLOTS):
        t = ctx.enter_context(nc.sbuf_tensor("ho_" + name, [P, n, cols], F32))
        return [t[:, s, :] for s in range(n)]

    sq, r, hs = sb("sq", UT), sb("r", UT), sb("hs", UT)
    a1, a2, vps, vts = sb("a1", UT), sb("a2", UT), sb("vps", UT), sb("vts", UT)
    g1s = sb("g1s", UT)
    tk, uk, kf, tq, uq, qf = (sb(n, UT) for n in ("tk", "uk", "kf", "tq", "uq", "qf"))
    sa, sc_ = sb("sa", 2 * UT), sb("sc", UT)
    cts, gt, gg = sb("cts", UT), sb("gt", UT), sb("gg", UT)
    mr, mi, mrs, mis = (sb(n, UT) for n in ("mr", "mi", "mrs", "mis"))
    pos, df, cb, nb, hb, o = (sb(n, UT) for n in ("pos", "df", "cb", "nb", "hb", "o"))
    rr, ri = mr, mi
    tab = ctx.enter_context(nc.sbuf_tensor("ho_tab", [P, 12, TOK], F32))
    turns, whole, red1, red2, red3, red, mag, low, sinp, cosp, sinn, cosn = (tab[:, k, :] for k in range(12))
    wgd = ctx.enter_context(nc.sbuf_tensor("ho_wgd", [32, P], F32))
    gb = ctx.enter_context(nc.sbuf_tensor("ho_gb", [P, 2], F32))
    unused = ctx.enter_context(nc.sbuf_tensor("ho_unused", [P, 4], F32))
    ps = psum
    n1 = Norm(nc, S, K, "n1", ps, 1, 2, sq, r)
    n2 = Norm(nc, S, K, "n2", ps, 1, 2, sq, r)

    def h(i, s):
        return H[:, bass.ds(i * (SLOTS * UT) + s * UT, UT)]

    def tiles(v, n):
        return v.rearrange("p (t k) -> p t k", t=n)

    def each(v, n):
        return v.unsqueeze(1).broadcast_to([P, n, v.shape[1]])

    block = ctx.enter_context(nc.Block())

    @block.sync
    def _(sp):
        fetch(sp)

    @block.tensor
    def _(pe):
        mm = nc.tensor.matmul
        pe.wait_ge(S["wg"], 1)

        def stage(step, i, s):
            if step == 1:
                n = SLOTS * i + s
                pe.wait_ge(S["hs"], n + 1)
                pe.wait_ge(S["n2_x"], past(n - (SLOTS - 1)))
                mm(area(ps, s, 0), W("ho_wk1"), hs[s], start=True, stop=True)
                mm(area(ps, s, 1), W("ho_wq1"), hs[s], start=True, stop=True)
                mm(area(ps, s, 2), W("ho_wvp"), hs[s], start=True, stop=True)
                for t in range(QT):
                    m = mm(area(ps, s, 3)[:, P * t:P * t + P], hs[s][:, P * t:P * t + P], W("ho_wvc"), start=True, stop=True)
                m.then_inc(S["vt"], 1)
            if step == 3:
                n = SLOTS * i + s
                pe.wait_ge(S["a1"], n + 1)
                pe.wait_ge(S["vps"], n + 1)
                mm(area(ps, s, 0), W("ho_wk2"), a1[s], start=True, stop=True)
                pe.wait_ge(S["a2"], n + 1)
                pe.wait_ge(S["vts"], n + 1)
                mm(area(ps, s, 1), W("ho_wq2"), a2[s], start=True, stop=True)
                mm(area(ps, s, 2)[0:32, :], W("ho_wg1"), hs[s], start=True, stop=True).then_inc(S["g1"], 1)
            if step == 4:
                n = SLOTS * i + s
                pe.wait_ge(S["g1s"], n + 1)
                mm(area(ps, s, 3), wgd[:, :], g1s[s][0:32, :], start=True, stop=True).then_inc(S["gd"], 1)
            if step == 7:
                n = SLOTS * i + s
                pe.wait_ge(S["kf"], n + 1)
                pe.wait_ge(S["qf"], n + 1)
                for img in range(2):
                    lo = 64 * img
                    for j in range(U):
                        c = TOK * j
                        m = mm(area(ps, s, img)[:, TOK * j:TOK * j + TOK], kf[s][lo:lo + 64, c:c + P], qf[s][lo:lo + 64, c:c + TOK], start=True, stop=True)
                m.then_inc(S["sa"], 1)
                pe.wait_ge(S["gt"], n + 1)
                for img in range(2):
                    lo = 64 * img
                    for j in range(U):
                        c = TOK * j + P
                        k = img * U + j
                        m = mm(area(ps, s, 2 + img)[:, P * j:P * j + P], kf[s][lo:lo + 64, c:c + P], qf[s][lo:lo + 64, c:c + P], start=True, stop=True)
                m.then_inc(S["sb"], 1)
            if step == 8:
                n = SLOTS * i + s
                pe.wait_ge(S["sas"], n + 1)
                pe.wait_ge(S["sbs"], n + 1)
                for j in range(U):
                    for img in range(2):
                        k = img * U + j
                        o_ = area(ps, s, 0)[64 * img:64 * img + 64, TOK * j:TOK * j + TOK]
                        v0 = vts[s][:, 2 * P * j + 64 * img:2 * P * j + 64 * img + 64]
                        v1 = vts[s][:, 2 * P * j + P + 64 * img:2 * P * j + P + 64 * img + 64]
                        mm(o_, v0, sa[s][:, TOK * k:TOK * k + TOK], start=True, stop=False, skip_group_check=True)
                        m = mm(o_[:, P:], v1, sc_[s][:, P * k:P * k + P], start=False, stop=True, skip_group_check=True)
                m.then_inc(S["ct"], 1)
            if step == 10:
                pe.wait_ge(S["cb"], SLOTS * i + s + 1)
                n1.centre(cb[s], s)
            if step == 11:
                n1.variance(pe, SLOTS * i + s, s)
            if step == 13:
                pe.wait_ge(S["nb"], SLOTS * i + s + 1)
                mm(area(ps, s, 3), W("ho_wo"), nb[s], start=True, stop=True).then_inc(S["wo"], 1)
            if step == 14:
                pe.wait_ge(S["o"], SLOTS * i + s + 1)
                n2.centre(o[s], s)
            if step == 15:
                n2.variance(pe, SLOTS * i + s, s)

        rounds(pe, STEPS, BEHIND, stage)

    @block.scalar
    def _(act):
        A = nc.scalar.activation
        act.wait_ge(S["pr6"], 1)
        A(sinp, red, ACT.Sin).then_inc(S["sn0"], 1)
        act.wait_ge(S["pr8"], 1)
        A(cosp, low, ACT.Sin).then_inc(S["sn1"], 1)
        act.wait_ge(S["gb"], 1)

        def one_table(k, i, s):
            if s % 2 == 0:
                act.wait_ge(S[f"silu{k}"], 2 * i + s // 2)
                A(unused[:, k:k + 1], K("eps"), ACT.Silu).then_inc(S[f"silu{k}"], 1)

        def stage(step, i, s):
            if step == 0:
                act.wait_ge(S["o"], past(SLOTS * i + s - (SLOTS - 1)))
                A(hs[s], h(i, s), ACT.Copy).then_inc(S["hs"], 1)
            if step == 1:
                n = SLOTS * i + s
                act.wait_ge(S["vt"], n + 1)
                one_table(0, i, s)
                A(a1[s], area(ps, s, 0), ACT.Tanh, bias=W("L1_attn_bk1")).then_inc(S["a1"], 1)
                A(a2[s], area(ps, s, 1), ACT.Tanh, bias=W("L1_attn_bq1")).then_inc(S["a2"], 1)
                A(vps[s], area(ps, s, 2), ACT.Identity, bias=W("L1_attn_bvp")).then_inc(S["vps"], 1)
            if step == 3:
                n = SLOTS * i + s
                act.wait_ge(S["g1"], n + 1)
                A(g1s[s][0:32, :], area(ps, s, 2)[0:32, :], ACT.Relu, bias=W("ho_bg1")).then_inc(S["g1s"], 1)
                one_table(1, i, s)
                A(tk[s], area(ps, s, 0), ACT.Tanh, bias=W("ho_bk2")).then_inc(S["tk"], 1)
            if step == 4:
                n = SLOTS * i + s
                act.wait_ge(S["gd"], n + 1)
                one_table(2, i, s)
                A(tq[s], area(ps, s, 1), ACT.Tanh, bias=W("ho_bq2")).then_inc(S["tq"], 1)
                A(gt[s], area(ps, s, 3), ACT.Tanh, bias=gb[:, 1:2], scale=0.5).then_inc(S["gt"], 1)
            if step == 6:
                n = SLOTS * i + s
                one_table(3, i, s)
                act.wait_ge(S["uk"], n + 1)
                A(kf[s], uk[s], ACT.Sin, bias=K("turn_bias"), scale=K("turn_scale")).then_inc(S["kf"], 1)
                act.wait_ge(S["uq"], n + 1)
                A(qf[s], uq[s], ACT.Sin, bias=K("turn_bias"), scale=K("turn_scale")).then_inc(S["qf"], 1)
            if step == 10:
                n1.square(act, SLOTS * i + s, s)
            if step == 11:
                n1.rstd(act, SLOTS * i + s, s)
            if step == 12:
                act.wait_ge(S["n1_x"], SLOTS * i + s + 1)
                A(nb[s], df[s], ACT.Identity, bias=W("L1_attn_ln_b"), scale=W("L1_attn_ln_g")).then_inc(S["nb"], 1)
            if step == 9:
                act.wait_ge(S["o"], past(SLOTS * i + s - (SLOTS - 1)))
                act.wait_ge(S["hs"], SLOTS * i + s + 1)
                A(hb[s], hs[s], ACT.Identity, bias=W("L1_attn_bo"), scale=2.0).then_inc(S["hb"], 1)
            if step == 14:
                n2.square(act, SLOTS * i + s, s)
            if step == 15:
                n2.rstd(act, SLOTS * i + s, s)

        rounds(act, STEPS, BEHIND, stage)

    @block.gpsimd
    def _(pool):
        G = nc.gpsimd
        pool.wait_ge(S["sn1"], 1)

        def stage(step, i, s):
            if step == 2:
                n = SLOTS * i + s
                pool.wait_ge(S["vps"], n + 1)
                pool.wait_ge(S["pos"], past(n - (SLOTS - 1)))
                G.tensor_tensor(tiles(mr[s], U), tiles(vps[s], U), each(cosp, U), ALU.mult).then_inc(S["mr"], 1)
                G.tensor_tensor(tiles(mi[s], U), tiles(vps[s], U), each(sinp, U), ALU.mult).then_inc(S["mi"], 1)

        rounds(pool, STEPS, BEHIND, stage)

    @block.vector
    def _(dve):
        V = nc.vector
        V.tensor_tensor(wgd[:, :], W("ho_wg2a"), W("ho_wg2b"), ALU.subtract).then_inc(S["wg"], 1)
        V.tensor_tensor(gb[:, 0:1], W("ho_bg2a"), W("ho_bg2b"), ALU.subtract).then_inc(S["pr0"], 1)
        dve.wait_ge(S["pr0"], 1)
        V.tensor_scalar(gb[:, 1:2], gb[:, 0:1], 0.5, None, ALU.mult).then_inc(S["gb"], 1)
        C1, C2 = 6.28125, 0.0019350051879882812
        C3 = 2 * np.pi - C1 - C2
        MAGIC = 1.5 * 2.0 ** 23
        ph = W("ho_phases")
        V.tensor_scalar(turns, ph, 1 / (2 * np.pi), MAGIC, ALU.mult, ALU.add).then_inc(S["pr1"], 1)
        dve.wait_ge(S["pr1"], 1)
        V.tensor_scalar(whole, turns, -MAGIC, None, ALU.add).then_inc(S["pr2"], 1)
        dve.wait_ge(S["pr2"], 1)
        V.scalar_tensor_tensor(red1, whole, -C1, ph, ALU.mult, ALU.add).then_inc(S["pr3"], 1)
        dve.wait_ge(S["pr3"], 1)
        V.scalar_tensor_tensor(red2, whole, -C2, red1, ALU.mult, ALU.add).then_inc(S["pr4"], 1)
        dve.wait_ge(S["pr4"], 1)
        V.scalar_tensor_tensor(red3, whole, -float(C3), red2, ALU.mult, ALU.add).then_inc(S["pr5"], 1)
        dve.wait_ge(S["pr5"], 1)
        V.tensor_scalar(red, red3, PI, -PI, ALU.min, ALU.max).then_inc(S["pr6"], 1)
        dve.wait_ge(S["pr6"], 1)
        V.scalar_tensor_tensor(mag, red, -1.0, red, ALU.mult, ALU.max).then_inc(S["pr7"], 1)
        dve.wait_ge(S["pr7"], 1)
        V.tensor_scalar(low, mag, -1.0, PI / 2, ALU.mult, ALU.add).then_inc(S["pr8"], 1)
        dve.wait_ge(S["sn1"], 1)
        dve.wait_ge(S["sn0"], 1)
        V.tensor_tensor(cosn, cosp, K("root"), ALU.mult)
        V.tensor_tensor(sinn, sinp, K("root"), ALU.mult).then_inc(S["pr0"], 1)
        dve.wait_ge(S["pr0"], 2)

        def stage(step, i, s):
            if step == 2:
                n = SLOTS * i + s
                dve.wait_ge(S["vt"], n + 1)
                dve.wait_ge(S["vps"], n + 1)
                V.tensor_tensor(tiles(vts[s], QT), tiles(area(ps, s, 3), QT), each(W("ho_bvc"), QT), ALU.add).then_inc(S["vts"], 1)
            if step == 5:
                n = SLOTS * i + s
                dve.wait_ge(S["tk"], n + 1)
                V.scalar_tensor_tensor(uk[s], tk[s], K("turn_sign"), tk[s], ALU.mult, ALU.max).then_inc(S["uk"], 1)
                dve.wait_ge(S["tq"], n + 1)
                V.scalar_tensor_tensor(uq[s], tq[s], K("turn_sign"), tq[s], ALU.mult, ALU.max).then_inc(S["uq"], 1)
            if step == 6:
                n = SLOTS * i + s
                dve.wait_ge(S["mr"], n + 1)
                for j in range(U):
                    m = V.tensor_tensor_scan(mrs[s][:, TOK * j:TOK * j + TOK], K("ones"), mr[s][:, TOK * j:TOK * j + TOK], 0.0, ALU.mult, ALU.add)
                m.then_inc(S["mrs"], 1)
                dve.wait_ge(S["mi"], n + 1)
                for j in range(U):
                    m = V.tensor_tensor_scan(mis[s][:, TOK * j:TOK * j + TOK], K("ones"), mi[s][:, TOK * j:TOK * j + TOK], 0.0, ALU.mult, ALU.add)
                m.then_inc(S["mis"], 1)
            if step == 8:
                n = SLOTS * i + s
                dve.wait_ge(S["sb"], n + 1)
                V.tensor_tensor(tiles(sa[s], 2 * U), areas(ps, s, 0), each(K("causal"), 2 * U), ALU.mult).then_inc(S["sas"], 1)
                for img in range(2):
                    m = V.tensor_tensor(tiles(sc_[s][:, P * U * img:P * U * (img + 1)], U), tiles(area(ps, s, 2 + img)[:, 0:U * P], U),
                                        each(K("causal")[:, 0:P], U), ALU.mult)
                m.then_inc(S["sbs"], 1)
            if step == 7:
                n = SLOTS * i + s
                dve.wait_ge(S["mrs"], n + 1)
                V.tensor_tensor(tiles(rr[s], U), tiles(mrs[s], U), each(cosn, U), ALU.mult).then_inc(S["rr"], 1)
                dve.wait_ge(S["mis"], n + 1)
                V.tensor_tensor(tiles(ri[s], U), tiles(mis[s], U), each(sinn, U), ALU.mult).then_inc(S["ri"], 1)
                dve.wait_ge(S["gt"], n + 1)
                V.tensor_scalar(gg[s], gt[s], 0.5, 0.5, ALU.mult, ALU.add).then_inc(S["gg"], 1)
                dve.wait_ge(S["rr"], n + 1)
                dve.wait_ge(S["ri"], n + 1)
                V.tensor_tensor(pos[s], rr[s], ri[s], ALU.add).then_inc(S["pos"], 1)
            if step == 9:
                n = SLOTS * i + s
                dve.wait_ge(S["ct"], n + 1)
                V.tensor_tensor(tiles(cts[s], U), tiles(area(ps, s, 0), U), each(K("root32"), U), ALU.mult).then_inc(S["cts"], 1)
                dve.wait_ge(S["cts"], n + 1)
                dve.wait_ge(S["pos"], n + 1)
                V.tensor_tensor(df[s], pos[s], cts[s], ALU.subtract).then_inc(S["df"], 1)
                dve.wait_ge(S["df"], n + 1)
                dve.wait_ge(S["gg"], n + 1)
                V.tensor_tensor(gg[s], df[s], gg[s], ALU.mult).then_inc(S["dg"], 1)
                dve.wait_ge(S["dg"], n + 1)
                V.tensor_tensor(cb[s], gg[s], cts[s], ALU.add).then_inc(S["cb"], 1)
            if step == 12:
                n1.scale(dve, SLOTS * i + s, s, df[s])
            if step == 13:
                n = SLOTS * i + s
                dve.wait_ge(S["hb"], n + 1)
                dve.wait_ge(S["wo"], n + 1)
                V.tensor_tensor(o[s], area(ps, s, 3), hb[s], ALU.add).then_inc(S["o"], 1)
            if step == 16:
                n2.scale(dve, SLOTS * i + s, s, h(i, s))

        rounds(dve, STEPS, BEHIND, stage)


NE, FF = 16, 128
FAR = 3.0e38


EXPERT_LOADS = 16 * 4


def expert_buffers(nc, ctx, w1_dram, w2_dram, sel_dram):
    stage = ctx.enter_context(nc.sbuf_tensor("mo_stage", [P, NE * FF], F32))
    stage2 = ctx.enter_context(nc.sbuf_tensor("mo_stage2", [P, NE * P], F32))
    w2 = ctx.enter_context(nc.sbuf_tensor("mo_wdown", [FF, NE * C], F32))
    fetched = ctx.enter_context(nc.semaphore("fetched"))

    def fetch(sp):
        for lo in (0, 64):
            sp.dma_start(stage[lo:lo + 64, :].rearrange("h (e f) -> h e f", e=NE), w1_dram.rearrange("e h f -> h e f")).then_inc(fetched, 16)
        sp.dma_start(stage2[0:PARTS * 2 * NE, :], sel_dram).then_inc(fetched, 16)
        sp.dma_start(w2[:, :].rearrange("f (e h) -> f e h", e=NE), w2_dram.rearrange("e f h -> f e h")).then_inc(fetched, 16)

    return stage, stage2, w2, fetched, fetch


def experts(nc, ctx, K, W, H, psum, stage, stage2, w2, fetched, out):
    U = 2
    UT, NU = U * TOK, NP // U
    QT = UT // P
    NT = 2 * QT
    GR = 2 * NE
    HID, Y, GB, M1, M2 = 0, 2, 4, 6, 7
    S = Sems(nc, ctx, "mo", "id16 wh wl sel b2h b2r b2m b2l"
             " hs xhi xlo lgp lg m1 e1 p1 q1 b1 l2 m2 e2 p2 q2 b2 dd ex s1 w1 w2 g1 g2 g gh gr gm_ gl gtp gts bb acc"
             " hid rel0 rel1 gb gbs y mul add fat fht sa ma xa sqa va ra na ga ba ha sz mz xz sqz vz rz o st0 st1")

    def sb(name, cols, dt=F32):
        t = ctx.enter_context(nc.sbuf_tensor("mo_" + name, [P, 2, cols], dt))
        return [t[:, s, :] for s in range(2)]

    wh = ctx.enter_context(nc.sbuf_tensor("mo_wh", [P, NE * FF], BF16))
    wl = ctx.enter_context(nc.sbuf_tensor("mo_wl", [P, NE * FF], BF16))
    sel = ctx.enter_context(nc.sbuf_tensor("mo_sel", [PARTS * GR, NE * P], BF16))
    b2p = ctx.enter_context(nc.sbuf_tensor("mo_b2p", [PARTS * GR, 3, P], BF16))
    b2r = ctx.enter_context(nc.sbuf_tensor("mo_b2r", [PARTS * GR, P], F32))
    ident16 = ctx.enter_context(nc.sbuf_tensor("mo_ident16", [P, P], BF16))
    hs, acc = sb("hs", UT), sb("acc", UT)
    xa, xb = sb("xsa", UT, BF16), sb("xsb", UT, BF16)
    lg, e1, p1, b1, l2, e2, p2, b2, g1, g2, gate, gr = (sb(n, NT * NE) for n in "lg e1 p1 b1 l2 e2 p2 b2 g1 g2 gate gr".split())
    m1, q1, m2, q2, dd, ex, s1, v1, v2 = (sb(n, NT) for n in "m1 q1 m2 q2 dd ex s1 v1 v2".split())
    g3 = sb("g3", QT * PARTS * GR, BF16)
    gts = sb("gts", UT, BF16)
    hid = sb("hid", 2 * UT)
    gbs, tmp = sb("gbs", UT), sb("tmp", UT)
    xc, sq, ya, yb = sb("xc", UT), sb("sq", UT), sb("ya", UT), sb("yb", UT)
    sm, mn, vs, rs = (sb(n, NT) for n in "sm mn vs rs".split())
    ps = psum

    def h(i, s):
        return H[:, bass.ds(i * (2 * UT) + s * UT, UT)]

    def tiles(v, n=NT):
        return v.rearrange("p (t k) -> p t k", t=n)

    def over(v, k):
        return v.unsqueeze(2).broadcast_to([P, v.shape[1], k])

    def each(v, n=NT):
        return v.unsqueeze(1).broadcast_to([P, n, v.shape[1]])

    def parts(v):
        return v.rearrange("p (t q r) -> p t q r", t=QT, q=PARTS)

    def turned(b):
        return ps[:, b, :].bitcast(BF16)

    out_v = out.rearrange("(u j m) (t p) c -> u p j t m c", j=U, m=2, p=P)
    block = ctx.enter_context(nc.Block())

    def sweep(eng, body):
        for s in (0, 1):
            body(0, s, first=(s == 0))
        with eng.Fori(1, NU // 2 - 1) as i:
            for s in (0, 1):
                body(i, s)
        for s in (0, 1):
            body(NU // 2 - 1, s, last=(s == 1))

    @block.sync
    def _(sp):
        def store(i, s):
            src = yb[s].rearrange("p (j t m c) -> p j t m c", j=U, t=2, m=2)
            sp.wait_ge(S["o"], 2 * i + s + 1)
            for j in range(U):
                for m in range(2):
                    sp.dma_start(out_v[bass.ds(2 * i + s, 1), :, j, :, m, :].rearrange("a p t c -> (a p) t c"), src[:, j, :, m, :])\
                      .then_inc(S[f"st{s}"], 16)

        for s in (0, 1):
            store(0, s)
        with sp.Fori(1, NU // 2) as i:
            for s in (0, 1):
                store(i, s)
        sp.wait_ge(S["st0"], 16 * 2 * U * (NU // 2))
        sp.wait_ge(S["st1"], 16 * 2 * U * (NU // 2))

    @block.tensor
    def _(pe):
        mm = nc.tensor.matmul

        def logits(g, s):
            pe.wait_ge(S["hs"], g + 1)
            pe.wait_ge(S["xa"], past(g - 1))
            for t in range(QT):
                m = mm(ps[:, M1, GR * t:GR * t + GR], hs[s][:, P * t:P * t + P], W("mo_gate"), start=True, stop=True)
            m.then_inc(S["lgp"], 1)

        def turn_gates(g, s):
            pe.wait_ge(S["gl"], g + 1)
            pe.wait_ge(S["ha"], past(g - 1))
            for t in range(QT):
                m = nc.tensor.transpose(turned(M2)[0:PARTS * GR, P * t:P * t + P], g3[s][:, PARTS * GR * t:PARTS * GR * (t + 1)], ident16[:, :])
            m.then_inc(S["gtp"], 1)

        def output_biases(g, s):
            pe.wait_ge(S["gts"], g + 1)
            for k in range(3):
                m = mm(ps[:, M2, :], b2p[:, k, :], gts[s][0:PARTS * GR, :], start=(k == 0), stop=(k == 2))
            m.then_inc(S["bb"], 1)

        def up(n, s, e):
            if e == 0:
                pe.wait_ge(S["xlo"], n + 1)
            for img, x in ((0, xa[s]), (1, xb[s])):
                pe.wait_ge(S[f"rel{img}"], n * NE + e)
                mm(ps[:, HID + img, :], wh[:, FF * e:FF * e + FF], x, start=True, stop=False)
                mm(ps[:, HID + img, :], wl[:, FF * e:FF * e + FF], x, start=False, stop=True).then_inc(S["hid"], 1)

        def spread_gate(n, s, e):
            pe.wait_ge(S["gbs"], n * NE + max(e - 1, 0))
            mm(ps[:, GB + e % 2, :], sel[:, P * e:P * e + P], gts[s][0:PARTS * GR, :], start=True, stop=True).then_inc(S["gb"], 1)

        def down(n, s, e):
            for img in range(2):
                pe.wait_ge(S[f"rel{img}"], n * NE + e + 1)
            pe.wait_ge(S["mul"], n * NE + max(e - 1, 0))
            for img in range(2):
                m = mm(ps[64 * img:64 * img + 64, Y + e % 2, :], w2[:, C * e:C * e + C], hid[e % 2][:, UT * img:UT * img + UT], start=True, stop=True)
            m.then_inc(S["y"], 1)

        def turn_tokens(f, s):
            pe.wait_ge(S["add"], NE * (f + 1))
            pe.wait_ge(S["lg"], f + 2)
            for t in range(QT):
                m = nc.tensor.transpose(ps[:, M1, P * t:P * t + P], acc[s][:, P * t:P * t + P], K("ident"))
            m.then_inc(S["fat"], 1)
            pe.wait_ge(S["acc"], f + 2)
            for t in range(QT):
                m = nc.tensor.transpose(ps[:, M2, P * t:P * t + P], hs[s][:, P * t:P * t + P], K("ident"))
            m.then_inc(S["fht"], 1)

        pe.wait_ge(fetched, EXPERT_LOADS)
        pe.wait_ge(S["sel"], 1)
        pe.wait_ge(S["wl"], 1)
        pe.wait_ge(S["b2l"], 1)
        pe.wait_ge(S["id16"], 1)
        logits(0, 0)
        turn_gates(0, 0)
        output_biases(0, 0)

        def body(i, s, first=False, last=False):
            n = 2 * i + s
            if first:
                up(n, s, 0)
            for e in range(NE):
                spread_gate(n, s, e)
                if e + 1 < NE:
                    up(n, s, e + 1)
                elif not last:
                    up(n + 1, 1 - s, 0)
                down(n, s, e)
                if e == 1 and not first:
                    turn_tokens(n - 1, 1 - s)
                if e == 3 and not last:
                    logits(n + 1, 1 - s)
                if e == 13 and not last:
                    turn_gates(n + 1, 1 - s)
                if e == 15 and not last:
                    output_biases(n + 1, 1 - s)

        sweep(pe, body)
        pe.wait_ge(S["add"], NE * NU)
        for t in range(QT):
            m = nc.tensor.transpose(ps[:, M1, P * t:P * t + P], acc[1][:, P * t:P * t + P], K("ident"))
        m.then_inc(S["fat"], 1)
        for t in range(QT):
            m = nc.tensor.transpose(ps[:, M2, P * t:P * t + P], hs[1][:, P * t:P * t + P], K("ident"))
        m.then_inc(S["fht"], 1)

    @block.scalar
    def _(act):
        A = nc.scalar.activation

        def tokens(i, s, g):
            act.wait_ge(S["fht"], past(g - 1))
            act.wait_ge(S["add"], past((g - 1) * NE))
            A(hs[s], h(i, s), ACT.Copy).then_inc(S["hs"], 1)

        def high_part(g, s, img):
            act.wait_ge(S["hs"], g + 1)
            lo = 64 * img
            A((xa, xb)[img][s][lo:lo + 64, :], hs[s][lo:lo + 64, :], ACT.Copy).then_inc(S["xhi"], 1)

        def exp(g, s):
            act.wait_ge(S["dd"], g + 1)
            A(ex[s], dd[s], ACT.Exp).then_inc(S["ex"], 1)

        def gates(g, s):
            act.wait_ge(S["gtp"], g + 1)
            A(gts[s][0:PARTS * GR, :], turned(M2)[0:PARTS * GR, 0:UT], ACT.Copy).then_inc(S["gts"], 1)

        def hidden(n, s, e):
            act.wait_ge(S["hid"], n * (2 * NE) + 2 * e + 1)
            act.wait_ge(S["y"], n * NE + max(e - 1, 0))
            A(hid[e % 2][:, 0:UT], ps[:, HID, :], ACT.Relu, bias=W("mo_b1")[:, e:e + 1]).then_inc(S["rel0"], 1)

        def spread(n, s, e):
            act.wait_ge(S["gb"], n * NE + e + 1)
            act.wait_ge(S["mul"], n * NE + max(e - 1, 0))
            A(gbs[e % 2], ps[:, GB + e % 2, :], ACT.Copy).then_inc(S["gbs"], 1)

        def square(f, s, ready, done):
            act.wait_ge(S[ready], f + 1)
            A(sq[s], xc[s], ACT.Square).then_inc(S[done], 1)

        def rstd(f, s, ready, done):
            act.wait_ge(S[ready], f + 1)
            A(rs[s], vs[s], ACT.Abs_reciprocal_sqrt, bias=K("eps"), scale=1.0 / C).then_inc(S[done], 1)

        tokens(0, 0, 0)
        high_part(0, 0, 0)
        high_part(0, 0, 1)
        exp(0, 0)
        gates(0, 0)

        def body(i, s, first=False, last=False):
            n = 2 * i + s
            for e in range(NE):
                hidden(n, s, e)
                spread(n, s, e)
                if not first:
                    if e == 4:
                        square(n - 1, 1 - s, "xa", "sqa")
                    if e == 8:
                        rstd(n - 1, 1 - s, "va", "ra")
                    if e == 13:
                        square(n - 1, 1 - s, "xz", "sqz")
                    if e == 15:
                        rstd(n - 1, 1 - s, "vz", "rz")
                if not last:
                    if e == 2:
                        tokens(i + s, 1 - s, n + 1)
                    if e in (5, 6):
                        high_part(n + 1, 1 - s, e - 5)
                    if e == 7:
                        exp(n + 1, 1 - s)
                    if e == 14:
                        gates(n + 1, 1 - s)

        sweep(act, body)
        square(NU - 1, 1, "xa", "sqa")
        rstd(NU - 1, 1, "va", "ra")
        square(NU - 1, 1, "xz", "sqz")
        rstd(NU - 1, 1, "vz", "rz")

    @block.gpsimd
    def _(pool):
        G = nc.gpsimd

        def affine(f, s):
            pool.wait_ge(S["na"], f + 1)
            G.tensor_tensor(tiles(ya[s]), tiles(ya[s]), each(W("mo_gamma")), ALU.mult).then_inc(S["ga"], 1)
            pool.wait_ge(S["ga"], f + 1)
            G.tensor_tensor(tiles(ya[s]), tiles(ya[s]), each(W("mo_beta")), ALU.add).then_inc(S["ba"], 1)

        def body(i, s, first=False, last=False):
            n = 2 * i + s
            pool.wait_ge(S["acc"], n + 1)
            for e in range(NE):
                pool.wait_ge(S["mul"], n * NE + e + 1)
                pool.wait_ge(S["add"], n * NE + e)
                G.tensor_tensor(acc[s], acc[s], tmp[e % 2], ALU.add).then_inc(S["add"], 1)
                if e == 9 and not first:
                    affine(n - 1, 1 - s)

        sweep(pool, body)
        affine(NU - 1, 1)

    @block.vector
    def _(dve):
        V = nc.vector

        def low_parts(g, s):
            dve.wait_ge(S["xhi"], 2 * (g + 1))
            V.tensor_tensor(xa[s][64:128, :], hs[s][0:64, :], xa[s][0:64, :], ALU.subtract)
            V.tensor_tensor(xb[s][0:64, :], hs[s][64:128, :], xb[s][64:128, :], ALU.subtract).then_inc(S["xlo"], 1)

        def logits(g, s):
            dve.wait_ge(S["lgp"], g + 1)
            V.tensor_tensor(tiles(lg[s]), tiles(ps[:, M1, 0:P]), each(W("mo_gate_b")), ALU.add).then_inc(S["lg"], 1)

        def best_a(g, s, src, mx, eq, ready, k_m, k_e):
            dve.wait_ge(S[ready], g + 1)
            V.tensor_reduce(mx[s], tiles(src[s]), AX.X, ALU.max).then_inc(S[k_m], 1)
            dve.wait_ge(S[k_m], g + 1)
            V.tensor_tensor(tiles(eq[s]), tiles(src[s]), over(mx[s], NE), ALU.is_equal).then_inc(S[k_e], 1)

        def best_b(g, s, eq, pr, pm, oh, k_e, k_p, k_q, k_o):
            dve.wait_ge(S[k_e], g + 1)
            V.tensor_tensor(tiles(pr[s]), tiles(eq[s]), each(K("priority")), ALU.mult).then_inc(S[k_p], 1)
            dve.wait_ge(S[k_p], g + 1)
            V.tensor_reduce(pm[s], tiles(pr[s]), AX.X, ALU.max).then_inc(S[k_q], 1)
            dve.wait_ge(S[k_q], g + 1)
            V.tensor_tensor(tiles(oh[s]), tiles(pr[s]), over(pm[s], NE), ALU.is_equal).then_inc(S[k_o], 1)

        def without_best(g, s):
            dve.wait_ge(S["b1"], g + 1)
            V.scalar_tensor_tensor(l2[s], b1[s], -FAR, lg[s], ALU.mult, ALU.add).then_inc(S["l2"], 1)

        def distance(g, s):
            dve.wait_ge(S["m2"], g + 1)
            V.tensor_tensor(dd[s], m2[s], m1[s], ALU.subtract).then_inc(S["dd"], 1)

        def gates(g, s):
            dve.wait_ge(S["ex"], g + 1)
            V.tensor_scalar(s1[s], ex[s], 1.0, None, ALU.add).then_inc(S["s1"], 1)
            dve.wait_ge(S["s1"], g + 1)
            V.reciprocal(v1[s], s1[s]).then_inc(S["w1"], 1)
            dve.wait_ge(S["w1"], g + 1)
            V.tensor_tensor(v2[s], ex[s], v1[s], ALU.mult).then_inc(S["w2"], 1)
            V.tensor_tensor(tiles(g1[s]), tiles(b1[s]), over(v1[s], NE), ALU.mult).then_inc(S["g1"], 1)
            dve.wait_ge(S["w2"], g + 1)
            dve.wait_ge(S["b2"], g + 1)
            V.tensor_tensor(tiles(g2[s]), tiles(b2[s]), over(v2[s], NE), ALU.mult).then_inc(S["g2"], 1)
            dve.wait_ge(S["g1"], g + 1)
            dve.wait_ge(S["g2"], g + 1)
            V.tensor_tensor(gate[s], g1[s], g2[s], ALU.add).then_inc(S["g"], 1)

        def split_gates(g, s):
            dve.wait_ge(S["g"], g + 1)
            t = gate[s].rearrange("p (t r) -> p t r", t=QT)
            r = gr[s].rearrange("p (t r) -> p t r", t=QT)
            V.tensor_copy(parts(g3[s])[:, :, 0, :], t).then_inc(S["gh"], 1)
            dve.wait_ge(S["gh"], g + 1)
            V.tensor_tensor(r, t, parts(g3[s])[:, :, 0, :], ALU.subtract).then_inc(S["gr"], 1)
            dve.wait_ge(S["gr"], g + 1)
            V.tensor_copy(parts(g3[s])[:, :, 1, :], r).then_inc(S["gm_"], 1)
            dve.wait_ge(S["gm_"], g + 1)
            V.tensor_tensor(parts(g3[s])[:, :, 2, :], r, parts(g3[s])[:, :, 1, :], ALU.subtract).then_inc(S["gl"], 1)

        def start_sum(g, s):
            dve.wait_ge(S["bb"], g + 1)
            dve.wait_ge(S["fat"], past(g - 1))
            V.tensor_tensor(acc[s], ps[:, M2, :], hs[s], ALU.add).then_inc(S["acc"], 1)

        def hidden(n, s, e):
            dve.wait_ge(S["hid"], n * (2 * NE) + 2 * e + 2)
            dve.wait_ge(S["y"], n * NE + max(e - 1, 0))
            V.tensor_scalar(hid[e % 2][:, UT:2 * UT], ps[:, HID + 1, :], W("mo_b1")[:, e:e + 1], 0.0, ALU.add, ALU.max).then_inc(S["rel1"], 1)

        def gated(n, s, e):
            dve.wait_ge(S["y"], n * NE + e + 1)
            dve.wait_ge(S["gbs"], n * NE + e + 1)
            dve.wait_ge(S["add"], n * NE + max(e - 1, 0))
            V.tensor_tensor(tmp[e % 2], ps[:, Y + e % 2, :], gbs[e % 2], ALU.mult).then_inc(S["mul"], 1)

        def norm_a(f, s, src, ready, k_s, k_m, k_x):
            dve.wait_ge(S[ready], f + 1)
            V.tensor_reduce(sm[s], tiles(src), AX.X, ALU.add).then_inc(S[k_s], 1)
            dve.wait_ge(S[k_s], f + 1)
            V.tensor_scalar(mn[s], sm[s], 1.0 / C, None, ALU.mult).then_inc(S[k_m], 1)
            dve.wait_ge(S[k_m], f + 1)
            V.tensor_tensor(tiles(xc[s]), tiles(src), over(mn[s], C), ALU.subtract).then_inc(S[k_x], 1)

        def norm_b(f, s, k_sq, k_v):
            dve.wait_ge(S[k_sq], f + 1)
            V.tensor_reduce(vs[s], tiles(sq[s]), AX.X, ALU.add).then_inc(S[k_v], 1)

        def norm_c(f, s, dst, k_r, k_o):
            dve.wait_ge(S[k_r], f + 1)
            V.tensor_tensor(tiles(dst[s]), tiles(xc[s]), over(rs[s], C), ALU.mult).then_inc(S[k_o], 1)

        def add_tokens(f, s):
            dve.wait_ge(S["ba"], f + 1)
            dve.wait_ge(S["fht"], f + 1)
            V.tensor_tensor(ya[s], ps[:, M2, :], ya[s], ALU.add).then_inc(S["ha"], 1)

        dve.wait_ge(fetched, EXPERT_LOADS)
        V.tensor_copy(wh[:, :], stage[:, :]).then_inc(S["wh"], 1)
        V.tensor_copy(sel[:, :], stage2[0:PARTS * GR, :]).then_inc(S["sel"], 1)
        dve.wait_ge(S["wh"], 1)
        V.tensor_tensor(wl[:, :], stage[:, :], wh[:, :], ALU.subtract).then_inc(S["wl"], 1)
        V.tensor_copy(ident16[:, :], K("ident")).then_inc(S["id16"], 1)
        b2f = W("mo_b2")
        V.tensor_copy(b2p[:, 0, :], b2f).then_inc(S["b2h"], 1)
        dve.wait_ge(S["b2h"], 1)
        V.tensor_tensor(b2r[:, :], b2f, b2p[:, 0, :], ALU.subtract).then_inc(S["b2r"], 1)
        dve.wait_ge(S["b2r"], 1)
        V.tensor_copy(b2p[:, 1, :], b2r[:, :]).then_inc(S["b2m"], 1)
        dve.wait_ge(S["b2m"], 1)
        V.tensor_tensor(b2p[:, 2, :], b2r[:, :], b2p[:, 1, :], ALU.subtract).then_inc(S["b2l"], 1)

        low_parts(0, 0)
        logits(0, 0)
        best_a(0, 0, lg, m1, e1, "lg", "m1", "e1")
        best_b(0, 0, e1, p1, q1, b1, "e1", "p1", "q1", "b1")
        without_best(0, 0)
        best_a(0, 0, l2, m2, e2, "l2", "m2", "e2")
        distance(0, 0)
        best_b(0, 0, e2, p2, q2, b2, "e2", "p2", "q2", "b2")
        gates(0, 0)
        split_gates(0, 0)
        start_sum(0, 0)

        def body(i, s, first=False, last=False):
            n = 2 * i + s
            o = 1 - s
            if first:
                hidden(n, s, 0)
            for e in range(NE):
                if e + 1 < NE:
                    hidden(n, s, e + 1)
                elif not last:
                    hidden(n + 1, o, 0)
                gated(n, s, e)
                if not first:
                    if e == 2:
                        norm_a(n - 1, o, ps[:, M1, :], "fat", "sa", "ma", "xa")
                    if e == 5:
                        norm_b(n - 1, o, "sqa", "va")
                    if e == 9:
                        norm_c(n - 1, o, ya, "ra", "na")
                    if e == 11:
                        add_tokens(n - 1, o)
                    if e == 12:
                        norm_a(n - 1, o, ya[o], "ha", "sz", "mz", "xz")
                    if e == 13:
                        norm_b(n - 1, o, "sqz", "vz")
                    if e == 14:
                        dve.wait_ge(S[f"st{o}"], (i - 1 + s) * (16 * 2 * U))
                        norm_c(n - 1, o, yb, "rz", "o")
                if not last:
                    if e == 13:
                        low_parts(n + 1, o)
                    if e == 3:
                        logits(n + 1, o)
                        best_a(n + 1, o, lg, m1, e1, "lg", "m1", "e1")
                    if e == 4:
                        best_b(n + 1, o, e1, p1, q1, b1, "e1", "p1", "q1", "b1")
                    if e == 6:
                        without_best(n + 1, o)
                        best_a(n + 1, o, l2, m2, e2, "l2", "m2", "e2")
                        distance(n + 1, o)
                    if e == 7:
                        best_b(n + 1, o, e2, p2, q2, b2, "e2", "p2", "q2", "b2")
                    if e == 8:
                        gates(n + 1, o)
                    if e == 10:
                        split_gates(n + 1, o)
            if not last:
                start_sum(n + 1, o)

        sweep(dve, body)
        norm_a(NU - 1, 1, ps[:, M1, :], "fat", "sa", "ma", "xa")
        norm_b(NU - 1, 1, "sqa", "va")
        norm_c(NU - 1, 1, ya, "ra", "na")
        add_tokens(NU - 1, 1)
        norm_a(NU - 1, 1, ya[1], "ha", "sz", "mz", "xz")
        norm_b(NU - 1, 1, "sqz", "vz")
        dve.wait_ge(S["st1"], (NU // 2 - 1) * (16 * 2 * U))
        norm_c(NU - 1, 1, yb, "rz", "o")


class Phase(ExitStack):

    def __init__(self, nc):
        super().__init__()
        self.nc, self.held = nc, []

    def semaphore(self, name):
        self.held.append(self.nc.alloc_semaphore(name=name))
        return self.held[-1]

    def done(self):
        self.nc.clear_and_free_semaphores(self.held)
        self.nc.all_engine_barrier()


def program(nc, x, consts, wts, w1, w2, sel, out, kat, wat):
    with ExitStack() as ctx:
        def phase(build, *args):
            with Phase(nc) as p:
                build(nc, p, *args)
            p.done()

        kb = ctx.enter_context(nc.sbuf_tensor("consts_sb", [P, consts.shape[1]], F32))
        wb = ctx.enter_context(nc.sbuf_tensor("weights_sb", [P, wts.shape[1]], F32))
        H = ctx.enter_context(nc.sbuf_tensor("tokens", [P, NP * TOK], F32))
        psum = ctx.enter_context(nc.psum_tensor("psum", [P, 8, CH], F32))
        loaded = ctx.enter_context(nc.semaphore("loaded"))

        def K(name):
            at, n, rows = kat[name]
            return kb[0:rows, at:at + n]

        def W(name):
            at, n, rows = wat[name]
            return wb[0:rows, at:at + n]

        with nc.Block() as block:
            @block.sync
            def _(sp):
                sp.dma_start(kb[:, :], consts).then_inc(loaded, 16)
                sp.dma_start(wb[:, :], wts).then_inc(loaded, 16)
                sp.wait_ge(loaded, 32)

        phase(tokenizer, x.rearrange("(n two) c h w -> n (two c) (h w)", two=2), K, W, H, psum)
        phase(attention, K, W, H, psum)
        phase(routed_ffn, K, W, H, psum)
        *buffers, fetch = expert_buffers(nc, ctx, w1, w2, sel)
        phase(holographic, K, W, H, psum, fetch)
        phase(experts, K, W, H, psum, *buffers, out)


def kernel(**inputs):
    import concourse.bacc as bacc
    from concourse.bass_utils import run_bass_kernel_spmd as run

    nc = bacc.Bacc("TRN2", target_bir_lowering=False, num_devices=1)
    k, w = shape_constants(), weights(inputs)
    arrays = {"x": np.ascontiguousarray(inputs["x"]), "consts": k.array(), "weights_in": w.array(),
              "experts_up": np.ascontiguousarray(inputs["L1_ffn_w1"]), "experts_down": np.ascontiguousarray(inputs["L1_ffn_w2"]),
              "gate_rows": gate_rows()}
    aps = [nc.dram_tensor(n, a.shape, F32, kind="ExternalInput").ap() for n, a in arrays.items()]
    out = nc.dram_tensor("out", (B, TOK, C), F32, kind="ExternalOutput").ap()
    program(nc, *aps, out, k.at, w.at)
    r = run(nc, [arrays], core_ids=[0])
    return r.results[0]["out"]
```
